# Optimizing a Trainium2 kernel written in Bass

```python
import numpy as np
import jax
import jax.numpy as jnp

def _softmax(x, axis=-1):
    return jax.nn.softmax(x, axis=axis)

def _gelu(x):
    return jax.nn.gelu(x, approximate=True)

def _silu(x):
    return jax.nn.silu(x)

def _sigmoid(x):
    return jax.nn.sigmoid(x)

def _layernorm(x, axis=-1, eps=1e-05):
    m = jnp.mean(x, axis=axis, keepdims=True)
    v = jnp.var(x, axis=axis, keepdims=True)
    return (x - m) / jnp.sqrt(v + eps)

def _scatter_add(tgt, idx, src, axis=0):
    return tgt.at[idx].add(src)

def _segment_sum(src, seg, n):
    return jax.ops.segment_sum(src, seg, n)
kernel_name = 'mk_perceiver_d1_seqx_r2_5f099f'

def setup_inputs(seed: int=0):
    np.random.seed(seed)
    _w = jnp.asarray

    def _rec_inputs():
        import jax
        import jax.numpy as jnp
        _rk = jax.random.key(seed)
        x = -0.0003929 + 0.9999 * jax.random.normal(jax.random.fold_in(_rk, 1), (32, 64, 512), jnp.float32)
        _lenS = 64 - jax.random.randint(jax.random.fold_in(_rk, 7), (32,), 0, max(1, 64 // 4) + 1, jnp.int32)
        _lenS2 = 512 - jax.random.randint(jax.random.fold_in(_rk, 8), (32,), 0, max(1, 512 // 4) + 1, jnp.int32)
        _ctx_512P = jax.random.normal(jax.random.fold_in(_rk, 11), (32, 16, 256), jnp.float32)
        _ctx_512c = jax.random.dirichlet(jax.random.fold_in(_rk, 511), 0.3 * jnp.ones((16,), jnp.float32), (32, 512))
        _ctx_512t = jnp.einsum('bsk,bkd->bsd', _ctx_512c, _ctx_512P)
        _ctx_512t = _ctx_512t * jax.lax.rsqrt(jnp.mean(jnp.square(_ctx_512t)) + 1e-12) * 0.953939
        ctx_512 = 4.13588e-05 + 0.999923 * (_ctx_512t + 0.3 * jax.random.normal(jax.random.fold_in(_rk, 611), (32, 512, 256), jnp.float32))
        return (x, ctx_512)
    x, ctx_512 = _rec_inputs()

    def _L0_xattn_setup():
        import jax, jax.numpy as jnp
        import numpy as np
        B, LQ, LK = (8, 1024, 1024)
        QD, KD, VD = (512, 256, 256)
        key = jax.random.key(seed)
        ks = jax.random.split(key, 9)
        s = 0.02
        return {'query': jax.random.normal(ks[0], (B, LQ, QD), jnp.float32), 'key': jax.random.normal(ks[1], (B, LK, KD), jnp.float32), 'value': jax.random.normal(ks[2], (B, LK, VD), jnp.float32), 'Wq': jax.random.normal(ks[3], (QD, QD), jnp.float32) * s, 'bq': jnp.zeros((QD,), jnp.float32), 'Wk': jax.random.normal(ks[4], (KD, QD), jnp.float32) * s, 'bk': jnp.zeros((QD,), jnp.float32), 'Wv': jax.random.normal(ks[5], (VD, QD), jnp.float32) * s, 'bv': jnp.zeros((QD,), jnp.float32)}
    _L0_xattn_all = _L0_xattn_setup()
    _L0_xattn_in = {k: v for k, v in _L0_xattn_all.items() if k in ('Wq', 'bq', 'Wk', 'bk', 'Wv', 'bv')}
    del _L0_xattn_all

    def _L0_attn_setup():
        import jax, jax.numpy as jnp
        import numpy as np
        H = 16
        EPS_LN = 1e-05

        def _ln(x, g, b):
            m = jnp.mean(x, axis=-1, keepdims=True)
            v = jnp.mean((x - m) ** 2, axis=-1, keepdims=True)
            return (x - m) / jnp.sqrt(v + EPS_LN) * g + b

        def _fwd(x, Wq, bq, gq, betaq, Wk, bk, gk, betak, Wv, bv, gv, betav, Wfq, bfq, Wfk, bfk, ga, ba, W1, b1, W2, b2):
            B, L, d = x.shape
            D = d // H
            Q = _ln(x @ Wq + bq, gq, betaq)
            Kc = _ln(x @ Wk + bk, gk, betak)
            Vc = _ln(x @ Wv + bv, gv, betav)
            z = jnp.zeros((B, 1, d), x.dtype)
            K = jnp.concatenate([z, Kc], axis=1)
            V = jnp.concatenate([z, Vc], axis=1)
            phi_Q = jnp.tanh(Q @ Wfq + bfq) + 1.0
            phi_K = jnp.tanh(K @ Wfk + bfk) + 1.0
            split = lambda t: t.reshape(B, t.shape[1], H, D).transpose(0, 2, 1, 3)
            Qh, Kh, Vh = (split(Q), split(K), split(V))
            pQ, pK = (split(phi_Q), split(phi_K))
            q_probe = jnp.mean(Qh, axis=2) / jnp.sqrt(jnp.asarray(D, x.dtype))
            score = jax.nn.softmax(jnp.einsum('bhd,bhkd->bhk', q_probe, Kh), axis=-1)
            pKw = pK * score[..., None]
            KV = jnp.einsum('bhkd,bhke->bhde', pKw, Vh)
            Ksum = jnp.sum(pKw, axis=2)
            num = jnp.einsum('bhqd,bhde->bhqe', pQ, KV)
            den = jnp.einsum('bhqd,bhd->bhq', pQ, Ksum)[..., None] + 1e-06
            out = num / den
            out = out.transpose(0, 2, 1, 3).reshape(B, L, d)
            a = _ln(out, ga, ba)
            h = a + (jax.nn.gelu(a @ W1 + b1, approximate=False) @ W2 + b2)
            return h + x
        key = jax.random.key(seed)
        B, L, d, mlp = (4, 2048, 512, 2048)
        ks = jax.random.split(key, 12)
        s = 0.02
        inp = {'x': jax.random.normal(ks[0], (B, L, d), jnp.float32), 'Wq': jax.random.normal(ks[1], (d, d), jnp.float32) * s, 'bq': jnp.zeros((d,), jnp.float32), 'gq': jnp.ones((d,), jnp.float32), 'betaq': jnp.zeros((d,), jnp.float32), 'Wk': jax.random.normal(ks[2], (d, d), jnp.float32) * s, 'bk': jnp.zeros((d,), jnp.float32), 'gk': jnp.ones((d,), jnp.float32), 'betak': jnp.zeros((d,), jnp.float32), 'Wv': jax.random.normal(ks[3], (d, d), jnp.float32) * s, 'bv': jnp.zeros((d,), jnp.float32), 'gv': jnp.ones((d,), jnp.float32), 'betav': jnp.zeros((d,), jnp.float32), 'Wfq': jax.random.normal(ks[4], (d, d), jnp.float32) * s, 'bfq': jnp.zeros((d,), jnp.float32), 'Wfk': jax.random.normal(ks[5], (d, d), jnp.float32) * s, 'bfk': jnp.zeros((d,), jnp.float32), 'ga': jnp.ones((d,), jnp.float32), 'ba': jnp.zeros((d,), jnp.float32), 'W1': jax.random.normal(ks[6], (d, mlp), jnp.float32) * s, 'b1': jnp.zeros((mlp,), jnp.float32), 'W2': jax.random.normal(ks[7], (mlp, d), jnp.float32) * s, 'b2': jnp.zeros((d,), jnp.float32)}
        return inp
    _L0_attn_all = _L0_attn_setup()
    _L0_attn_in = {k: v for k, v in _L0_attn_all.items() if k in ('Wq', 'bq', 'gq', 'betaq', 'Wk', 'bk', 'gk', 'betak', 'Wv', 'bv', 'gv', 'betav', 'Wfq', 'bfq', 'Wfk', 'bfk', 'ga', 'ba', 'W1', 'b1', 'W2', 'b2')}
    del _L0_attn_all

    def _L0_ffn_setup():
        import jax, jax.numpy as jnp
        import numpy as np
        SINKHORN_ITERS = 8
        TEMPERATURE = 1.0
        EPS = 1e-06

        def sinkhorn(t):
            t = jnp.log(jnp.clip(t, EPS)) / TEMPERATURE
            for _ in range(SINKHORN_ITERS):
                t = t - jax.nn.logsumexp(t, axis=-2, keepdims=True)
                t = t - jax.nn.logsumexp(t, axis=-1, keepdims=True)
            return jnp.exp(t)
        key = jax.random.key(seed)
        k1, k2, k3 = jax.random.split(key, 3)
        B, N, D, E = (4, 2048, 512, 8)
        x = jax.random.normal(k1, (B, N, D), dtype=jnp.float32)
        gate_w = jax.random.normal(k2, (D, E), dtype=jnp.float32) * D ** (-0.5)
        experts = jax.random.normal(k3, (E, D, D), dtype=jnp.float32) * D ** (-0.5)
        return {'x': x, 'gate_w': gate_w, 'experts': experts}
    _L0_ffn_all = _L0_ffn_setup()
    _L0_ffn_in = {k: v for k, v in _L0_ffn_all.items() if k in ('gate_w', 'experts')}
    del _L0_ffn_all
    return {'x': x, 'ctx_512': ctx_512, 'L0_xattn_Wq': _L0_xattn_in['Wq'], 'L0_xattn_bq': _L0_xattn_in['bq'], 'L0_xattn_Wk': _L0_xattn_in['Wk'], 'L0_xattn_bk': _L0_xattn_in['bk'], 'L0_xattn_Wv': _L0_xattn_in['Wv'], 'L0_xattn_bv': _L0_xattn_in['bv'], 'L0_attn_Wq': _L0_attn_in['Wq'], 'L0_attn_bq': _L0_attn_in['bq'], 'L0_attn_gq': _L0_attn_in['gq'], 'L0_attn_betaq': _L0_attn_in['betaq'], 'L0_attn_Wk': _L0_attn_in['Wk'], 'L0_attn_bk': _L0_attn_in['bk'], 'L0_attn_gk': _L0_attn_in['gk'], 'L0_attn_betak': _L0_attn_in['betak'], 'L0_attn_Wv': _L0_attn_in['Wv'], 'L0_attn_bv': _L0_attn_in['bv'], 'L0_attn_gv': _L0_attn_in['gv'], 'L0_attn_betav': _L0_attn_in['betav'], 'L0_attn_Wfq': _L0_attn_in['Wfq'], 'L0_attn_bfq': _L0_attn_in['bfq'], 'L0_attn_Wfk': _L0_attn_in['Wfk'], 'L0_attn_bfk': _L0_attn_in['bfk'], 'L0_attn_ga': _L0_attn_in['ga'], 'L0_attn_ba': _L0_attn_in['ba'], 'L0_attn_W1': _L0_attn_in['W1'], 'L0_attn_b1': _L0_attn_in['b1'], 'L0_attn_W2': _L0_attn_in['W2'], 'L0_attn_b2': _L0_attn_in['b2'], 'L0_ffn_gate_w': _L0_ffn_in['gate_w'], 'L0_ffn_experts': _L0_ffn_in['experts']}

def reference(x, ctx_512, L0_xattn_Wq, L0_xattn_bq, L0_xattn_Wk, L0_xattn_bk, L0_xattn_Wv, L0_xattn_bv, L0_attn_Wq, L0_attn_bq, L0_attn_gq, L0_attn_betaq, L0_attn_Wk, L0_attn_bk, L0_attn_gk, L0_attn_betak, L0_attn_Wv, L0_attn_bv, L0_attn_gv, L0_attn_betav, L0_attn_Wfq, L0_attn_bfq, L0_attn_Wfk, L0_attn_bfk, L0_attn_ga, L0_attn_ba, L0_attn_W1, L0_attn_b1, L0_attn_W2, L0_attn_b2, L0_ffn_gate_w, L0_ffn_experts):
    import jax
    import jax.numpy as jnp

    def _L0_xattn_ref(query, key, value, Wq, bq, Wk, bk, Wv, bv):
        import jax, jax.numpy as jnp
        import numpy as np
        B, LQ, LK = (8, 1024, 1024)
        QD, KD, VD = (512, 256, 256)
        q = jnp.einsum('bld,de->ble', query, Wq) + bq
        k = jnp.einsum('bld,de->ble', key, Wk) + bk
        v = jnp.einsum('bld,de->ble', value, Wv) + bv
        scores = jnp.einsum('bqe,bke->bqk', q, k)
        attn = jax.nn.softmax(scores, axis=-1)
        out = jnp.einsum('bqk,bke->bqe', attn, v)
        return out

    def _L0_attn_ref(x, Wq, bq, gq, betaq, Wk, bk, gk, betak, Wv, bv, gv, betav, Wfq, bfq, Wfk, bfk, ga, ba, W1, b1, W2, b2):
        import jax, jax.numpy as jnp
        import numpy as np
        H = 16
        EPS_LN = 1e-05

        def _ln(x, g, b):
            m = jnp.mean(x, axis=-1, keepdims=True)
            v = jnp.mean((x - m) ** 2, axis=-1, keepdims=True)
            return (x - m) / jnp.sqrt(v + EPS_LN) * g + b

        def _fwd(x, Wq, bq, gq, betaq, Wk, bk, gk, betak, Wv, bv, gv, betav, Wfq, bfq, Wfk, bfk, ga, ba, W1, b1, W2, b2):
            B, L, d = x.shape
            D = d // H
            Q = _ln(x @ Wq + bq, gq, betaq)
            Kc = _ln(x @ Wk + bk, gk, betak)
            Vc = _ln(x @ Wv + bv, gv, betav)
            z = jnp.zeros((B, 1, d), x.dtype)
            K = jnp.concatenate([z, Kc], axis=1)
            V = jnp.concatenate([z, Vc], axis=1)
            phi_Q = jnp.tanh(Q @ Wfq + bfq) + 1.0
            phi_K = jnp.tanh(K @ Wfk + bfk) + 1.0
            split = lambda t: t.reshape(B, t.shape[1], H, D).transpose(0, 2, 1, 3)
            Qh, Kh, Vh = (split(Q), split(K), split(V))
            pQ, pK = (split(phi_Q), split(phi_K))
            q_probe = jnp.mean(Qh, axis=2) / jnp.sqrt(jnp.asarray(D, x.dtype))
            score = jax.nn.softmax(jnp.einsum('bhd,bhkd->bhk', q_probe, Kh), axis=-1)
            pKw = pK * score[..., None]
            KV = jnp.einsum('bhkd,bhke->bhde', pKw, Vh)
            Ksum = jnp.sum(pKw, axis=2)
            num = jnp.einsum('bhqd,bhde->bhqe', pQ, KV)
            den = jnp.einsum('bhqd,bhd->bhq', pQ, Ksum)[..., None] + 1e-06
            out = num / den
            out = out.transpose(0, 2, 1, 3).reshape(B, L, d)
            a = _ln(out, ga, ba)
            h = a + (jax.nn.gelu(a @ W1 + b1, approximate=False) @ W2 + b2)
            return h + x
        return _fwd(x, Wq, bq, gq, betaq, Wk, bk, gk, betak, Wv, bv, gv, betav, Wfq, bfq, Wfk, bfk, ga, ba, W1, b1, W2, b2)

    def _L0_ffn_ref(x, gate_w, experts):
        import jax, jax.numpy as jnp
        import numpy as np
        SINKHORN_ITERS = 8
        TEMPERATURE = 1.0
        EPS = 1e-06

        def sinkhorn(t):
            t = jnp.log(jnp.clip(t, EPS)) / TEMPERATURE
            for _ in range(SINKHORN_ITERS):
                t = t - jax.nn.logsumexp(t, axis=-2, keepdims=True)
                t = t - jax.nn.logsumexp(t, axis=-1, keepdims=True)
            return jnp.exp(t)
        B, N, D = x.shape
        E = gate_w.shape[-1]
        M = N // E
        gate_logits = jnp.einsum('bnd,de->bne', x, gate_w)
        competitive_gates = sinkhorn(gate_logits)
        vals, idx = jax.lax.top_k(jnp.swapaxes(competitive_gates, -1, -2), M)
        gate_values = jnp.swapaxes(vals, -1, -2)
        routed_indices = jnp.swapaxes(idx, -1, -2)
        b_idx = jnp.arange(B)[:, None, None]
        routed = x[b_idx, routed_indices]
        routed = jnp.transpose(routed, (2, 0, 1, 3))
        outputs = jnp.einsum('ebmd,edf->ebmf', routed, experts)
        outputs = outputs * jnp.transpose(gate_values, (2, 0, 1))[..., None]
        vals_bmed = jnp.transpose(outputs, (1, 2, 0, 3))
        routed_back = jnp.zeros_like(x).at[b_idx, routed_indices].set(vals_bmed)
        return routed_back
    x = x + _L0_xattn_ref(_layernorm(x, axis=-1), ctx_512, ctx_512, L0_xattn_Wq, L0_xattn_bq, L0_xattn_Wk, L0_xattn_bk, L0_xattn_Wv, L0_xattn_bv)
    x = x + _L0_attn_ref(_layernorm(x, axis=-1), L0_attn_Wq, L0_attn_bq, L0_attn_gq, L0_attn_betaq, L0_attn_Wk, L0_attn_bk, L0_attn_gk, L0_attn_betak, L0_attn_Wv, L0_attn_bv, L0_attn_gv, L0_attn_betav, L0_attn_Wfq, L0_attn_bfq, L0_attn_Wfk, L0_attn_bfk, L0_attn_ga, L0_attn_ba, L0_attn_W1, L0_attn_b1, L0_attn_W2, L0_attn_b2)
    x = x + _L0_ffn_ref(_layernorm(x, axis=-1), L0_ffn_gate_w, L0_ffn_experts)
    return x

_drawn_inputs = setup_inputs


def setup_inputs(seed=0):
    import zlib

    import numpy as np

    out = dict(_drawn_inputs(seed))
    spreads = {'L0_xattn_bq': (0.0, 0.1),
     'L0_xattn_bk': (0.0, 2.0),
     'L0_xattn_bv': (0.0, 0.1),
     'L0_attn_bq': (0.0, 0.1),
     'L0_attn_gq': (1.0, 0.59),
     'L0_attn_betaq': (0.0, 0.1),
     'L0_attn_bk': (0.0, 0.633),
     'L0_attn_gk': (1.0, 0.558),
     'L0_attn_betak': (0.0, 2.0),
     'L0_attn_bv': (0.0, 0.1),
     'L0_attn_gv': (1.0, 0.2),
     'L0_attn_betav': (0.0, 0.1),
     'L0_attn_bfq': (0.0, 2.0),
     'L0_attn_bfk': (0.0, 2.0),
     'L0_attn_ga': (1.0, 0.2),
     'L0_attn_ba': (0.0, 0.1),
     'L0_attn_b1': (0.0, 0.1),
     'L0_attn_b2': (0.0, 0.1)}
    factors = {'L0_attn_Wfq': 10.911}
    for name, (base, spread) in spreads.items():
        noise = np.random.default_rng([zlib.crc32(name.encode()), seed]).standard_normal(out[name].shape)
        drawn = base * np.exp(spread * noise) if base else spread * noise
        out[name] = jnp.asarray(drawn.astype(out[name].dtype))
    for name, factor in factors.items():
        out[name] = (out[name] * factor).astype(out[name].dtype)
    return out
```

```python
import concourse.bass as bass
from concourse import mybir
from contextlib import ExitStack


B, NQ, D = 32, 64, 512
NK, KD = 512, 256
H, DH = 16, 32
MLP = 2048
E, SLOTS = 8, 8
P = 128
T = B * NQ // P
BPT = P // NQ
DC = D // P
CC = KD // P
KC = NK // P
FC = MLP // P
HC = P // DH
KVW = P + HC
LN_EPS = 1e-5
GATE_MIN = 1e-6
DEN_EPS = 1e-6
SINKHORN_ROUNDS = 8

CONST_COLS = {}
_at = 0
for _name, _width in [("ident", P), ("block_mask", KVW), ("off_batch", P), ("head_of_row", H), ("row_to_feature", P),
                      ("row_is_bc", BPT * DC), ("same_batch", P), ("slot_code", P), ("token_id", 1),
                      ("expert_of_row", E), ("tile_of_row", T), ("ones", P), ("minus_half", 4)]:
    CONST_COLS[_name] = (_at, _at + _width)
    _at += _width
CONST_WIDTH = _at

ROWS = ["x_bv", "bq", "bk", "bv", "gv", "betav", "bfk", "ga", "b2"]
COLS = ["x_bq", "x_bk", "bfq", "betaq", "betak", "gq", "gk", "ga", "ba", "bfk"]


def build(nc, d, out):
    fp32 = mybir.dt.float32
    u32 = mybir.dt.uint32
    ALU = mybir.AluOpType
    ACT = mybir.ActivationFunctionType
    AX = mybir.AxisListType.X

    def after(eng, sem, per_tile, t, k):
        value = t * per_tile + k
        if isinstance(value, int) and value <= 0:
            return
        eng.wait_ge(sem, value)

    ctx = ExitStack()
    with ctx:
        def after_apart(eng, sem, per_tile, t, k):
            value = t * per_tile + k
            if isinstance(value, int):
                after(eng, sem, per_tile, t, k)
            else:
                eng.wait_ge(sem, value).then_inc(waits_passed, 1)

        def sb(name, shape, dt=fp32):
            return ctx.enter_context(nc.sbuf_tensor(name, shape, dt))

        def sem(name):
            return ctx.enter_context(nc.semaphore(name))

        cst = sb("cst", [P, CONST_WIDTH])
        c = {n: cst[:, a:b] for n, (a, b) in CONST_COLS.items()}
        rows = sb("rows", [P, len(ROWS), D])
        row = {n: rows[:, i, :] for i, n in enumerate(ROWS)}
        cols = sb("cols", [P, len(COLS), DC])
        col = {n: cols[:, i, :] for i, n in enumerate(COLS)}
        b1c = sb("b1c", [P, FC])
        res = sb("res", [P, T, D])
        w12 = sb("w12", [P, 2 * FC * D])
        w1 = w12[:, 0:FC * D].rearrange("p (c f) -> p c f", c=DC)
        w2 = w12[:, FC * D:2 * FC * D].rearrange("p (f d) -> p f d", f=FC)
        experts = w12[:, :].rearrange("p (e c d) -> p e c d", e=E, c=DC)
        scratch = w12[:, FC * D:2 * FC * D]
        xwq = scratch[:, 0:2048].rearrange("p (c e) -> p c e", c=DC)
        xwqT = scratch[:, 2048:4096].rearrange("p (c e) -> p c e", c=DC)
        xwk = scratch[:, 4096:5120].rearrange("p (c e) -> p c e", c=CC)
        xwkT = scratch[:, 5120:6144].rearrange("p (c e) -> p c e", c=DC)
        betak_b = scratch[:, 6144:6656].rearrange("p (c e) -> p c e", c=DC)
        xbq_b = scratch[:, 6656:7168].rearrange("p (c e) -> p c e", c=DC)
        proj = sb("proj", [P, 5, DC, D])
        wq, wk, wv, wfq, wfk = (proj[:, i] for i in range(5))
        xwv = sb("xwv", [P, CC, D])
        qk = sb("qk", [P, DC, KD])
        qk_bias = sb("qk_bias", [P, CC])
        q_bk = sb("q_bk", [P, DC])
        bq_bk = sb("bq_bk", [P, 1])
        tq = sb("tq", [P, DC])
        s0feat = sb("s0feat", [P, DC])
        zero_key = sb("zero_key", [P, DC, HC])
        gw = sb("gw", [P, DC, E])
        ctxs = sb("ctxs", [P, BPT, KC, KD])
        ctxT = sb("ctxT", [P, CC, NK])
        lnx = sb("lnx", [P, D])
        lnxT = sb("lnxT", [P, DC, P])
        aT = sb("aT", [P, CC, P])
        s0 = sb("s0", [P, 1])
        amax = sb("amax", [P, 2])
        abias = sb("abias", [P, 1])
        probs = lnx
        lsum = sb("lsum", [P, 1])
        rl = sb("rl", [P, 1])
        pT = sb("pT", [P, KC, P])
        oT = sb("oT", [P, CC, P])
        xn = sb("xn", [P, D])
        xnT = sb("xnT", [P, DC, P])
        zq, zk = (sb(n, [P, D]) for n in ("zq", "zk"))
        zqT, zkT = (sb(n, [P, DC, P]) for n in ("zqT", "zkT"))
        pk = zk
        pqT = sb("pqT", [P, DC, P])
        probe = sb("probe", [P, DC, BPT])
        pm0 = sb("pm0", [P, DC, DH])
        pm1 = sb("pm1", [P, DC, DH])
        lm = sb("lm", [P, P])
        lneg = sb("lneg", [P, 2])
        lsm = sb("lsm", [P, 4])
        scd = sb("scd", [P, P])
        s0bc = sb("s0bc", [P, BPT * DC])
        s0kv = sb("s0kv", [P, BPT * DC, HC])
        sv = sb("sv", [P, DC, KVW])
        zv = sv[:, :, 0:P]
        kv = sb("kv", [P, BPT, DC, KVW])
        den = sb("den", [P, DC, HC])
        on = zq
        hT = sb("hT", [P, DC, P])
        gated = sb("gated", [P, D])
        gT = sb("gT", [P, 2, HC, P])
        yt = sb("yt", [P, D])
        yT = pT
        gates = sb("gates", [P, T, E])
        stat_y = sb("stat_y", [P, T, 2])
        routed_x = proj[:, :, :, :].rearrange("p a c e -> p (a c e)")[:, 0:DC * E * T * P // E]\
            .rearrange("p (c e s) -> p c e s", c=DC, e=E)
        won = ctxs[:, :, :, :].rearrange("p b k c -> p (b k c)").rearrange("p (t s) -> p t s", t=T)
        wonT = rows[:, 0:4, :].rearrange("p a c -> p (a c)").rearrange("p (t s) -> p t s", t=T)
        picks = rows[:, 4:6, :]
        expert_y = rows[:, 6:8, :]
        returned = proj[:, 4, :, :]
        col_inv = sb("col_inv", [P, T * E])
        row_sum = sb("row_sum", [P, T])
        gates_t = sb("gates_t", [P, P])
        top_v = sb("top_v", [P, BPT, SLOTS])
        top_i = sb("top_i", [P, BPT, SLOTS], u32)
        top_f = sb("top_f", [P, BPT, SLOTS])
        slots = sb("slots", [P, E, BPT * SLOTS])
        best = sb("best", [P, 2, HC])
        gate_of = sb("gate_of", [P, T])
        NORMS = ["x", "x1", "q", "k", "v", "o", "y"]
        bn = {n: sb("bn_" + n, [P, 6]) for n in NORMS}
        mv = {n: sb("mv_" + n, [P, 2]) for n in NORMS}
        rstd = {n: sb("rstd_" + n, [P, 1]) for n in NORMS}
        var_eps = {n: sb("var_eps_" + n, [P, 1]) for n in NORMS}
        bank = [ctx.enter_context(nc.psum_tensor(f"bank{i}", [P, 512], fp32)) for i in range(8)]

        def split(ap, n):
            return ap.rearrange("p (a b) -> p a b", a=n)

        ctx_d = d["ctx"].rearrange("(t b) (k p) c -> t p b k c", b=BPT, p=P)
        x_d = d["x"].rearrange("(t b) q d -> (b q) t d", b=BPT)
        slot_rows = nc.dram_tensor("slot_rows", [T, E, BPT * SLOTS, D], fp32, kind="Internal").ap()
        out_d = out.rearrange("(t b) q d -> (b q) t d", b=BPT)

        in_x = sem("in_x")
        in_const = sem("in_const")
        in_cross = sem("in_cross")
        in_small = sem("in_small")
        in_proj = sem("in_proj")
        in_w1 = sem("in_w1")
        in_w2 = sem("in_w2")
        in_ctx = sem("in_ctx")
        prep_bc = sem("prep_bc")
        prep_t = sem("prep_t")
        prep_tcopy = sem("prep_tcopy")
        prep_mm = sem("prep_mm")
        prep_act = sem("prep_act")
        prep_chain = sem("prep_chain")
        qk_ready = sem("qk_ready")
        mlp_bias_ready = sem("mlp_bias_ready")
        stat_kept = sem("stat_kept")
        weights_ready = sem("weights_ready")
        mv_ready = {n: sem("mv_ready_" + n) for n in NORMS}
        rstd_ready = {n: sem("rstd_ready_" + n) for n in NORMS}
        waits_passed = sem("waits_passed")
        bn_done = {n: sem("bn_done_" + n) for n in NORMS}
        eps_done = {n: sem("eps_done_" + n) for n in NORMS}
        a_t = sem("a_t")
        a_tcopy = sem("a_tcopy")
        a_mm = sem("a_mm")
        a_used = sem("a_used")
        lnx_ready = sem("lnx_ready")
        s0_ready = sem("s0_ready")
        xbv_ready = sem("xbv_ready")
        scores0_done = sem("scores0_done")
        amax_done = sem("amax_done")
        abias_ready = sem("abias_ready")
        rl_ready = sem("rl_ready")
        x1_ready = sem("x1_ready")
        b_mm = sem("b_mm")
        b2_used = sem("b2_used")
        b3_used = sem("b3_used")
        xn_ready = sem("xn_ready")
        res_xn = sem("res_xn")
        y_raw = {n: sem("y_raw_" + n) for n in "qkv"}
        z_ready = {n: sem("z_ready_" + n) for n in "qkv"}
        v_scaled = sem("v_scaled")
        v_ready = sem("v_ready")
        tanh_q = sem("tanh_q")
        pqT_ready = sem("pqT_ready")
        tanh_k = sem("tanh_k")
        pk_ready = sem("pk_ready")
        probe_chain = sem("probe_chain")
        pm_ready = sem("pm_ready")
        lg_mm = sem("lg_mm")
        lm_chain = sem("lm_chain")
        lm_ready = sem("lm_ready")
        exp_ready = sem("exp_ready")
        sc_chain = sem("sc_chain")
        score_ready = sem("score_ready")
        ex_mm = sem("ex_mm")
        sv_ready = sem("sv_ready")
        kv_ready = sem("kv_ready")
        den_chain = sem("den_chain")
        o_raw = sem("o_raw")
        za_ready = sem("za_ready")
        gated_chain = sem("gated_chain")
        res_ready = sem("res_ready")
        h1_mm = sem("h1_mm")
        g_ready = sem("g_ready")
        h2_mm = sem("h2_mm")
        x2_ready = sem("x2_ready")
        yt_ready = sem("yt_ready")
        yT_mm = sem("yT_mm")
        yT_ready = sem("yT_ready")
        gl_mm = sem("gl_mm")
        gl_used = sem("gl_used")

        out_done = sem("out_done")
        cs_mm = sem("cs_mm")
        sink_chain = sem("sink_chain")
        sink_done = sem("sink_done")
        gates_mm = sem("gates_mm")
        top_chain = sem("top_chain")
        picks_ready = sem("picks_ready")
        picks_mm = sem("picks_mm")
        won_chain = sem("won_chain")
        won_ready = sem("won_ready")
        wonT_mm = sem("wonT_mm")
        wonT_ready = sem("wonT_ready")
        y_again = sem("y_again")
        gather_mm = sem("gather_mm")
        gathered = sem("gathered")
        in_experts = sem("in_experts")
        expert_mm = sem("expert_mm")
        expert_copied = sem("expert_copied")
        expert_stored = [sem(f"expert_stored{k}") for k in range(2)]
        in_returned = [sem(f"in_returned{k}") for k in range(4)]
        scatter_mm = sem("scatter_mm")
        x3_ready = sem("x3_ready")

        A_T, A_MM, B_MM, B2, B3 = 6, 4, 15, 8, 7
        O_MM = 3
        SMALL = 16 * (len(ROWS) + len(COLS) + 3)

        block = ctx.enter_context(nc.Block())

        def rounds(eng, body):
            for i in range(4):
                body(i, i, i - 1 if i >= 1 else None, i - 2 if i >= 2 else None, i - 3 if i >= 3 else None)
            with eng.Fori(4, T) as i:
                body(i, i, i - 1, i - 2, i - 3)
            for i in range(T, T + 3):
                body(i, None, i - 1 if i - 1 < T else None, i - 2 if i - 2 < T else None, i - 3)

        @block.sync
        def _(sp):
            sp.dma_start(cst[:, :], d["consts"]).then_inc(in_const, 16)
            sp.dma_start(xwq, d["x_wq"].rearrange("(c p) e -> p c e", p=P)).then_inc(in_cross, 16)
            sp.dma_start(xwk, d["x_wk"].rearrange("(c p) e -> p c e", p=P)).then_inc(in_cross, 16)
            sp.dma_start(res[:, 0:4, :], x_d[:, 0:4, :]).then_inc(in_x, 16)
            sp.dma_start(ctxs[:, 0], ctx_d[0, :, 0]).then_inc(in_ctx, 16)
            sp.dma_start(ctxs[:, 1], ctx_d[0, :, 1]).then_inc(in_ctx, 16)
            sp.dma_start(xwv[:, :, :], d["x_wv"].rearrange("(c p) e -> p c e", p=P)).then_inc(in_cross, 16)
            for n, w in (("wfq", wfq), ("wfk", wfk), ("wq", wq), ("wk", wk), ("wv", wv)):
                sp.dma_start(w, d[n].rearrange("(c p) e -> p c e", p=P)).then_inc(in_proj, 16)

            def reload(i, a, b, m, g):
                if a is not None and not (isinstance(a, int) and a == 0):
                    after(sp, a_mm, A_MM, a - 1, O_MM)
                    sp.dma_start(ctxs[:, 0], ctx_d[a, :, 0]).then_inc(in_ctx, 16)
                    sp.dma_start(ctxs[:, 1], ctx_d[a, :, 1]).then_inc(in_ctx, 16)
                if isinstance(i, int) and i == 1:
                    sp.dma_start(w1, d["w1"].rearrange("(c p) f -> p c f", p=P)).then_inc(in_w1, 16)
                    sp.dma_start(res[:, 4:T, :], x_d[:, 4:T, :]).then_inc(in_x, 16)
                    sp.wait_ge(prep_mm, 2)
                    sp.dma_start(w2, d["w2"].rearrange("(f p) e -> p f e", p=P)).then_inc(in_w2, 16)
            rounds(sp, reload)
            sp.wait_ge(h2_mm, 4 * T)
            for e in range(E):
                sp.dma_start(experts[:, e], d["experts"][e].rearrange("(c p) f -> p c f", p=P)).then_inc(in_experts, 16)
            for e in range(E):
                for half in range(2):
                    u = 2 * e + half
                    sp.wait_ge(expert_copied, u + 1)
                    sp.dma_start(slot_rows[half * T // 2:(half + 1) * T // 2, e, :, :], expert_y[:, u % 2, :])\
                        .then_inc(expert_stored[u % 2], 16)
            for k in range(2):
                sp.wait_ge(expert_stored[k], 16 * E)
            for t in range(T + 3):
                if t < T:
                    if t >= 4:
                        sp.wait_ge(scatter_mm, t - 3)
                    sp.dma_start(returned[:, t % 4, :], slot_rows[t].rearrange("e s f -> (e s) f"))\
                        .then_inc(in_returned[t % 4], 16)
                if t >= 3:
                    sp.wait_ge(x3_ready, t - 2)
                    sp.dma_start(out_d[:, t - 3, :], res[:, t - 3, :]).then_inc(out_done, 16)
            sp.wait_ge(out_done, 16 * T)

        @block.gpsimd
        def _(pool):
            pool.wait_ge(in_const, 16)
            pool.wait_ge(in_small, SMALL)
            pool.wait_ge(prep_bc, 1)

            def rsqrt(n, t):
                after_apart(pool, mv_ready[n], 1, t, 1)
                pool.tensor_scalar(var_eps[n][:, :], mv[n][:, 1:2], LN_EPS, None, ALU.add).then_inc(eps_done[n], 1)
                after_apart(pool, eps_done[n], 1, t, 1)
                pool.tensor_tensor(rstd[n][:, :], var_eps[n][:, :], c["minus_half"][:, 0:1], ALU.pow)\
                    .then_inc(rstd_ready[n], 1)

            def body(i, a, b, m, g):
                if a is not None:
                    rsqrt("x", a)
                if b is not None:
                    after_apart(pool, xn_ready, 1, b, 1)
                    pool.tensor_tensor(res[:, b, :], res[:, b, :], xn[:, :], ALU.add).then_inc(res_xn, 1)
                    rsqrt("q", b)
                if a is not None:
                    after_apart(pool, lnx_ready, 1, a, 1)
                    pool.tensor_tensor(res[:, a, :], res[:, a, :], row["x_bv"], ALU.add).then_inc(xbv_ready, 1)
                if b is not None:
                    rsqrt("k", b)
                    rsqrt("v", b)
                    after_apart(pool, z_ready["v"], 1, b, 1)
                    pool.tensor_tensor(zv, zv, split(row["gv"], DC), ALU.mult).then_inc(v_scaled, 1)
                    after_apart(pool, v_scaled, 1, b, 1)
                    pool.tensor_tensor(zv, zv, split(row["betav"], DC), ALU.add).then_inc(v_ready, 1)
                    after_apart(pool, tanh_k, 1, b, 1)
                    pool.tensor_scalar(pk[:, :], pk[:, :], 1.0, None, ALU.add).then_inc(pk_ready, 1)
                if a is not None:
                    rsqrt("x1", a)
                if b is not None:
                    rsqrt("o", b)
                if m is not None:
                    rsqrt("y", m)
                if b is not None:
                    after_apart(pool, za_ready, 1, b, 1)
                    after_apart(pool, res_xn, 1, b, 1)
                    pool.tensor_tensor(gated[:, :], on[:, :], row["ga"], ALU.mult).then_inc(gated_chain, 1)
                    pool.tensor_tensor(res[:, b, :], res[:, b, :], row["b2"], ALU.add).then_inc(gated_chain, 1)
                    after_apart(pool, gated_chain, 2, b, 2)
                    pool.tensor_tensor(res[:, b, :], res[:, b, :], gated[:, :], ALU.add).then_inc(res_ready, 1)
            rounds(pool, body)

        @block.scalar
        def _(act):
            for n in COLS:
                act.dma_start(col[n], d["c_" + n].rearrange("(c p) -> p c", p=P), allow_slow_non_contiguous=True).then_inc(in_small, 16)
            act.dma_start(b1c[:, :], d["b1"].rearrange("(c p) -> p c", p=P), allow_slow_non_contiguous=True).then_inc(in_small, 16)
            act.dma_start(gw[:, :, :], d["gate_w"].rearrange("(c p) e -> p c e", p=P)).then_inc(in_small, 16)
            for n in ROWS:
                act.dma_start(row[n], d["r_" + n].partition_broadcast(P)).then_inc(in_small, 16)
            act.dma_start(on[:, :], d["c_ba"].partition_broadcast(P)).then_inc(in_small, 16)
            act.wait_ge(in_small, SMALL)
            act.activation(s0feat[:, :], col["bfk"], ACT.Tanh).then_inc(prep_act, 1)

            def body(i, a, b, m, g):
                def gelu(j):
                    after(act, h1_mm, 4, m, j + 1)
                    after(act, h2_mm, 4, m, j - 1)
                    for f in range(HC):
                        g_ins = act.activation(gT[:, j % 2, f, :], bank[5 + j % 2][:, f * P:(f + 1) * P], ACT.Gelu,
                                               bias=b1c[:, j * HC + f:j * HC + f + 1])
                    g_ins.then_inc(g_ready, 1)
                if b is not None:
                    after(act, b_mm, B_MM, b, 1)
                    act.copy(xnT[:, :, :], split(bank[2][:, :], DC)).then_inc(b2_used, 1)
                if m is not None:
                    if isinstance(m, int) and m == 0:
                        act.wait_ge(mlp_bias_ready, 1)
                    gelu(0)
                if a is not None:
                    after(act, a_t, A_T, a, 1)
                    act.copy(lnxT[:, :, :], split(bank[0][:, :], DC)).then_inc(a_tcopy, 1)
                if g is not None:
                    after(act, yT_mm, 1, g, 1)
                    act.copy(yT[:, :, :], split(bank[7][:, :], DC)).then_inc(yT_ready, 1)
                if m is not None:
                    gelu(1)
                if a is not None:
                    after(act, a_t, A_T, a, 3)
                    act.copy(ctxT[:, 1, :], bank[0][:, :]).then_inc(a_tcopy, 1)
                if b is not None:
                    after(act, b_mm, B_MM, b, 6)
                    act.copy(zkT[:, :, :], split(bank[3][:, :], DC)).then_inc(b3_used, 1)
                if m is not None:
                    gelu(2)
                if b is not None:
                    after(act, b_mm, B_MM, b, 7)
                    for f in range(DC):
                        t_ins = act.activation(pqT[:, f, :], bank[2][:, f * P:(f + 1) * P], ACT.Tanh,
                                               bias=tq[:, f:f + 1])
                    t_ins.then_inc(tanh_q, 1)
                if a is not None:
                    after(act, a_t, A_T, a, 5)
                    act.copy(ctxT[:, 1, :], bank[0][:, :]).then_inc(a_tcopy, 1)
                if b is not None:
                    after(act, b3_used, B3, b, 4)
                    act.activation(pk[:, :], pk[:, :], ACT.Tanh).then_inc(tanh_k, 1)
                if a is not None:
                    after(act, abias_ready, 1, a, 1)
                    act.activation(probs[:, :], bank[1][:, :], ACT.Exp, bias=abias[:, 0:1],
                                   accum_out=lsum[:, 0:1]).then_inc(a_used, 1)
                if b is not None:
                    after(act, lm_ready, 1, b, 1)
                    act.activation(scd[:, :], lm[:, :], ACT.Exp, bias=lneg[:, 1:2], accum_out=lsm[:, 0:1])
                    act.activation(lsm[:, 1:2], lneg[:, 1:2], ACT.Exp).then_inc(exp_ready, 1)
                if m is not None:
                    gelu(3)
                if b is not None:
                    after(act, b_mm, B_MM, b, 15)
                    act.copy(hT[:, :, :], split(bank[2][:, :], DC)).then_inc(b2_used, 1)
            rounds(act, body)
            for k in range(T // 4):
                act.wait_ge(wonT_mm, k + 1)
                act.copy(wonT[:, 4 * k:4 * k + 4, :], split(bank[4 + k % 2][:, :], 4)).then_inc(wonT_ready, 1)
            for t in range(T):
                act.wait_ge(gather_mm, t + 1)
                act.copy(routed_x[:, :, :, t * BPT * SLOTS:(t + 1) * BPT * SLOTS],
                         bank[4 + t % 2][:, :].rearrange("p (c e s) -> p c e s", c=DC, e=E)).then_inc(gathered, 1)
            for u in range(2 * E):
                act.wait_ge(expert_mm, u + 1)
                if u >= 2:
                    act.wait_ge(expert_stored[u % 2], 16 * (u // 2))
                act.copy(expert_y[:, u % 2, :], bank[6 + u % 2][:, :]).then_inc(expert_copied, 1)

        @block.vector
        def _(dve):
            def bc(ap, n, shape):
                return ap.unsqueeze(n).broadcast_to(shape)

            def stats(n, t, ap):
                dve.bn_stats(bn[n][:, :], ap).then_inc(bn_done[n], 1)
                after_apart(dve, bn_done[n], 1, t, 1)
                dve.bn_aggr(mv[n][:, :], bn[n][:, :]).then_inc(mv_ready[n], 1)

            def norm(n, t, out_, in_):
                after(dve, rstd_ready[n], 1, t, 1)
                return dve.tensor_scalar(out_, in_, mv[n][:, 0:1], rstd[n][:, 0:1], ALU.subtract, ALU.mult)

            dve.memset(pm0[:, :, :], 0.0)
            dve.memset(pm1[:, :, :], 0.0)
            dve.wait_ge(in_const, 16)
            dve.wait_ge(prep_t, 1)
            for k in range(DC):
                dve.tensor_copy(xwqT[:, k, :], bank[k][:, :])
            dve.tensor_copy(xwkT[:, 0:2, :], split(bank[4][:, :], 2))
            dve.tensor_copy(xwkT[:, 2:4, :], split(bank[5][:, :], 2)).then_inc(prep_tcopy, 1)
            dve.wait_ge(in_small, SMALL)
            for k in range(DC):
                dve.tensor_scalar(betak_b[:, k, :], c["ones"], col["betak"][:, k:k + 1], None, ALU.mult)
                dve.tensor_scalar(xbq_b[:, k, :], c["ones"], col["x_bq"][:, k:k + 1], None, ALU.mult)
            dve.tensor_tensor(row["b2"], row["b2"], on[:, :], ALU.add).then_inc(prep_bc, 1)
            dve.wait_ge(prep_mm, 1)
            dve.tensor_copy(qk[:, 0:2, :], split(bank[6][:, :], 2))
            dve.tensor_copy(qk[:, 2:4, :], split(bank[7][:, :], 2))
            dve.tensor_copy(qk_bias[:, :], bank[0][:, 0:CC])
            dve.tensor_copy(q_bk[:, :], bank[0][:, 8:8 + DC])
            dve.tensor_copy(bq_bk[:, :], bank[0][:, 16:17]).then_inc(qk_ready, 1)

            def prepare_attention():
                dve.wait_ge(prep_mm, 2)
                dve.tensor_tensor(tq[:, :], bank[3][:, 0:DC], col["bfq"], ALU.add)
                dve.tensor_tensor(row["bfk"], bank[2][:, :], row["bfk"], ALU.add)
                for k in range(DC):
                    dve.tensor_scalar(wfq[:, k, :], wfq[:, k, :], col["gq"][:, k:k + 1], None, ALU.mult)
                    dve.tensor_scalar(wfk[:, k, :], wfk[:, k, :], col["gk"][:, k:k + 1], None, ALU.mult)
                dve.wait_ge(prep_act, 1)
                dve.tensor_scalar(s0feat[:, :], s0feat[:, :], 1.0, None, ALU.add).then_inc(prep_chain, 1)
                dve.wait_ge(prep_chain, 1)
                dve.tensor_tensor(zero_key[:, :, :], bc(s0feat[:, :], 2, [P, DC, HC]),
                                  bc(c["block_mask"][:, P:KVW], 1, [P, DC, HC]), ALU.mult)
                dve.tensor_scalar(col["gq"], col["gq"], 1.0 / (NQ * DH ** 0.5), None, ALU.mult)
                dve.tensor_scalar(col["betaq"], col["betaq"], 1.0 / DH ** 0.5, None, ALU.mult).then_inc(weights_ready, 1)
                dve.wait_ge(weights_ready, 1)

            def prepare_mlp():
                dve.wait_ge(prep_mm, 3)
                dve.tensor_tensor(b1c[:, :], bank[5][:, 0:FC], b1c[:, :], ALU.add).then_inc(mlp_bias_ready, 1)
                for k in range(DC):
                    last = dve.tensor_scalar(w1[:, k, :], w1[:, k, :], col["ga"][:, k:k + 1], None, ALU.mult)
                last.then_inc(weights_ready, 1)
                dve.wait_ge(in_x, 32)

            def project(n, z, bk, k, used, per_tile, count, b):
                after(dve, b_mm, B_MM, b, k)
                dve.tensor_tensor(z, split(bank[bk][:, :], DC), split(row["b" + n], DC), ALU.add).then_inc(used, 1)
                after(dve, used, per_tile, b, count)
                stats(n, b, z)

            def body(i, a, b, m, g):
                if isinstance(i, int) and i == 0:
                    dve.wait_ge(in_x, 16)
                if isinstance(i, int) and i == 1:
                    prepare_attention()
                if isinstance(i, int) and i == 2:
                    prepare_mlp()
                if a is not None:
                    stats("x", a, res[:, a, :])
                    norm("x", a, lnx[:, :], res[:, a, :]).then_inc(lnx_ready, 1)
                if b is not None:
                    after(dve, res_ready, 1, b, 0)
                    project("q", split(zq[:, :], DC), 3, 2, b3_used, B3, 1, b)
                if g is not None:
                    after(dve, gl_mm, 1, g, 1)
                    dve.tensor_scalar(gates[:, g, :], bank[7][:, 0:E], GATE_MIN, None, ALU.max).then_inc(gl_used, 1)
                if a is not None:
                    after(dve, a_mm, A_MM, a, 1)
                    for k in range(CC):
                        dve.tensor_scalar(aT[:, k, :], bank[1][:, k * P:(k + 1) * P], qk_bias[:, k:k + 1], None, ALU.add)
                    dve.tensor_tensor(s0[:, :], bank[1][:, 256:257], bq_bk[:, :], ALU.add).then_inc(a_used, 1)
                if b is not None:
                    norm("q", b, zq[:, :], zq[:, :]).then_inc(z_ready["q"], 1)
                    project("k", split(zk[:, :], DC), 2, 3, b2_used, B2, 2, b)
                if a is not None:
                    after(dve, a_t, A_T, a, 2)
                    dve.tensor_copy(ctxT[:, 0, :], bank[0][:, :]).then_inc(a_tcopy, 1)
                if b is not None:
                    norm("k", b, zk[:, :], zk[:, :]).then_inc(z_ready["k"], 1)
                    project("v", zv, 3, 4, b3_used, B3, 2, b)
                    after(dve, b_mm, B_MM, b, 5)
                    dve.tensor_copy(zqT[:, :, :], split(bank[2][:, :], DC)).then_inc(b2_used, 1)
                    norm("v", b, zv, zv).then_inc(z_ready["v"], 1)
                    after(dve, b2_used, B2, b, 3)
                    dve.tensor_reduce(probe[:, :, :].rearrange("p c b -> p (c b)"),
                                      zqT[:, :, :].rearrange("p c (b q) -> p (c b) q", b=BPT), AX, ALU.add)\
                        .then_inc(probe_chain, 1)
                    after(dve, probe_chain, 4, b, 1)
                    dve.tensor_tensor(probe[:, :, :], probe[:, :, :], bc(col["gq"], 2, [P, DC, BPT]), ALU.mult)\
                        .then_inc(probe_chain, 1)
                    after(dve, probe_chain, 4, b, 2)
                    dve.tensor_tensor(probe[:, :, :], probe[:, :, :], bc(col["betaq"], 2, [P, DC, BPT]), ALU.add)\
                        .then_inc(probe_chain, 1)
                    after(dve, probe_chain, 4, b, 3)
                    dve.tensor_tensor(pm0[:, :, 0:BPT * HC].rearrange("p c (b h) -> p c b h", b=BPT),
                                      bc(probe[:, :, :], 3, [P, DC, BPT, HC]),
                                      c["block_mask"][:, P:KVW].unsqueeze(1).unsqueeze(1).broadcast_to([P, DC, BPT, HC]),
                                      ALU.mult).then_inc(probe_chain, 1)
                    after(dve, probe_chain, 4, b, 4)
                    dve.tensor_tensor(pm1[:, :, 0:BPT * HC], pm0[:, :, 0:BPT * HC],
                                      bc(col["gk"], 2, [P, DC, BPT * HC]), ALU.mult).then_inc(pm_ready, 1)
                if a is not None:
                    after(dve, a_t, A_T, a, 4)
                    dve.tensor_copy(ctxT[:, 0, :], bank[0][:, :]).then_inc(a_tcopy, 1)
                if b is not None:
                    after(dve, tanh_q, 1, b, 1)
                    dve.tensor_scalar(pqT[:, :, :], pqT[:, :, :], 1.0, None, ALU.add).then_inc(b2_used, 1)
                    after(dve, b_mm, B_MM, b, 8)
                    dve.tensor_tensor(pk[:, :], bank[3][:, :], row["bfk"], ALU.add).then_inc(b3_used, 1)
                if a is not None:
                    after(dve, a_mm, A_MM, a, 2)
                    dve.tensor_reduce(amax[:, 0:1], bank[1][:, :], AX, ALU.max).then_inc(amax_done, 1)
                    after(dve, amax_done, 2, a, 1)
                    dve.tensor_tensor(amax[:, 1:2], amax[:, 0:1], s0[:, :], ALU.add).then_inc(amax_done, 1)
                    after(dve, amax_done, 2, a, 2)
                    dve.tensor_tensor(abias[:, :], s0[:, :], amax[:, 1:2], ALU.subtract).then_inc(abias_ready, 1)
                if b is not None:
                    after(dve, lg_mm, 1, b, 1)
                    dve.tensor_copy(lsm[:, 3:4], bank[4][:, P:P + 1]).then_inc(lm_chain, 1)
                    after(dve, lm_chain, 3, b, 1)
                    dve.scalar_tensor_tensor(lm[:, :], bank[4][:, 0:P], lsm[:, 3:4], c["off_batch"], ALU.add, ALU.add)\
                        .then_inc(lm_chain, 1)
                    after(dve, lm_chain, 3, b, 2)
                    dve.tensor_reduce(lneg[:, 0:1], lm[:, :], AX, ALU.max).then_inc(lm_chain, 1)
                    after(dve, lm_chain, 3, b, 3)
                    dve.tensor_scalar(lneg[:, 1:2], lneg[:, 0:1], 0.0, -1.0, ALU.max, ALU.mult).then_inc(lm_ready, 1)
                if a is not None:
                    after(dve, a_t, A_T, a, 6)
                    dve.tensor_copy(pT[:, :, :], split(bank[0][:, :], KC)).then_inc(a_tcopy, 1)
                    dve.reciprocal(rl[:, :], lsum[:, :]).then_inc(rl_ready, 1)
                if b is not None:
                    after(dve, exp_ready, 1, b, 1)
                    dve.tensor_tensor(lsm[:, 2:3], lsm[:, 0:1], lsm[:, 1:2], ALU.add).then_inc(sc_chain, 1)
                    after(dve, sc_chain, 2, b, 1)
                    dve.reciprocal(lsm[:, 2:3], lsm[:, 2:3]).then_inc(sc_chain, 1)
                    after(dve, sc_chain, 2, b, 2)
                    dve.tensor_scalar(scd[:, :], scd[:, :], lsm[:, 2:3], None, ALU.mult)
                    dve.tensor_scalar(s0bc[:, :], c["row_is_bc"], lsm[:, 1:2], lsm[:, 2:3], ALU.mult, ALU.mult)\
                        .then_inc(score_ready, 1)
                    after(dve, ex_mm, 1, b, 1)
                    after(dve, v_ready, 1, b, 1)
                    score = bank[4][:, 256:256 + H].rearrange("p (c h) -> p c h", c=DC)
                    zvh = zv.rearrange("p c (h e) -> p c h e", h=HC)
                    dve.tensor_tensor(zvh, zvh,
                                      bc(score, 3, [P, DC, HC, DH]), ALU.mult)
                    dve.tensor_copy(sv[:, :, P:KVW], score)
                    dve.tensor_tensor(s0kv[:, :, :].rearrange("p (b c) h -> p b c h", b=BPT),
                                      bc(bank[4][:, 288:288 + BPT * DC].rearrange("p (b c) -> p b c", b=BPT), 3,
                                         [P, BPT, DC, HC]),
                                      zero_key[:, :, :].unsqueeze(1).broadcast_to([P, BPT, DC, HC]), ALU.mult)\
                        .then_inc(sv_ready, 1)
                if a is not None:
                    after(dve, a_mm, A_MM, a, 3)
                    dve.tensor_copy(oT[:, :, :], split(bank[1][:, 0:CC * P], CC)).then_inc(a_used, 1)
                if b is not None:
                    for k in range(4):
                        bt, half = k // 2, k % 2
                        after(dve, b_mm, B_MM, b, 9 + k)
                        dve.tensor_tensor(kv[:, bt, 2 * half:2 * half + 2, :], split(bank[2 + half][:, 0:2 * KVW], 2),
                                          bc(c["block_mask"], 1, [P, 2, KVW]), ALU.mult)\
                            .then_inc(b3_used if half else b2_used, 1)
                    after(dve, b2_used, B2, b, 6)
                    after(dve, b3_used, B3, b, 6)
                    after(dve, sv_ready, 1, b, 1)
                    dve.tensor_tensor(kv[:, :, :, P:KVW], kv[:, :, :, P:KVW],
                                      s0kv[:, :, :].rearrange("p (b c) h -> p b c h", b=BPT), ALU.add).then_inc(kv_ready, 1)
                if a is not None:
                    after(dve, a_mm, A_MM, a, 4)
                    after(dve, xbv_ready, 1, a, 1)
                    after(dve, rl_ready, 1, a, 1)
                    dve.scalar_tensor_tensor(res[:, a, :], bank[1][:, :], rl[:, 0:1], res[:, a, :], ALU.mult, ALU.add)\
                        .then_inc(a_used, 1)
                    after_apart(dve, a_used, A_MM, a, 4)
                    stats("x1", a, res[:, a, :])
                if b is not None:
                    for half in range(2):
                        after(dve, b_mm, B_MM, b, 13 + half)
                        pv = split(bank[2 + half][:, 0:2 * KVW], 2)
                        dn = den[:, 2 * half:2 * half + 2, :]
                        dve.tensor_scalar(dn, pv[:, :, P:KVW], DEN_EPS, None, ALU.add).then_inc(den_chain, 1)
                        after(dve, den_chain, 4, b, 2 * half + 1)
                        dve.reciprocal(dn, dn).then_inc(den_chain, 1)
                        after(dve, den_chain, 4, b, 2 * half + 2)
                        dve.tensor_tensor(on[:, half * 256:(half + 1) * 256].rearrange("p (c h e) -> p c h e", c=2, h=HC),
                                          pv[:, :, 0:P].rearrange("p c (h e) -> p c h e", h=HC),
                                          bc(dn, 3, [P, 2, HC, DH]), ALU.mult).then_inc(b3_used if half else b2_used, 1)
                    after(dve, b2_used, B2, b, 7)
                    after(dve, b3_used, B3, b, 7)
                    stats("o", b, on[:, :])
                if a is not None:
                    norm("x1", a, xn[:, :], res[:, a, :]).then_inc(xn_ready, 1)
                if b is not None:
                    norm("o", b, on[:, :], on[:, :]).then_inc(za_ready, 1)
                if m is not None:
                    after(dve, h2_mm, 4, m, 4)
                    after(dve, res_ready, 1, m, 1)
                    dve.tensor_tensor(res[:, m, :], bank[7][:, :], res[:, m, :], ALU.add).then_inc(x2_ready, 1)
                    after_apart(dve, x2_ready, 1, m, 1)
                    stats("y", m, res[:, m, :])
                    norm("y", m, yt[:, :], res[:, m, :]).then_inc(yt_ready, 1)
                    dve.tensor_copy(stat_y[:, m, 0:1], mv["y"][:, 0:1])
                    dve.tensor_copy(stat_y[:, m, 1:2], rstd["y"][:, 0:1]).then_inc(stat_kept, 1)
            rounds(dve, body)

            dve.wait_ge(gl_used, T)
            gates_flat = gates[:, :, :].rearrange("p t e -> p (t e)")
            dve.wait_ge(stat_kept, T).then_inc(sink_done, 1)
            with dve.Fori(0, SINKHORN_ROUNDS) as r:
                after(dve, cs_mm, 1, r, 1)
                dve.reciprocal(col_inv[:, :], bank[0][:, 0:T * E]).then_inc(sink_chain, 1)
                after(dve, sink_chain, 4, r, 1)
                dve.tensor_tensor(gates_flat, gates_flat, col_inv[:, :], ALU.mult).then_inc(sink_chain, 1)
                after(dve, sink_chain, 4, r, 2)
                dve.tensor_reduce(row_sum[:, :], gates[:, :, :], AX, ALU.add).then_inc(sink_chain, 1)
                after(dve, sink_chain, 4, r, 3)
                dve.reciprocal(row_sum[:, :], row_sum[:, :]).then_inc(sink_chain, 1)
                after(dve, sink_chain, 4, r, 4)
                dve.tensor_tensor(gates[:, :, :], gates[:, :, :], bc(row_sum[:, :], 2, [P, T, E]), ALU.mult)\
                    .then_inc(sink_done, 1)
            dve.wait_ge(gates_mm, 1)
            dve.tensor_copy(gates_t[:, :], bank[1][:, 0:P]).then_inc(top_chain, 1)
            dve.wait_ge(top_chain, 1)
            for b in range(BPT):
                dve.max(top_v[:, b, :], gates_t[:, b * NQ:(b + 1) * NQ]).then_inc(top_chain, 1)
            dve.wait_ge(top_chain, 1 + BPT)
            for b in range(BPT):
                dve.max_index(top_i[:, b, :], top_v[:, b, :], gates_t[:, b * NQ:(b + 1) * NQ]).then_inc(top_chain, 1)
            dve.wait_ge(top_chain, 1 + 2 * BPT)
            for b in range(BPT):
                last = dve.tensor_scalar(top_f[:, b, :], top_i[:, b, :], float(b * NQ), None, ALU.add)
            last.then_inc(top_chain, 1)
            dve.wait_ge(top_chain, 2 + 2 * BPT)
            dve.tensor_tensor(slots[:, :, :], bc(top_f[:, :, :].rearrange("p b s -> p (b s)"), 1, [P, E, BPT * SLOTS]),
                              bc(c["expert_of_row"], 2, [P, E, BPT * SLOTS]), ALU.mult).then_inc(top_chain, 1)
            dve.wait_ge(top_chain, 3 + 2 * BPT)
            for k in range(T // 4):
                if k >= 2:
                    dve.wait_ge(picks_mm, k - 1)
                pk4 = picks[:, k % 2, :].rearrange("p (t s) -> p t s", t=4)
                dve.tensor_tensor(pk4, bc(slots[:, :, :].rearrange("p e s -> p (e s)"), 1, [P, 4, P]),
                                  bc(c["tile_of_row"][:, 4 * k:4 * k + 4], 2, [P, 4, P]), ALU.mult).then_inc(picks_ready, 1)
                w4 = won[:, 4 * k:4 * k + 4, :]
                dve.wait_ge(picks_mm, k + 1)
                dve.scalar_tensor_tensor(w4, split(bank[2 + k % 2][:, :], 4), c["token_id"],
                                         bc(c["slot_code"], 1, [P, 4, P]), ALU.is_equal, ALU.mult).then_inc(won_chain, 1)
                dve.wait_ge(won_chain, 5 * k + 1)
                dve.tensor_reduce(best[:, 0, :], w4, AX, ALU.max).then_inc(won_chain, 1)
                dve.wait_ge(won_chain, 5 * k + 2)
                dve.tensor_scalar(best[:, 1, :], best[:, 0, :], 0.5, None, ALU.max).then_inc(won_chain, 1)
                dve.wait_ge(won_chain, 5 * k + 3)
                dve.tensor_tensor(w4, w4, bc(best[:, 1, :], 2, [P, 4, P]), ALU.is_equal).then_inc(won_chain, 1)
                dve.wait_ge(won_chain, 5 * k + 4)
                g4 = yt[:, :].rearrange("p (t e s) -> p t e s", t=4, e=E)
                dve.tensor_tensor(g4, w4.rearrange("p t (e s) -> p t e s", e=E),
                                  bc(gates[:, 4 * k:4 * k + 4, :], 3, [P, 4, E, BPT * SLOTS]), ALU.mult).then_inc(won_chain, 1)
                dve.wait_ge(won_chain, 5 * k + 5)
                dve.tensor_reduce(gate_of[:, 4 * k:4 * k + 4], yt[:, :].rearrange("p (t s) -> p t s", t=4), AX, ALU.add)\
                    .then_inc(won_ready, 1)
            dve.wait_ge(stat_kept, T)
            dve.wait_ge(won_ready, T // 4)
            ring = (zq, zk)
            for t in range(T):
                if t >= 2:
                    dve.wait_ge(gather_mm, t - 1)
                dve.tensor_scalar(ring[t % 2][:, :], res[:, t, :], stat_y[:, t, 0:1], stat_y[:, t, 1:2],
                                  ALU.subtract, ALU.mult).then_inc(y_again, 1)
            for t in range(T):
                dve.wait_ge(scatter_mm, t + 1)
                dve.scalar_tensor_tensor(res[:, t, :], bank[2 + t % 2][:, :], gate_of[:, t:t + 1], res[:, t, :],
                                         ALU.mult, ALU.add).then_inc(x3_ready, 1)

        @block.tensor
        def _(pe):
            ident = c["ident"]

            def transposes(bk, in_, n):
                for k in range(n):
                    ins = pe.transpose(bank[bk][:, k * P:(k + 1) * P], in_(k), ident)
                return ins

            def product(out_, pairs):
                for k, (lhsT, rhs) in enumerate(pairs):
                    ins = pe.matmul(out_, lhsT, rhs, start=(k == 0), stop=(k == len(pairs) - 1))
                return ins

            pe.wait_ge(in_const, 16)
            pe.wait_ge(in_cross, 48)
            for e in range(DC):
                transposes(e, lambda k: xwq[:, k, e * P:(e + 1) * P], DC)
            for e in range(DC):
                for k in range(CC):
                    at = (e % 2) * KD + k * P
                    last = pe.transpose(bank[4 + e // 2][:, at:at + P], xwk[:, k, e * P:(e + 1) * P], ident)
            last.then_inc(prep_t, 1)
            pe.wait_ge(prep_tcopy, 1)
            for k in range(DC):
                product(bank[6 + k // 2][:, (k % 2) * KD:(k % 2 + 1) * KD],
                        [(xwqT[:, e, k * P:(k + 1) * P], xwkT[:, e, :]) for e in range(DC)])
            pe.wait_ge(prep_bc, 1)
            for k in range(CC):
                product(bank[0][:, k:k + 1], [(xwkT[:, e, k * P:(k + 1) * P], col["x_bq"][:, e:e + 1]) for e in range(DC)])
            for k in range(DC):
                product(bank[0][:, 8 + k:9 + k],
                        [(xwqT[:, e, k * P:(k + 1) * P], col["x_bk"][:, e:e + 1]) for e in range(DC)])
            product(bank[0][:, 16:17], [(xbq_b[:, e, :], col["x_bk"][:, e:e + 1]) for e in range(DC)]).then_inc(prep_mm, 1)
            pe.wait_ge(qk_ready, 1)

            def prepare_attention():
                pe.wait_ge(in_proj, 80)
                product(bank[2][:, :], [(betak_b[:, e, :], wfk[:, e, :]) for e in range(DC)])
                for f in range(DC):
                    last = product(bank[3][:, f:f + 1],
                                   [(wfq[:, e, f * P:(f + 1) * P], col["betaq"][:, e:e + 1]) for e in range(DC)])
                last.then_inc(prep_mm, 1)
                pe.wait_ge(weights_ready, 1)

            def prepare_mlp():
                pe.wait_ge(in_w1, 16)
                pe.wait_ge(in_w2, 16)
                for f in range(FC):
                    last = product(bank[5][:, f:f + 1],
                                   [(w1[:, e, f * P:(f + 1) * P], col["ba"][:, e:e + 1]) for e in range(DC)])
                last.then_inc(prep_mm, 1)
                pe.wait_ge(weights_ready, 2)

            def body(i, a, b, m, g):
                def h1(j):
                    after(pe, g_ready, 4, m, j - 1)
                    for f in range(HC):
                        ff = j * HC + f
                        last = product(bank[5 + j % 2][:, f * P:(f + 1) * P],
                                       [(w1[:, k, ff * P:(ff + 1) * P], hT[:, k, :]) for k in range(DC)])
                    last.then_inc(h1_mm, 1)

                def h2(j):
                    after(pe, g_ready, 4, m, j + 1)
                    for f in range(HC):
                        last = pe.matmul(bank[7][:, :], gT[:, j % 2, f, :], w2[:, j * HC + f, :],
                                         start=(j == 0 and f == 0), stop=(j == 3 and f == HC - 1))
                    last.then_inc(h2_mm, 1)

                def context(k):
                    bt, cc = k // 2, k % 2
                    after(pe, a_tcopy, A_T, a, k + 1)
                    transposes(0, lambda kk: ctxs[:, bt, kk, cc * P:(cc + 1) * P], KC).then_inc(a_t, 1)

                def scores(bt):
                    after(pe, a_tcopy, A_T, a, 3 + 2 * bt)
                    if bt == 0:
                        after(pe, a_used, A_MM, a, 1)
                    product(bank[1][bt * NQ:(bt + 1) * NQ, :],
                            [(aT[:, k, bt * NQ:(bt + 1) * NQ], ctxT[:, k, :]) for k in range(CC)])\
                        .then_inc(scores0_done if bt == 0 else a_mm, 1)

                def row_product(bk, xT, w):
                    return product(bank[bk][:, :], [(xT[:, k, :], w[:, k, :]) for k in range(DC)])

                if isinstance(i, int) and i == 1:
                    prepare_attention()
                if isinstance(i, int) and i == 2:
                    prepare_mlp()
                if b is not None:
                    after(pe, xn_ready, 1, b, 1)
                    after(pe, b2_used, B2, b, 0)
                    transposes(2, lambda k: xn[:, k * P:(k + 1) * P], DC).then_inc(b_mm, 1)
                if m is not None:
                    after(pe, b2_used, B2, m, B2)
                    h1(0)
                if a is not None:
                    after(pe, lnx_ready, 1, a, 1)
                    after(pe, a_tcopy, A_T, a, 0)
                    transposes(0, lambda k: lnx[:, k * P:(k + 1) * P], DC).then_inc(a_t, 1)
                if g is not None:
                    after(pe, yt_ready, 1, g, 1)
                    transposes(7, lambda k: yt[:, k * P:(k + 1) * P], DC).then_inc(yT_mm, 1)
                if b is not None:
                    after(pe, b2_used, B2, b, 1)
                    after(pe, b3_used, B3, b, 0)
                    row_product(3, xnT, wq).then_inc(b_mm, 1)
                if g is not None:
                    after(pe, yT_ready, 1, g, 1)
                    product(bank[7][:, 0:E], [(yT[:, k, :], gw[:, k, :]) for k in range(DC)]).then_inc(gl_mm, 1)
                if a is not None:
                    after(pe, a_tcopy, A_T, a, 1)
                    after(pe, a_used, A_MM, a, 0)
                    for cc in range(CC):
                        product(bank[1][:, cc * P:(cc + 1) * P],
                                [(qk[:, k, cc * P:(cc + 1) * P], lnxT[:, k, :]) for k in range(DC)])
                    product(bank[1][:, 256:257], [(lnxT[:, k, :], q_bk[:, k:k + 1]) for k in range(DC)]).then_inc(a_mm, 1)
                if b is not None:
                    row_product(2, xnT, wk).then_inc(b_mm, 1)
                if a is not None:
                    after(pe, in_ctx, 32, a, 32)
                    context(0)
                if m is not None:
                    h1(1)
                if b is not None:
                    after(pe, b3_used, B3, b, 1)
                    row_product(3, xnT, wv).then_inc(b_mm, 1)
                if a is not None:
                    context(1)
                if m is not None:
                    after(pe, gl_used, 1, m, 0)
                    h2(0)
                if b is not None:
                    after(pe, z_ready["q"], 1, b, 1)
                    after(pe, b2_used, B2, b, 2)
                    transposes(2, lambda k: zq[:, k * P:(k + 1) * P], DC).then_inc(b_mm, 1)
                if a is not None:
                    scores(0)
                if b is not None:
                    after(pe, z_ready["k"], 1, b, 1)
                    after(pe, b3_used, B3, b, 2)
                    transposes(3, lambda k: zk[:, k * P:(k + 1) * P], DC).then_inc(b_mm, 1)
                if a is not None:
                    context(2)
                if m is not None:
                    h1(2)
                if b is not None:
                    after(pe, b2_used, B2, b, 3)
                    for f in range(DC):
                        last = product(bank[2][:, f * P:(f + 1) * P],
                                       [(wfq[:, k, f * P:(f + 1) * P], zqT[:, k, :]) for k in range(DC)])
                    last.then_inc(b_mm, 1)
                if a is not None:
                    context(3)
                if b is not None:
                    after(pe, b3_used, B3, b, 3)
                    row_product(3, zkT, wfk).then_inc(b_mm, 1)
                if a is not None:
                    scores(1)
                if b is not None:
                    after(pe, pm_ready, 1, b, 1)
                    after(pe, sv_ready, 1, b, 0)
                    for k in range(DC):
                        pe.matmul(bank[4][k * DH:(k + 1) * DH, 0:P], pm1[:, k, :], zkT[:, k, :], start=True, stop=True)
                        last = pe.matmul(bank[4][k * DH:(k + 1) * DH, P:P + 1], pm0[:, k, :], col["betak"][:, k:k + 1],
                                         start=True, stop=True)
                    last.then_inc(lg_mm, 1)
                if m is not None:
                    h2(1)
                if a is not None:
                    after(pe, a_used, A_MM, a, 2)
                    after(pe, a_tcopy, A_T, a, 5)
                    transposes(0, lambda k: probs[:, k * P:(k + 1) * P], KC).then_inc(a_t, 1)
                if m is not None:
                    h1(3)
                if b is not None:
                    after(pe, score_ready, 1, b, 1)
                    pe.matmul(bank[4][:, 256:256 + H], scd[:, :], c["head_of_row"], start=True, stop=True)
                    pe.matmul(bank[4][:, 288:288 + BPT * DC], c["row_to_feature"], s0bc[:, :], start=True, stop=True)\
                        .then_inc(ex_mm, 1)
                if a is not None:
                    after(pe, a_tcopy, A_T, a, 6)
                    for cc in range(CC):
                        for bt in range(BPT):
                            at = cc * P + bt * NQ
                            last = product(bank[1][:, at:at + NQ],
                                           [(ctxs[:, bt, k, cc * P:(cc + 1) * P], pT[:, k, bt * NQ:(bt + 1) * NQ])
                                            for k in range(KC)])
                    last.then_inc(a_mm, 1)
                if b is not None:
                    def keys_values(k):
                        bt, half = k // 2, k % 2
                        used, per = (b3_used, B3) if half else (b2_used, B2)
                        after(pe, used, per, b, 4 + k // 2)
                        for cc in range(2):
                            chunk = 2 * half + cc
                            last = pe.matmul(bank[2 + half][:, cc * KVW:(cc + 1) * KVW],
                                             pk[bt * NQ:(bt + 1) * NQ, chunk * P:(chunk + 1) * P],
                                             sv[bt * NQ:(bt + 1) * NQ, chunk, :], start=True, stop=True)
                        last.then_inc(b_mm, 1)
                    after(pe, pk_ready, 1, b, 1)
                    after(pe, sv_ready, 1, b, 1)
                    keys_values(0)
                    keys_values(1)
                if m is not None:
                    h2(2)
                if b is not None:
                    keys_values(2)
                    keys_values(3)
                if a is not None:
                    after(pe, a_used, A_MM, a, 3)
                    product(bank[1][:, :], [(oT[:, k, :], xwv[:, k, :]) for k in range(CC)]).then_inc(a_mm, 1)
                if b is not None:
                    after(pe, kv_ready, 1, b, 1)
                    for half in range(2):
                        for bt in range(BPT):
                            for cc in range(2):
                                chunk = 2 * half + cc
                                last = pe.matmul(bank[2 + half][bt * NQ:(bt + 1) * NQ, cc * KVW:(cc + 1) * KVW],
                                                 pqT[:, chunk, bt * NQ:(bt + 1) * NQ], kv[:, bt, chunk, :],
                                                 start=True, stop=True)
                        last.then_inc(b_mm, 1)
                if m is not None:
                    h2(3)
                if b is not None:
                    after(pe, za_ready, 1, b, 1)
                    transposes(2, lambda k: on[:, k * P:(k + 1) * P], DC).then_inc(b_mm, 1)
            rounds(pe, body)

            with pe.Fori(0, SINKHORN_ROUNDS) as r:
                after(pe, sink_done, 1, r, 1)
                pe.matmul(bank[0][:, 0:T * E], c["same_batch"], gates[:, :, :].rearrange("p t e -> p (t e)"),
                          start=True, stop=True).then_inc(cs_mm, 1)
            pe.wait_ge(sink_done, SINKHORN_ROUNDS + 1)
            pe.transpose(bank[1][:, 0:P], gates[:, :, :].rearrange("p t e -> p (t e)"), ident).then_inc(gates_mm, 1)
            for k in range(T // 4):
                pe.wait_ge(picks_ready, k + 1)
                if k >= 2:
                    pe.wait_ge(won_ready, k - 1)
                pe.matmul(bank[2 + k % 2][:, :], c["ones"], picks[:, k % 2, :], start=True, stop=True).then_inc(picks_mm, 1)
                if k >= 1:
                    pe.wait_ge(won_ready, k)
                    if k >= 3:
                        pe.wait_ge(wonT_ready, k - 2)
                    transposes(4 + (k - 1) % 2, lambda kk: won[:, 4 * (k - 1) + kk, :], 4).then_inc(wonT_mm, 1)
            k = T // 4 - 1
            pe.wait_ge(won_ready, k + 1)
            pe.wait_ge(wonT_ready, k - 1)
            transposes(4 + k % 2, lambda kk: won[:, 4 * k + kk, :], 4).then_inc(wonT_mm, 1)
            pe.wait_ge(wonT_ready, T // 4)
            for t in range(T):
                pe.wait_ge(y_again, t + 1)
                if t >= 2:
                    pe.wait_ge(gathered, t - 1)
                for k in range(DC):
                    last = pe.matmul(bank[4 + t % 2][:, k * P:(k + 1) * P], (zq, zk)[t % 2][:, k * P:(k + 1) * P],
                                     won[:, t, :], start=True, stop=True)
                last.then_inc(gather_mm, 1)
            pe.wait_ge(gathered, T)
            for u in range(2 * E):
                e, half = u // 2, u % 2
                pe.wait_ge(in_experts, 16 * E)
                if u >= 2:
                    pe.wait_ge(expert_copied, u - 1)
                product(bank[6 + u % 2][:, :], [(routed_x[:, k, e, half * P:(half + 1) * P], experts[:, e, k, :])
                                                for k in range(DC)]).then_inc(expert_mm, 1)
            for t in range(T):
                pe.wait_ge(in_returned[t % 4], 16 * (t // 4 + 1))
                if t >= 2:
                    pe.wait_ge(x3_ready, t - 1)
                pe.matmul(bank[2 + t % 2][:, :], wonT[:, t, :], returned[:, t % 4, :], start=True, stop=True)\
                    .then_inc(scatter_mm, 1)


_NAMES = {
    "x": "x", "ctx": "ctx_512", "x_wq": "L0_xattn_Wq", "x_wk": "L0_xattn_Wk", "x_wv": "L0_xattn_Wv",
    "c_x_bq": "L0_xattn_bq", "c_x_bk": "L0_xattn_bk", "r_x_bv": "L0_xattn_bv",
    "wq": "L0_attn_Wq", "wk": "L0_attn_Wk", "wv": "L0_attn_Wv", "wfq": "L0_attn_Wfq", "wfk": "L0_attn_Wfk",
    "r_bq": "L0_attn_bq", "r_bk": "L0_attn_bk", "r_bv": "L0_attn_bv", "c_gq": "L0_attn_gq", "c_betaq": "L0_attn_betaq",
    "c_gk": "L0_attn_gk", "c_betak": "L0_attn_betak", "r_gv": "L0_attn_gv", "r_betav": "L0_attn_betav",
    "c_bfq": "L0_attn_bfq", "bfk": "L0_attn_bfk", "ga": "L0_attn_ga", "c_ba": "L0_attn_ba",
    "w1": "L0_attn_W1", "b1": "L0_attn_b1", "w2": "L0_attn_W2", "r_b2": "L0_attn_b2",
    "gate_w": "L0_ffn_gate_w", "experts": "L0_ffn_experts",
}


def constants():
    import numpy as np
    p = np.arange(P)
    cc = np.zeros((P, CONST_WIDTH), np.float32)

    def put(name, value):
        a, b = CONST_COLS[name]
        cc[:, a:b] = value
    put("ident", np.eye(P))
    feature = p[:, None] // DH
    put("block_mask", np.concatenate([feature == p[None, :] // DH, feature == np.arange(HC)[None, :]], 1))
    chunk, rest = p // DH, p % DH
    bt, hd, real = rest // HC % BPT, rest % HC, rest < BPT * HC
    put("off_batch", np.where(bt[:, None] == p[None, :] // NQ, 0.0, -1e30))
    put("head_of_row", real[:, None] & ((chunk * HC + hd)[:, None] == np.arange(H)[None, :]))
    put("row_to_feature", real[:, None] & (hd[:, None] == p[None, :] // DH))
    put("row_is_bc", real[:, None] & ((bt * DC + chunk)[:, None] == np.arange(BPT * DC)[None, :]))
    put("same_batch", p[:, None] // NQ == p[None, :] // NQ)
    put("slot_code", (p % SLOTS * E + p // (BPT * SLOTS) + 1)[None, :])
    put("token_id", p[:, None])
    put("expert_of_row", p[:, None] % E == np.arange(E)[None, :])
    put("tile_of_row", p[:, None] // E == np.arange(T)[None, :])
    put("ones", 1.0)
    put("minus_half", -0.5)
    return cc


def kernel(**inputs):
    import numpy as np
    import concourse.bacc as bacc
    from concourse import mybir as _mybir
    from concourse.bass_utils import run_bass_kernel_spmd as run

    nc = bacc.Bacc("TRN2", target_bir_lowering=False, num_devices=1, dynamic_dma_scratch_size=1024)
    arrays, d = {}, {}
    for short, name in [*_NAMES.items(), ("consts", None)]:
        a = np.ascontiguousarray(inputs[name] if name else constants())
        arrays["in_" + short] = a
        d[short] = nc.dram_tensor("in_" + short, a.shape, _mybir.dt.from_np(a.dtype), kind="ExternalInput").ap()
    for n in ("bfk", "ga"):
        d["r_" + n] = d["c_" + n] = d[n]
    out = nc.dram_tensor("out", (B, NQ, D), _mybir.dt.float32, kind="ExternalOutput").ap()
    build(nc, d, out)
    return run(nc, [arrays], core_ids=[0]).results[0]["out"]
```

```python
import concourse.bass as bass
from concourse import mybir
from contextlib import ExitStack


B, NQ, D = 32, 64, 512
NK, KD = 512, 256
H, DH = 16, 32
MLP = 2048
E, SLOTS = 8, 8
P = 128
T = B * NQ // P
BPT = P // NQ
DC = D // P
CC = KD // P
KC = NK // P
FC = MLP // P
HC = P // DH
KVW = P + HC
LN_EPS = 1e-5
GATE_MIN = 1e-6
DEN_EPS = 1e-6
SINKHORN_ROUNDS = 8

Z_SCALE = 2.0 ** 11
W_TOP = 2.0 ** 14
G_TOP = 2.0 ** 15
Z_NORM = 22.75
EXPONENT_BITS = 0x7F800000
SCALES = ["qk", "wfq", "wfk", "wq", "wk", "wv", "w1", "w2", "b1", "g"]
MATS = {n: i for i, n in enumerate(SCALES)}
PROJ = ["wfq", "wfk", "wq", "wk", "wv"]
square_count = [0, 1, 5] + list(range(9, 21))

CONST_COLS = {}
_at = 0
for _name, _width in [("ident", P), ("block_mask", KVW), ("off_batch", P), ("head_of_row", H), ("row_to_feature", P),
                      ("row_is_bc", BPT * DC), ("same_batch", P), ("slot_code", P), ("token_id", 1),
                      ("expert_of_row", E), ("tile_of_row", T), ("ones", P), ("minus_half", 4)]:
    CONST_COLS[_name] = (_at, _at + _width)
    _at += _width
CONST_WIDTH = _at

ROWS = ["x_bv", "bq", "bk", "bv", "gv", "betav", "bfk", "ga", "b2"]
COLS = ["x_bq", "x_bk", "bfq", "betaq", "betak", "gq", "gk", "ga", "ba", "bfk"]


def build(nc, d, out):
    fp32 = mybir.dt.float32
    fp16 = mybir.dt.float16
    bf16 = mybir.dt.bfloat16
    i32 = mybir.dt.int32
    u32 = mybir.dt.uint32
    ALU = mybir.AluOpType
    ACT = mybir.ActivationFunctionType
    AX = mybir.AxisListType.X

    def after(eng, sem, per_tile, t, k):
        value = t * per_tile + k
        if isinstance(value, int) and value <= 0:
            return
        eng.wait_ge(sem, value)

    ctx = ExitStack()
    with ctx:
        def after_apart(eng, sem, per_tile, t, k):
            value = t * per_tile + k
            if isinstance(value, int):
                after(eng, sem, per_tile, t, k)
            else:
                eng.wait_ge(sem, value).then_inc(waits_passed, 1)

        def sb(name, shape, dt=fp32):
            return ctx.enter_context(nc.sbuf_tensor(name, shape, dt))

        def sem(name):
            return ctx.enter_context(nc.semaphore(name))

        cst = sb("cst", [P, CONST_WIDTH])
        c = {n: cst[:, a:b] for n, (a, b) in CONST_COLS.items()}
        rows = sb("rows", [P, len(ROWS), D])
        row = {n: rows[:, i, :] for i, n in enumerate(ROWS)}
        cols = sb("cols", [P, len(COLS), DC])
        col = {n: cols[:, i, :] for i, n in enumerate(COLS)}
        b1c = sb("b1c", [P, FC])
        res = sb("res", [P, T, D])
        w12 = sb("w12", [P, 2 * FC * D])
        w1_32 = w12[:, 0:FC * D].rearrange("p (c f) -> p c f", c=DC)
        w2_32 = w12[:, FC * D:2 * FC * D].rearrange("p (f d) -> p f d", f=FC)

        def as_pair(ap, **kw):
            return ap.bitcast(fp16).rearrange("p (l n) -> p l n", l=2)
        CHUNK = DC * D
        w1 = [as_pair(w12[:, k * CHUNK:(k + 1) * CHUNK]) for k in range(DC)]
        w2 = [as_pair(w12[:, FC * D + k * CHUNK:FC * D + (k + 1) * CHUNK]).rearrange("p l (f d) -> p l f d", f=FC // DC)
              for k in range(DC)]
        experts = w12[:, :].rearrange("p (e c d) -> p e c d", e=E, c=DC)
        scratch = w12[:, FC * D:2 * FC * D]
        xwq = scratch[:, 0:2048].rearrange("p (c e) -> p c e", c=DC)
        xwqT = scratch[:, 2048:4096].rearrange("p (c e) -> p c e", c=DC)
        xwk = scratch[:, 4096:5120].rearrange("p (c e) -> p c e", c=CC)
        xwkT = scratch[:, 5120:6144].rearrange("p (c e) -> p c e", c=DC)
        qk_32 = scratch[:, 7168:8192]
        betak_b = scratch[:, 6144:6656].rearrange("p (c e) -> p c e", c=DC)
        xbq_b = scratch[:, 6656:7168].rearrange("p (c e) -> p c e", c=DC)
        proj = sb("proj", [P, 5, DC, D])
        proj_32 = {n: proj[:, i] for i, n in enumerate(("wq", "wk", "wv", "wfq", "wfk"))}
        wq, wk, wv, wfq, wfk = (as_pair(proj[:, i].rearrange("p c e -> p (c e)")).rearrange("p l (c e) -> p l c e", c=DC)
                                for i in range(5))
        xwv = sb("xwv", [P, CC, D])
        qk = sb("qk", [P, 2, DC, KD], fp16)
        qk_bias = sb("qk_bias", [P, CC])
        q_bk = sb("q_bk", [P, 3, DC], bf16)
        q_bk_rest = sb("q_bk_rest", [P, DC])
        bq_bk = sb("bq_bk", [P, 1])
        tq = sb("tq", [P, DC])
        s0feat = sb("s0feat", [P, DC])
        zero_key = sb("zero_key", [P, DC, HC])
        gw = sb("gw", [P, DC, E])
        ctxs = sb("ctxs", [P, BPT, KC, KD])
        ctxT = sb("ctxT", [P, CC, NK])
        probs = sb("probs", [P, NK])
        lnx = probs[:, :].bitcast(fp16).rearrange("p (l d) -> p l d", l=2)
        lnxT = sb("lnxT", [P, 2, DC, P], fp16)
        aT = sb("aT", [P, CC, P])
        s0 = sb("s0", [P, 1])
        amax = sb("amax", [P, 2])
        abias = sb("abias", [P, 1])
        lsum = sb("lsum", [P, 1])
        rl = sb("rl", [P, 1])
        pT = sb("pT", [P, KC, P])
        oT = aT
        xn = sb("xn", [P, D])
        xnT = sb("xnT", [P, 2, DC, P], fp16)
        zq, zk = (sb(n, [P, D]) for n in ("zq", "zk"))
        zq2, zk2 = (sb(n, [P, 2, D], fp16) for n in ("zq2", "zk2"))
        xn2 = zk2
        za2 = zq2
        pqT = sb("pqT", [P, DC, P])
        zqT = pqT[:, :, :].rearrange("p c q -> p (c q)").bitcast(fp16).rearrange("p (l c q) -> p l c q", l=2, c=DC)
        zkT = sb("zkT", [P, 2, DC, P], fp16)
        pk = zk
        probe = sb("probe", [P, DC, BPT])
        pm0 = sb("pm0", [P, DC, DH])
        pm1 = sb("pm1", [P, DC, BPT * HC])
        pm1s = sb("pm1s", [P, 3, DC, DH], bf16)
        lm = sb("lm", [P, P])
        lneg = sb("lneg", [P, 2])
        lsm = sb("lsm", [P, 4])
        scd = lm
        s0bc = sb("s0bc", [P, BPT * DC])
        s0kv = sb("s0kv", [P, BPT * DC, HC])
        sv = sb("sv", [P, DC, KVW])
        zv = sv[:, :, 0:P]
        kv = sb("kv", [P, BPT, DC, KVW])
        den = sb("den", [P, DC, HC])
        on = zq
        ztmp = zk
        hT = sb("hT", [P, 2, DC, P], fp16)
        gf = sb("gf", [P, HC, P])
        gT = sb("gT", [P, 2, 2, HC, P], fp16)
        yt = sb("yt", [P, D])
        y2 = yt[:, :].bitcast(fp16).rearrange("p (l d) -> p l d", l=2)
        yT = pT[:, :, :].rearrange("p c q -> p (c q)").bitcast(fp16).rearrange("p (l c q) -> p l c q", l=2, c=DC)
        gw2 = sb("gw2", [P, 3, DC, E], bf16)
        ident16 = sb("ident16", [P, P], fp16)
        sums = sb("sums", [P, 21])
        total = sb("total", [P, len(SCALES)])
        root = sb("root", [P, len(SCALES)])
        scale = sb("scale", [P, len(SCALES)])
        unscale = sb("unscale", [P, len(SCALES)])
        gain_scale = {n: sb("gain_scale_" + n, [P, DC]) for n in ("wfq", "wfk", "w1")}
        squared = {0: kv[:, :, :, :].rearrange("p b c w -> p (b c w)").bitcast(bf16)[:, 0:CHUNK],
                   1: gT[:, :, :, :, :].rearrange("p a l f q -> p (a l f q)").bitcast(bf16)}
        staged = [res[:, 8 + 4 * k:12 + 4 * k, :].rearrange("p t d -> p (t d)") for k in range(2)]
        gates = sb("gates", [P, T, E])
        stat_y = sb("stat_y", [P, T, 2])
        routed_x = proj[:, :, :, :].rearrange("p a c e -> p (a c e)")[:, 0:DC * E * T * P // E]\
            .rearrange("p (c e s) -> p c e s", c=DC, e=E)
        won = ctxs[:, :, :, :].rearrange("p b k c -> p (b k c)").rearrange("p (t s) -> p t s", t=T)
        won16 = ctxT[:, :, :].rearrange("p a b -> p (a b)").bitcast(fp16).rearrange("p (t s) -> p t s", t=T)
        y_ring = (zq2, zk2)
        wonT = rows[:, 0:4, :].rearrange("p a c -> p (a c)").rearrange("p (t s) -> p t s", t=T)
        picks = rows[:, 4:6, :]
        expert_y = rows[:, 6:8, :]
        returned = proj[:, 4, :, :]
        kv_flat = kv[:, :, :, :].rearrange("p b c w -> p (b c w)")
        col_inv = kv_flat[:, 0:T * E]
        gates_t = kv_flat[:, T * E:2 * T * E]
        slots = kv_flat[:, 2 * T * E:3 * T * E].rearrange("p (e s) -> p e s", e=E)
        row_sum = sb("row_sum", [P, T])
        top_v = sb("top_v", [P, BPT, SLOTS])
        top_i = sb("top_i", [P, BPT, SLOTS], u32)
        top_f = sb("top_f", [P, BPT, SLOTS])
        best = sb("best", [P, 2, HC])
        gate_of = sb("gate_of", [P, T])
        NORMS = ["x", "x1", "q", "k", "v", "o", "y"]
        bn = {n: sb("bn_" + n, [P, 6]) for n in NORMS}
        mv = {n: sb("mv_" + n, [P, 2]) for n in NORMS}
        rstd = {n: sb("rstd_" + n, [P, 1]) for n in NORMS}
        var_eps = {n: sb("var_eps_" + n, [P, 1]) for n in NORMS}
        bank = [ctx.enter_context(nc.psum_tensor(f"bank{i}", [P, 512], fp32)) for i in range(8)]

        def bank16(k):
            return bank[k][:, :].bitcast(fp16).rearrange("p (l c q) -> p l c q", l=2, c=DC)

        def flat(ap):
            return ap.rearrange("p c e -> p (c e)")

        def split(ap, n):
            return ap.rearrange("p (a b) -> p a b", a=n)

        ctx_d = d["ctx"].rearrange("(t b) (k p) c -> t p b k c", b=BPT, p=P)
        x_d = d["x"].rearrange("(t b) q d -> (b q) t d", b=BPT)
        slot_rows = nc.dram_tensor("slot_rows", [T, E, BPT * SLOTS, D], fp32, kind="Internal").ap()
        out_d = out.rearrange("(t b) q d -> (b q) t d", b=BPT)

        in_x = sem("in_x")
        in_const = sem("in_const")
        in_cross = sem("in_cross")
        in_small = sem("in_small")
        in_proj = sem("in_proj")
        in_w1 = sem("in_w1")
        in_w2 = sem("in_w2")
        in_ctx = sem("in_ctx")
        prep_bc = sem("prep_bc")
        prep_t = sem("prep_t")
        prep_tcopy = sem("prep_tcopy")
        prep_mm = sem("prep_mm")
        prep_act = sem("prep_act")
        prep_chain = sem("prep_chain")
        qk_ready = sem("qk_ready")
        folded = sem("folded")
        squares = sem("squares")
        totals = sem("totals")
        scale_chain = sem("scale_chain")
        root_ready = sem("root_ready")
        scales_ready = sem("scales_ready")
        chunk_staged = sem("chunk_staged")
        chunk_split = sem("chunk_split")
        hi_split = sem("hi_split")
        consts16 = sem("consts16")
        stat_kept = sem("stat_kept")
        weights_ready = sem("weights_ready")
        mv_ready = {n: sem("mv_ready_" + n) for n in NORMS}
        rstd_ready = {n: sem("rstd_ready_" + n) for n in NORMS}
        waits_passed = sem("waits_passed")
        bn_done = {n: sem("bn_done_" + n) for n in NORMS}
        eps_done = {n: sem("eps_done_" + n) for n in NORMS}
        a_t = sem("a_t")
        a_tcopy = sem("a_tcopy")
        a_mm = sem("a_mm")
        a_used = sem("a_used")
        z_chain = {n: sem("z_chain_" + n) for n in NORMS}
        g_raw = sem("g_raw")
        g_hi = sem("g_hi")
        gs_chain = sem("gs_chain")
        qb_chain = sem("qb_chain")
        lnx_ready = sem("lnx_ready")
        s0_ready = sem("s0_ready")
        xbv_ready = sem("xbv_ready")
        scores0_done = sem("scores0_done")
        amax_done = sem("amax_done")
        abias_ready = sem("abias_ready")
        rl_ready = sem("rl_ready")
        x1_ready = sem("x1_ready")
        b_mm = sem("b_mm")
        b2_used = sem("b2_used")
        b3_used = sem("b3_used")
        xn_ready = sem("xn_ready")
        res_xn = sem("res_xn")
        y_raw = {n: sem("y_raw_" + n) for n in "qkv"}
        z_ready = {n: sem("z_ready_" + n) for n in "qkv"}
        v_scaled = sem("v_scaled")
        v_ready = sem("v_ready")
        tanh_q = sem("tanh_q")
        pqT_ready = sem("pqT_ready")
        tanh_k = sem("tanh_k")
        pk_ready = sem("pk_ready")
        probe_chain = sem("probe_chain")
        pm_ready = sem("pm_ready")
        lg_mm = sem("lg_mm")
        lm_chain = sem("lm_chain")
        lm_ready = sem("lm_ready")
        exp_ready = sem("exp_ready")
        sc_chain = sem("sc_chain")
        score_ready = sem("score_ready")
        ex_mm = sem("ex_mm")
        sv_ready = sem("sv_ready")
        kv_ready = sem("kv_ready")
        den_chain = sem("den_chain")
        o_raw = sem("o_raw")
        za_ready = sem("za_ready")
        gated_chain = sem("gated_chain")
        res_ready = sem("res_ready")
        h1_mm = sem("h1_mm")
        g_ready = sem("g_ready")
        h2_mm = sem("h2_mm")
        x2_ready = sem("x2_ready")
        yt_ready = sem("yt_ready")
        yT_mm = sem("yT_mm")
        yT_ready = sem("yT_ready")
        gl_mm = sem("gl_mm")
        gl_used = sem("gl_used")

        out_done = sem("out_done")
        cs_mm = sem("cs_mm")
        sink_chain = sem("sink_chain")
        sink_done = sem("sink_done")
        gates_mm = sem("gates_mm")
        top_chain = sem("top_chain")
        picks_ready = sem("picks_ready")
        picks_mm = sem("picks_mm")
        won_chain = sem("won_chain")
        won_ready = sem("won_ready")
        wonT_mm = sem("wonT_mm")
        wonT_ready = sem("wonT_ready")
        y_again = sem("y_again")
        y_chain = sem("y_chain")
        gather_mm = sem("gather_mm")
        gathered = sem("gathered")
        in_experts = sem("in_experts")
        expert_mm = sem("expert_mm")
        expert_copied = sem("expert_copied")
        expert_stored = [sem(f"expert_stored{k}") for k in range(2)]
        in_returned = [sem(f"in_returned{k}") for k in range(4)]
        scatter_mm = sem("scatter_mm")
        x3_ready = sem("x3_ready")

        A_T, A_MM, B_MM, B2, B3 = 6, 4, 15, 8, 7
        O_MM = 3
        SMALL = 16 * (len(ROWS) + len(COLS) + 3)

        block = ctx.enter_context(nc.Block())

        def rounds(eng, body):
            def some(t):
                return t if 0 <= t < T else None
            for i in range(4):
                body(i, *(some(i + 1 - k) for k in range(5)))
            with eng.Fori(4, T - 1) as i:
                body(i, i + 1, i, i - 1, i - 2, i - 3)
            for i in range(T - 1, T + 3):
                body(i, *(some(i + 1 - k) for k in range(5)))

        @block.sync
        def _(sp):
            sp.dma_start(cst[:, :], d["consts"]).then_inc(in_const, 16)
            sp.dma_start(xwq, d["x_wq"].rearrange("(c p) e -> p c e", p=P)).then_inc(in_cross, 16)
            sp.dma_start(xwk, d["x_wk"].rearrange("(c p) e -> p c e", p=P)).then_inc(in_cross, 16)
            sp.dma_start(res[:, 0:4, :], x_d[:, 0:4, :]).then_inc(in_x, 16)
            sp.dma_start(ctxs[:, 0], ctx_d[0, :, 0]).then_inc(in_ctx, 16)
            sp.dma_start(ctxs[:, 1], ctx_d[0, :, 1]).then_inc(in_ctx, 16)
            sp.dma_start(xwv[:, :, :], d["x_wv"].rearrange("(c p) e -> p c e", p=P)).then_inc(in_cross, 16)
            for n in ("wfq", "wfk", "wq", "wk", "wv"):
                sp.dma_start(proj_32[n], d[n].rearrange("(c p) e -> p c e", p=P)).then_inc(in_proj, 16)
            sp.dma_start(w1_32, d["w1"].rearrange("(c p) f -> p c f", p=P)).then_inc(in_w1, 16)
            sp.wait_ge(prep_mm, 2)
            sp.wait_ge(chunk_split, 1)
            sp.dma_start(w2_32, d["w2"].rearrange("(f p) e -> p f e", p=P)).then_inc(in_w2, 16)

            def reload(i, x, a, b, m, g):
                if a is not None and not (isinstance(a, int) and a == 0):
                    after(sp, a_mm, A_MM, a - 1, O_MM)
                    sp.dma_start(ctxs[:, 0], ctx_d[a, :, 0]).then_inc(in_ctx, 16)
                    sp.dma_start(ctxs[:, 1], ctx_d[a, :, 1]).then_inc(in_ctx, 16)
                if isinstance(i, int) and i == 2:
                    sp.wait_ge(chunk_split, 14)
                    sp.dma_start(res[:, 4:T, :], x_d[:, 4:T, :]).then_inc(in_x, 16)
            rounds(sp, reload)
            sp.wait_ge(h2_mm, 4 * T)
            for e in range(E):
                sp.dma_start(experts[:, e], d["experts"][e].rearrange("(c p) f -> p c f", p=P)).then_inc(in_experts, 16)
            for e in range(E):
                for half in range(2):
                    u = 2 * e + half
                    sp.wait_ge(expert_copied, u + 1)
                    sp.dma_start(slot_rows[half * T // 2:(half + 1) * T // 2, e, :, :], expert_y[:, u % 2, :])\
                        .then_inc(expert_stored[u % 2], 16)
            for k in range(2):
                sp.wait_ge(expert_stored[k], 16 * E)
            for t in range(T + 3):
                if t < T:
                    if t >= 4:
                        sp.wait_ge(scatter_mm, t - 3)
                    sp.dma_start(returned[:, t % 4, :], slot_rows[t].rearrange("e s f -> (e s) f"))\
                        .then_inc(in_returned[t % 4], 16)
                if t >= 3:
                    sp.wait_ge(x3_ready, t - 2)
                    sp.dma_start(out_d[:, t - 3, :], res[:, t - 3, :]).then_inc(out_done, 16)
            sp.wait_ge(out_done, 16 * T)

        @block.gpsimd
        def _(pool):
            pool.wait_ge(in_const, 16)
            pool.wait_ge(in_small, SMALL)
            pool.wait_ge(prep_bc, 1)

            def roots(n, a, b, exponent=0):
                pool.wait_ge(scale_chain, n)
                pool.tensor_tensor(root[:, a:b], total[:, a:b], c["minus_half"][:, 0:1].broadcast_to([P, b - a]), ALU.pow)\
                    .then_inc(root_ready, 1)

            roots(1, 0, 1)

            def rsqrt(n, t):
                after_apart(pool, mv_ready[n], 1, t, 1)
                pool.tensor_scalar(var_eps[n][:, :], mv[n][:, 1:2], LN_EPS, None, ALU.add).then_inc(eps_done[n], 1)
                after_apart(pool, eps_done[n], 1, t, 1)
                pool.tensor_tensor(rstd[n][:, :], var_eps[n][:, :], c["minus_half"][:, 0:1], ALU.pow)\
                    .then_inc(rstd_ready[n], 1)

            def body(i, x, a, b, m, g):
                if isinstance(i, int) and i == 0:
                    roots(2, 1, 6)
                if isinstance(i, int) and i == 1:
                    roots(3, 6, 9)
                if b is not None:
                    after_apart(pool, xn_ready, 1, b, 1)
                    pool.tensor_tensor(res[:, b, :], res[:, b, :], xn[:, :], ALU.add).then_inc(res_xn, 1)
                    rsqrt("q", b)
                if a is not None:
                    after_apart(pool, lnx_ready, 1, a, 1)
                    pool.tensor_tensor(res[:, a, :], res[:, a, :], row["x_bv"], ALU.add).then_inc(xbv_ready, 1)
                if b is not None:
                    rsqrt("k", b)
                    rsqrt("v", b)
                    after_apart(pool, z_ready["v"], 1, b, 1)
                    pool.tensor_tensor(zv, zv, split(row["gv"], DC), ALU.mult).then_inc(v_scaled, 1)
                    after_apart(pool, v_scaled, 1, b, 1)
                    pool.tensor_tensor(zv, zv, split(row["betav"], DC), ALU.add).then_inc(v_ready, 1)
                    after_apart(pool, tanh_k, 1, b, 1)
                    pool.tensor_scalar(pk[:, :], pk[:, :], 1.0, None, ALU.add).then_inc(pk_ready, 1)
                if x is not None:
                    rsqrt("x", x)
                if a is not None:
                    rsqrt("x1", a)
                if b is not None:
                    rsqrt("o", b)
                if m is not None:
                    rsqrt("y", m)
                if b is not None:
                    after_apart(pool, za_ready, 1, b, 1)
                    after_apart(pool, res_xn, 1, b, 1)
                    pool.tensor_tensor(on[:, :], on[:, :], row["ga"], ALU.mult).then_inc(gated_chain, 1)
                    pool.tensor_tensor(res[:, b, :], res[:, b, :], row["b2"], ALU.add).then_inc(gated_chain, 1)
                    after_apart(pool, gated_chain, 2, b, 2)
                    pool.tensor_tensor(res[:, b, :], res[:, b, :], on[:, :], ALU.add).then_inc(res_ready, 1)
            rsqrt("x", 0)
            rounds(pool, body)

        @block.scalar
        def _(act):
            for n in COLS:
                act.dma_start(col[n], d["c_" + n].rearrange("(c p) -> p c", p=P), allow_slow_non_contiguous=True).then_inc(in_small, 16)
            act.dma_start(b1c[:, :], d["b1"].rearrange("(c p) -> p c", p=P), allow_slow_non_contiguous=True).then_inc(in_small, 16)
            act.dma_start(gw[:, :, :], d["gate_w"].rearrange("(c p) e -> p c e", p=P)).then_inc(in_small, 16)
            for n in ROWS:
                act.dma_start(row[n], d["r_" + n].partition_broadcast(P)).then_inc(in_small, 16)
            act.dma_start(on[:, :], d["c_ba"].partition_broadcast(P)).then_inc(in_small, 16)
            act.wait_ge(in_small, SMALL)
            act.activation(s0feat[:, :], col["bfk"], ACT.Tanh).then_inc(prep_act, 1)

            def parts(chunk, gains):
                n = 1 if gains is None else gains.shape[1]
                return [(slice(f * (chunk.shape[1] // n), (f + 1) * (chunk.shape[1] // n)),
                         None if gains is None else gains[:, f:f + 1]) for f in range(n)]

            def square(k, chunk, gains=None):
                for f, (at, gain) in enumerate(parts(chunk, gains)):
                    after(act, squares, 1, 0, square_count[k] + f)
                    act.activation(squared[int(k >= 6)][:, 0:at.stop - at.start], chunk[:, at], ACT.Square,
                                   scale=1.0 if gain is None else gain,
                                   accum_out=sums[:, square_count[k] + f:square_count[k] + f + 1]).then_inc(squares, 1)

            def stage(k, chunk, n, gains=None):
                if k >= 2:
                    act.wait_ge(chunk_split, k - 1)
                for at, gain in parts(chunk, gains):
                    last = act.activation(staged[k % 2][:, at], chunk[:, at], ACT.Copy,
                                          scale=scale[:, MATS[n]:MATS[n] + 1] if gain is None else gain)
                last.then_inc(chunk_staged, 1)

            act.wait_ge(qk_ready, 1)
            square(0, qk_32)
            act.wait_ge(scales_ready, 1)
            stage(0, qk_32, "qk")

            def square_attention():
                act.wait_ge(in_proj, 80)
                for k, n in enumerate(PROJ):
                    square(1 + k, flat(proj_32[n]), {"wfq": col["gq"], "wfk": col["gk"]}.get(n))
                act.wait_ge(scales_ready, 2)

            def square_mlp():
                act.wait_ge(in_w1, 16)
                for k in range(2 * DC):
                    if k == DC:
                        act.wait_ge(in_w2, 16)
                    square(6 + k, w12[:, k * CHUNK:(k + 1) * CHUNK], col["ga"][:, k:k + 1] if k < DC else None)
                act.wait_ge(folded, 1)
                square(14, b1c[:, :])
                act.wait_ge(scales_ready, 3)

            def stage_attention(k):
                stage(1 + k, flat(proj_32[PROJ[k]]), PROJ[k], gain_scale.get(PROJ[k]))

            def stage_mlp(k):
                stage(6 + k, w12[:, k * CHUNK:(k + 1) * CHUNK], "w1" if k < DC else "w2",
                      gain_scale["w1"][:, k:k + 1] if k < DC else None)

            def body(i, x, a, b, m, g):
                def weights(k):
                    if isinstance(i, int) and i == 0 and k < 5:
                        stage_attention(k)
                    if isinstance(i, int) and i == 1:
                        stage_mlp(k)

                if isinstance(i, int) and i == 0:
                    square_attention()
                if isinstance(i, int) and i == 1:
                    square_mlp()

                def gelu(j):
                    after(act, h1_mm, 4, m, j + 1)
                    after(act, g_ready, 4, m, j)
                    for f in range(HC):
                        g_ins = act.activation(gf[:, f, :], bank[5 + j % 2][:, f * P:(f + 1) * P], ACT.Gelu,
                                               bias=b1c[:, j * HC + f:j * HC + f + 1],
                                               scale=unscale[:, MATS["w1"]:MATS["w1"] + 1])
                    g_ins.then_inc(g_raw, 1)
                    after(act, g_raw, 4, m, j + 1)
                    after(act, h2_mm, 4, m, j - 1)
                    act.activation(gT[:, j % 2, 0], gf[:, :, :], ACT.Copy, scale=scale[:, MATS["g"]:MATS["g"] + 1])\
                        .then_inc(g_hi, 1)
                if a is not None:
                    after(act, a_t, A_T, a, 1)
                    act.copy(lnxT[:, :, :, :], bank16(0)).then_inc(a_tcopy, 1)
                weights(0)
                if b is not None:
                    after(act, b_mm, B_MM, b, 1)
                    act.copy(xnT[:, :, :, :], bank16(2)).then_inc(b2_used, 1)
                weights(1)
                if m is not None:
                    gelu(0)
                if g is not None:
                    after(act, yT_mm, 1, g, 1)
                    act.copy(yT, bank16(7)).then_inc(yT_ready, 1)
                if m is not None:
                    gelu(1)
                weights(2)
                if a is not None:
                    after(act, a_t, A_T, a, 3)
                    act.copy(ctxT[:, 1, :], bank[0][:, :]).then_inc(a_tcopy, 1)
                weights(3)
                if b is not None:
                    after(act, b_mm, B_MM, b, 6)
                    act.copy(zkT[:, :, :, :], bank16(3)).then_inc(b3_used, 1)
                if m is not None:
                    gelu(2)
                weights(4)
                if b is not None:
                    after(act, b_mm, B_MM, b, 7)
                    after(act, pm_ready, 1, b, 1)
                    for f in range(DC):
                        t_ins = act.activation(pqT[:, f, :], bank[2][:, f * P:(f + 1) * P], ACT.Tanh,
                                               bias=tq[:, f:f + 1], scale=unscale[:, MATS["wfq"]:MATS["wfq"] + 1])
                    t_ins.then_inc(tanh_q, 1)
                if a is not None:
                    after(act, a_t, A_T, a, 5)
                    act.copy(ctxT[:, 1, :], bank[0][:, :]).then_inc(a_tcopy, 1)
                weights(5)
                if b is not None:
                    after(act, b3_used, B3, b, 4)
                    act.activation(pk[:, :], pk[:, :], ACT.Tanh).then_inc(tanh_k, 1)
                if a is not None:
                    after(act, abias_ready, 1, a, 1)
                    act.activation(probs[:, :], bank[1][:, :], ACT.Exp, bias=abias[:, 0:1],
                                   accum_out=lsum[:, 0:1]).then_inc(a_used, 1)
                weights(6)
                if b is not None:
                    after(act, lm_ready, 1, b, 1)
                    act.activation(scd[:, :], lm[:, :], ACT.Exp, bias=lneg[:, 1:2], accum_out=lsm[:, 0:1])
                    act.activation(lsm[:, 1:2], lneg[:, 1:2], ACT.Exp).then_inc(exp_ready, 1)
                if m is not None:
                    gelu(3)
                weights(7)
                if b is not None:
                    after(act, b_mm, B_MM, b, 15)
                    act.copy(hT[:, :, :, :], bank16(2)).then_inc(b2_used, 1)
            rounds(act, body)
            for k in range(T // 4):
                act.wait_ge(wonT_mm, k + 1)
                act.copy(wonT[:, 4 * k:4 * k + 4, :], split(bank[4 + k % 2][:, :], 4)).then_inc(wonT_ready, 1)
            for t in range(T):
                act.wait_ge(gather_mm, t + 1)
                act.activation(routed_x[:, :, :, t * BPT * SLOTS:(t + 1) * BPT * SLOTS],
                               bank[4 + t % 2][:, :].rearrange("p (c e s) -> p c e s", c=DC, e=E), ACT.Copy,
                               scale=1.0 / Z_SCALE).then_inc(gathered, 1)
            for u in range(2 * E):
                act.wait_ge(expert_mm, u + 1)
                if u >= 2:
                    act.wait_ge(expert_stored[u % 2], 16 * (u // 2))
                act.copy(expert_y[:, u % 2, :], bank[6 + u % 2][:, :]).then_inc(expert_copied, 1)

        @block.vector
        def _(dve):
            def bc(ap, n, shape):
                return ap.unsqueeze(n).broadcast_to(shape)

            def stats(n, t, ap):
                dve.bn_stats(bn[n][:, :], ap).then_inc(bn_done[n], 1)
                after_apart(dve, bn_done[n], 1, t, 1)
                dve.bn_aggr(mv[n][:, :], bn[n][:, :]).then_inc(mv_ready[n], 1)

            def norm_split(n, t, pair, z, in_, ready):
                norm(n, t, z, in_).then_inc(z_chain[n], 1)
                after(dve, z_chain[n], 2, t, 1)
                dve.tensor_scalar(pair[:, 0, :], z, Z_SCALE, None, ALU.mult).then_inc(z_chain[n], 1)
                after(dve, z_chain[n], 2, t, 2)
                dve.scalar_tensor_tensor(pair[:, 1, :], z, Z_SCALE, pair[:, 0, :], ALU.mult, ALU.subtract)\
                    .then_inc(ready, 1)

            def norm(n, t, out_, in_):
                after(dve, rstd_ready[n], 1, t, 1)
                return dve.tensor_scalar(out_, in_, mv[n][:, 0:1], rstd[n][:, 0:1], ALU.subtract, ALU.mult)

            dve.memset(pm0[:, :, :], 0.0)
            dve.memset(pm1s[:, :, :, :], 0.0)
            dve.wait_ge(in_const, 16)
            dve.tensor_copy(ident16[:, :], c["ident"]).then_inc(consts16, 1)
            dve.wait_ge(prep_t, 1)
            for k in range(DC):
                dve.tensor_copy(xwqT[:, k, :], bank[k][:, :])
            dve.tensor_copy(xwkT[:, 0:2, :], split(bank[4][:, :], 2))
            dve.tensor_copy(xwkT[:, 2:4, :], split(bank[5][:, :], 2)).then_inc(prep_tcopy, 1)
            dve.wait_ge(in_small, SMALL)
            for k in range(DC):
                dve.tensor_scalar(betak_b[:, k, :], c["ones"], col["betak"][:, k:k + 1], None, ALU.mult)
                dve.tensor_scalar(xbq_b[:, k, :], c["ones"], col["x_bq"][:, k:k + 1], None, ALU.mult)
            dve.tensor_tensor(row["b2"], row["b2"], on[:, :], ALU.add).then_inc(prep_bc, 1)
            dve.wait_ge(prep_mm, 1)
            dve.tensor_copy(qk_32[:, 0:512], bank[6][:, :])
            dve.tensor_copy(qk_32[:, 512:1024], bank[7][:, :])
            dve.tensor_copy(qk_bias[:, :], bank[0][:, 0:CC])
            dve.tensor_copy(q_bk_rest[:, :], bank[0][:, 8:8 + DC])
            dve.tensor_copy(bq_bk[:, :], bank[0][:, 16:17]).then_inc(qk_ready, 1)

            dve.wait_ge(qk_ready, 1)
            dve.tensor_copy(q_bk[:, 0, :], q_bk_rest[:, :]).then_inc(qb_chain, 1)
            dve.wait_ge(qb_chain, 1)
            dve.tensor_tensor(q_bk_rest[:, :], q_bk_rest[:, :], q_bk[:, 0, :], ALU.subtract).then_inc(qb_chain, 1)
            dve.wait_ge(qb_chain, 2)
            dve.tensor_copy(q_bk[:, 1, :], q_bk_rest[:, :]).then_inc(qb_chain, 1)
            dve.wait_ge(qb_chain, 3)
            dve.tensor_tensor(q_bk[:, 2, :], q_bk_rest[:, :], q_bk[:, 1, :], ALU.subtract)
            dve.tensor_copy(gw2[:, 0], gw[:, :, :]).then_inc(gs_chain, 1)
            dve.wait_ge(gs_chain, 1)
            dve.tensor_tensor(gw[:, :, :], gw[:, :, :], gw2[:, 0], ALU.subtract).then_inc(gs_chain, 1)
            dve.wait_ge(gs_chain, 2)
            dve.tensor_copy(gw2[:, 1], gw[:, :, :]).then_inc(gs_chain, 1)
            dve.wait_ge(gs_chain, 3)
            dve.tensor_tensor(gw2[:, 2], gw[:, :, :], gw2[:, 1], ALU.subtract).then_inc(gs_chain, 1)

            def scales(n, a, b, source):
                dve.wait_ge(totals, n)
                dve.tensor_scalar(total[:, a:b], source, 1e-30, None, ALU.add).then_inc(scale_chain, 1)
                dve.wait_ge(root_ready, n)
                dve.tensor_scalar(scale[:, a:b], root[:, a:b], W_TOP, None, ALU.mult).then_inc(gs_chain, 1)
                dve.wait_ge(gs_chain, 4 + 3 * n - 2)
                dve.tensor_scalar(scale[:, a:b].bitcast(i32), scale[:, a:b].bitcast(i32), EXPONENT_BITS, None,
                                  ALU.bitwise_and).then_inc(gs_chain, 1)
                dve.wait_ge(gs_chain, 4 + 3 * n - 1)
                dve.reciprocal(unscale[:, a:b], scale[:, a:b]).then_inc(gs_chain, 1)
                dve.wait_ge(gs_chain, 4 + 3 * n)
                return dve.tensor_scalar(unscale[:, a:b], unscale[:, a:b], 1.0 / Z_SCALE, None, ALU.mult)

            def halves(k, pair):
                n = pair.shape[2]
                dve.wait_ge(chunk_staged, k + 1)
                dve.tensor_copy(pair[:, 0, :], staged[k % 2][:, 0:n]).then_inc(hi_split, 1)
                dve.wait_ge(hi_split, k + 1)
                dve.tensor_tensor(pair[:, 1, :], staged[k % 2][:, 0:n], pair[:, 0, :], ALU.subtract)\
                    .then_inc(chunk_split, 1)

            scales(1, 0, 1, bank[0][:, 32:33]).then_inc(scales_ready, 1)
            halves(0, qk[:, :, :, :].rearrange("p l c e -> p l (c e)"))

            def gains(n, g_):
                return dve.tensor_scalar(gain_scale[n][:, :], col[g_], scale[:, MATS[n]:MATS[n] + 1], None, ALU.mult)

            def prepare_attention():
                dve.wait_ge(prep_mm, 2)
                dve.tensor_tensor(tq[:, :], bank[3][:, 0:DC], col["bfq"], ALU.add)
                dve.tensor_tensor(row["bfk"], bank[2][:, :], row["bfk"], ALU.add)
                dve.wait_ge(prep_act, 1)
                dve.tensor_scalar(s0feat[:, :], s0feat[:, :], 1.0, None, ALU.add).then_inc(prep_chain, 1)
                dve.wait_ge(prep_chain, 1)
                dve.tensor_tensor(zero_key[:, :, :], bc(s0feat[:, :], 2, [P, DC, HC]),
                                  bc(c["block_mask"][:, P:KVW], 1, [P, DC, HC]), ALU.mult)
                scales(2, 1, 6, bank[6][:, 32:37])
                gains("wfq", "gq")
                gains("wfk", "gk").then_inc(scales_ready, 1)
                dve.wait_ge(scales_ready, 2)
                dve.tensor_scalar(col["gq"], col["gq"], 1.0 / (NQ * DH ** 0.5 * Z_SCALE), None, ALU.mult)
                dve.tensor_scalar(col["betaq"], col["betaq"], 1.0 / DH ** 0.5, None, ALU.mult).then_inc(weights_ready, 1)
                dve.wait_ge(weights_ready, 1)

            def prepare_mlp():
                dve.wait_ge(prep_mm, 3)
                dve.tensor_tensor(b1c[:, :], bank[5][:, 0:FC], b1c[:, :], ALU.add).then_inc(folded, 1)
                scales(3, 6, 9, bank[6][:, 32:35])
                gains("w1", "ga").then_inc(gs_chain, 1)
                w1_, w2_, b1_, g_ = (MATS[n] for n in ("w1", "w2", "b1", "g"))
                dve.tensor_tensor(total[:, w1_:b1_ + 1], total[:, w1_:b1_ + 1], root[:, w1_:b1_ + 1], ALU.mult)\
                    .then_inc(gs_chain, 1)
                dve.wait_ge(gs_chain, 15)
                dve.scalar_tensor_tensor(total[:, g_:g_ + 1], total[:, w1_:w1_ + 1], Z_NORM, total[:, b1_:b1_ + 1],
                                         ALU.mult, ALU.add).then_inc(gs_chain, 1)
                dve.wait_ge(gs_chain, 16)
                dve.reciprocal(root[:, g_:g_ + 1], total[:, g_:g_ + 1]).then_inc(gs_chain, 1)
                dve.wait_ge(gs_chain, 17)
                dve.tensor_scalar(scale[:, g_:g_ + 1], root[:, g_:g_ + 1], G_TOP, None, ALU.mult).then_inc(gs_chain, 1)
                dve.wait_ge(gs_chain, 18)
                dve.tensor_scalar(scale[:, g_:g_ + 1].bitcast(i32), scale[:, g_:g_ + 1].bitcast(i32), EXPONENT_BITS, None,
                                  ALU.bitwise_and).then_inc(gs_chain, 1)
                dve.wait_ge(gs_chain, 19)
                dve.reciprocal(unscale[:, g_:g_ + 1], scale[:, g_:g_ + 1]).then_inc(gs_chain, 1)
                dve.wait_ge(gs_chain, 20)
                dve.tensor_scalar(unscale[:, w2_:w2_ + 1], unscale[:, w2_:w2_ + 1], unscale[:, g_:g_ + 1], Z_SCALE,
                                  ALU.mult, ALU.mult).then_inc(scales_ready, 1)

            def project(n, z, bk, k, used, per_tile, count, b):
                after(dve, b_mm, B_MM, b, k)
                dve.scalar_tensor_tensor(z, split(bank[bk][:, :], DC), unscale[:, MATS["w" + n]:MATS["w" + n] + 1],
                                         split(row["b" + n], DC), ALU.mult, ALU.add).then_inc(used, 1)
                after(dve, used, per_tile, b, count)
                stats(n, b, z)

            def body(i, x, a, b, m, g):
                def weights(k):
                    if isinstance(i, int) and i == 0 and k < 5:
                        halves(1 + k, (wfq, wfk, wq, wk, wv)[k].rearrange("p l c e -> p l (c e)"))
                    if isinstance(i, int) and i == 1:
                        halves(6 + k, as_pair(w12[:, k * CHUNK:(k + 1) * CHUNK]))

                def gelu_low(j):
                    after(dve, g_hi, 4, m, j + 1)
                    dve.scalar_tensor_tensor(gT[:, j % 2, 1], gf[:, :, :], scale[:, MATS["g"]:MATS["g"] + 1],
                                             gT[:, j % 2, 0], ALU.mult, ALU.subtract).then_inc(g_ready, 1)

                if isinstance(i, int) and i == 0:
                    prepare_attention()
                if isinstance(i, int) and i == 1:
                    prepare_mlp()
                if m is not None:
                    gelu_low(0)
                weights(0)
                if b is not None:
                    after(dve, res_ready, 1, b, 0)
                    project("q", split(zq[:, :], DC), 3, 2, b3_used, B3, 1, b)
                if g is not None:
                    after(dve, gl_mm, 1, g, 1)
                    dve.tensor_scalar(gates[:, g, :], bank[7][:, 0:E], 1.0 / Z_SCALE, GATE_MIN, ALU.mult, ALU.max).then_inc(gl_used, 1)
                if a is not None:
                    after(dve, a_mm, A_MM, a, 1)
                    for k in range(CC):
                        dve.tensor_scalar(aT[:, k, :], bank[1][:, k * P:(k + 1) * P], unscale[:, 0:1], qk_bias[:, k:k + 1],
                                          ALU.mult, ALU.add)
                    dve.scalar_tensor_tensor(s0[:, :], bank[1][:, 256:257], 1.0 / Z_SCALE, bq_bk[:, :], ALU.mult, ALU.add)\
                        .then_inc(a_used, 1)
                weights(1)
                if b is not None:
                    norm_split("q", b, zq2, zq[:, :], zq[:, :], z_ready["q"])
                    project("k", split(zk[:, :], DC), 2, 3, b2_used, B2, 2, b)
                if a is not None:
                    after(dve, a_t, A_T, a, 2)
                    dve.tensor_copy(ctxT[:, 0, :], bank[0][:, :]).then_inc(a_tcopy, 1)
                if m is not None:
                    gelu_low(1)
                weights(2)
                if b is not None:
                    norm_split("k", b, zk2, zk[:, :], zk[:, :], z_ready["k"])
                    project("v", zv, 3, 4, b3_used, B3, 2, b)
                    after(dve, b_mm, B_MM, b, 5)
                    dve.tensor_copy(zqT, bank16(2)).then_inc(b2_used, 1)
                    norm("v", b, zv, zv).then_inc(z_ready["v"], 1)
                    after(dve, b2_used, B2, b, 3)
                    dve.tensor_reduce(probe[:, :, :].rearrange("p c b -> p (c b)"),
                                      zqT.rearrange("p l c (b q) -> p (c b) l q", b=BPT), mybir.AxisListType.XY, ALU.add)\
                        .then_inc(probe_chain, 1)
                    after(dve, probe_chain, 9, b, 1)
                    dve.tensor_tensor(probe[:, :, :], probe[:, :, :], bc(col["gq"], 2, [P, DC, BPT]), ALU.mult)\
                        .then_inc(probe_chain, 1)
                    after(dve, probe_chain, 9, b, 2)
                    dve.tensor_tensor(probe[:, :, :], probe[:, :, :], bc(col["betaq"], 2, [P, DC, BPT]), ALU.add)\
                        .then_inc(probe_chain, 1)
                    after(dve, probe_chain, 9, b, 3)
                    dve.tensor_tensor(pm0[:, :, 0:BPT * HC].rearrange("p c (b h) -> p c b h", b=BPT),
                                      bc(probe[:, :, :], 3, [P, DC, BPT, HC]),
                                      c["block_mask"][:, P:KVW].unsqueeze(1).unsqueeze(1).broadcast_to([P, DC, BPT, HC]),
                                      ALU.mult).then_inc(probe_chain, 1)
                    after(dve, probe_chain, 9, b, 4)
                    dve.tensor_tensor(pm1[:, :, :], pm0[:, :, 0:BPT * HC],
                                      bc(col["gk"], 2, [P, DC, BPT * HC]), ALU.mult).then_inc(probe_chain, 1)
                    n_ = BPT * HC
                    after(dve, probe_chain, 9, b, 5)
                    dve.tensor_copy(pm1s[:, 0, :, 0:n_], pm1[:, :, :]).then_inc(probe_chain, 1)
                    after(dve, probe_chain, 9, b, 6)
                    dve.tensor_tensor(pm1[:, :, :], pm1[:, :, :], pm1s[:, 0, :, 0:n_], ALU.subtract).then_inc(probe_chain, 1)
                    after(dve, probe_chain, 9, b, 7)
                    dve.tensor_copy(pm1s[:, 1, :, 0:n_], pm1[:, :, :]).then_inc(probe_chain, 1)
                    after(dve, probe_chain, 9, b, 8)
                    dve.tensor_tensor(pm1[:, :, :], pm1[:, :, :], pm1s[:, 1, :, 0:n_], ALU.subtract).then_inc(probe_chain, 1)
                    after(dve, probe_chain, 9, b, 9)
                    dve.tensor_copy(pm1s[:, 2, :, 0:n_], pm1[:, :, :]).then_inc(pm_ready, 1)
                if a is not None:
                    after(dve, a_t, A_T, a, 4)
                    dve.tensor_copy(ctxT[:, 0, :], bank[0][:, :]).then_inc(a_tcopy, 1)
                weights(3)
                if m is not None:
                    gelu_low(2)
                weights(4)
                if b is not None:
                    after(dve, tanh_q, 1, b, 1)
                    dve.tensor_scalar(pqT[:, :, :], pqT[:, :, :], 1.0, None, ALU.add).then_inc(b2_used, 1)
                    after(dve, b_mm, B_MM, b, 8)
                    dve.scalar_tensor_tensor(pk[:, :], bank[3][:, :], unscale[:, MATS["wfk"]:MATS["wfk"] + 1], row["bfk"],
                                             ALU.mult, ALU.add).then_inc(b3_used, 1)
                if a is not None:
                    after(dve, a_mm, A_MM, a, 2)
                    dve.tensor_reduce(amax[:, 0:1], bank[1][:, :], AX, ALU.max).then_inc(amax_done, 1)
                    after(dve, amax_done, 2, a, 1)
                    dve.tensor_tensor(amax[:, 1:2], amax[:, 0:1], s0[:, :], ALU.add).then_inc(amax_done, 1)
                    after(dve, amax_done, 2, a, 2)
                    dve.tensor_tensor(abias[:, :], s0[:, :], amax[:, 1:2], ALU.subtract).then_inc(abias_ready, 1)
                weights(5)
                if b is not None:
                    after(dve, lg_mm, 1, b, 1)
                    dve.tensor_copy(lsm[:, 3:4], bank[4][:, P:P + 1]).then_inc(lm_chain, 1)
                    after(dve, lm_chain, 4, b, 1)
                    dve.tensor_scalar(lm[:, :], bank[4][:, 0:P], 1.0 / Z_SCALE, lsm[:, 3:4], ALU.mult, ALU.add)\
                        .then_inc(lm_chain, 1)
                    after(dve, lm_chain, 4, b, 2)
                    dve.tensor_tensor(lm[:, :], lm[:, :], c["off_batch"], ALU.add).then_inc(lm_chain, 1)
                    after(dve, lm_chain, 4, b, 3)
                    dve.tensor_reduce(lneg[:, 0:1], lm[:, :], AX, ALU.max).then_inc(lm_chain, 1)
                    after(dve, lm_chain, 4, b, 4)
                    dve.tensor_scalar(lneg[:, 1:2], lneg[:, 0:1], 0.0, -1.0, ALU.max, ALU.mult).then_inc(lm_ready, 1)
                if a is not None:
                    after(dve, a_t, A_T, a, 6)
                    dve.tensor_copy(pT[:, :, :], split(bank[0][:, :], KC)).then_inc(a_tcopy, 1)
                    dve.reciprocal(rl[:, :], lsum[:, :]).then_inc(rl_ready, 1)
                if b is not None:
                    after(dve, exp_ready, 1, b, 1)
                    dve.tensor_tensor(lsm[:, 2:3], lsm[:, 0:1], lsm[:, 1:2], ALU.add).then_inc(sc_chain, 1)
                    after(dve, sc_chain, 2, b, 1)
                    dve.reciprocal(lsm[:, 2:3], lsm[:, 2:3]).then_inc(sc_chain, 1)
                    after(dve, sc_chain, 2, b, 2)
                    dve.tensor_scalar(scd[:, :], scd[:, :], lsm[:, 2:3], None, ALU.mult)
                    dve.tensor_scalar(s0bc[:, :], c["row_is_bc"], lsm[:, 1:2], lsm[:, 2:3], ALU.mult, ALU.mult)\
                        .then_inc(score_ready, 1)
                    after(dve, ex_mm, 1, b, 1)
                    after(dve, v_ready, 1, b, 1)
                    score = bank[4][:, 256:256 + H].rearrange("p (c h) -> p c h", c=DC)
                    zvh = zv.rearrange("p c (h e) -> p c h e", h=HC)
                    dve.tensor_tensor(zvh, zvh,
                                      bc(score, 3, [P, DC, HC, DH]), ALU.mult)
                    dve.tensor_copy(sv[:, :, P:KVW], score)
                    dve.tensor_tensor(s0kv[:, :, :].rearrange("p (b c) h -> p b c h", b=BPT),
                                      bc(bank[4][:, 288:288 + BPT * DC].rearrange("p (b c) -> p b c", b=BPT), 3,
                                         [P, BPT, DC, HC]),
                                      zero_key[:, :, :].unsqueeze(1).broadcast_to([P, BPT, DC, HC]), ALU.mult)\
                        .then_inc(sv_ready, 1)
                if m is not None:
                    gelu_low(3)
                weights(6)
                if a is not None:
                    after(dve, a_mm, A_MM, a, 3)
                    dve.tensor_copy(oT[:, :, :], split(bank[1][:, 0:CC * P], CC)).then_inc(a_used, 1)
                weights(7)
                if b is not None:
                    for k in range(4):
                        bt, half = k // 2, k % 2
                        after(dve, b_mm, B_MM, b, 9 + k)
                        dve.tensor_tensor(kv[:, bt, 2 * half:2 * half + 2, :], split(bank[2 + half][:, 0:2 * KVW], 2),
                                          bc(c["block_mask"], 1, [P, 2, KVW]), ALU.mult)\
                            .then_inc(b3_used if half else b2_used, 1)
                    after(dve, b2_used, B2, b, 6)
                    after(dve, b3_used, B3, b, 6)
                    after(dve, sv_ready, 1, b, 1)
                    dve.tensor_tensor(kv[:, :, :, P:KVW], kv[:, :, :, P:KVW],
                                      s0kv[:, :, :].rearrange("p (b c) h -> p b c h", b=BPT), ALU.add).then_inc(kv_ready, 1)
                if x is not None:
                    if isinstance(i, int) and i == 3:
                        dve.wait_ge(in_x, 32)
                    stats("x", x, res[:, x, :])
                    norm_split("x", x, lnx, ztmp[:, :], res[:, x, :], lnx_ready)
                if a is not None:
                    after(dve, a_mm, A_MM, a, 4)
                    after(dve, xbv_ready, 1, a, 1)
                    after(dve, rl_ready, 1, a, 1)
                    dve.scalar_tensor_tensor(res[:, a, :], bank[1][:, :], rl[:, 0:1], res[:, a, :], ALU.mult, ALU.add)\
                        .then_inc(a_used, 1)
                    after_apart(dve, a_used, A_MM, a, 4)
                    stats("x1", a, res[:, a, :])
                if b is not None:
                    for half in range(2):
                        after(dve, b_mm, B_MM, b, 13 + half)
                        pv = split(bank[2 + half][:, 0:2 * KVW], 2)
                        dn = den[:, 2 * half:2 * half + 2, :]
                        dve.tensor_scalar(dn, pv[:, :, P:KVW], DEN_EPS, None, ALU.add).then_inc(den_chain, 1)
                        after(dve, den_chain, 4, b, 2 * half + 1)
                        dve.reciprocal(dn, dn).then_inc(den_chain, 1)
                        after(dve, den_chain, 4, b, 2 * half + 2)
                        dve.tensor_tensor(on[:, half * 256:(half + 1) * 256].rearrange("p (c h e) -> p c h e", c=2, h=HC),
                                          pv[:, :, 0:P].rearrange("p c (h e) -> p c h e", h=HC),
                                          bc(dn, 3, [P, 2, HC, DH]), ALU.mult).then_inc(b3_used if half else b2_used, 1)
                    after(dve, b2_used, B2, b, 7)
                    after(dve, b3_used, B3, b, 7)
                    stats("o", b, on[:, :])
                if a is not None:
                    norm_split("x1", a, xn2, xn[:, :], res[:, a, :], xn_ready)
                if b is not None:
                    norm_split("o", b, za2, on[:, :], on[:, :], za_ready)
                if m is not None:
                    after(dve, h2_mm, 4, m, 4)
                    after(dve, res_ready, 1, m, 1)
                    dve.scalar_tensor_tensor(res[:, m, :], bank[7][:, :], unscale[:, MATS["w2"]:MATS["w2"] + 1],
                                             res[:, m, :], ALU.mult, ALU.add).then_inc(x2_ready, 1)
                    after_apart(dve, x2_ready, 1, m, 1)
                    stats("y", m, res[:, m, :])
                    norm_split("y", m, y2, ztmp[:, :], res[:, m, :], yt_ready)
                    dve.tensor_copy(stat_y[:, m, 0:1], mv["y"][:, 0:1])
                    dve.tensor_copy(stat_y[:, m, 1:2], rstd["y"][:, 0:1]).then_inc(stat_kept, 1)
            dve.wait_ge(in_x, 16)
            stats("x", 0, res[:, 0, :])
            norm_split("x", 0, lnx, ztmp[:, :], res[:, 0, :], lnx_ready)
            rounds(dve, body)

            dve.wait_ge(gl_used, T)
            gates_flat = gates[:, :, :].rearrange("p t e -> p (t e)")
            dve.wait_ge(stat_kept, T).then_inc(sink_done, 1)
            with dve.Fori(0, SINKHORN_ROUNDS) as r:
                after(dve, cs_mm, 1, r, 1)
                dve.reciprocal(col_inv[:, :], bank[0][:, 0:T * E]).then_inc(sink_chain, 1)
                after(dve, sink_chain, 4, r, 1)
                dve.tensor_tensor(gates_flat, gates_flat, col_inv[:, :], ALU.mult).then_inc(sink_chain, 1)
                after(dve, sink_chain, 4, r, 2)
                dve.tensor_reduce(row_sum[:, :], gates[:, :, :], AX, ALU.add).then_inc(sink_chain, 1)
                after(dve, sink_chain, 4, r, 3)
                dve.reciprocal(row_sum[:, :], row_sum[:, :]).then_inc(sink_chain, 1)
                after(dve, sink_chain, 4, r, 4)
                dve.tensor_tensor(gates[:, :, :], gates[:, :, :], bc(row_sum[:, :], 2, [P, T, E]), ALU.mult)\
                    .then_inc(sink_done, 1)
            dve.wait_ge(gates_mm, 1)
            dve.tensor_copy(gates_t[:, :], bank[1][:, 0:P]).then_inc(top_chain, 1)
            dve.wait_ge(top_chain, 1)
            for b in range(BPT):
                dve.max(top_v[:, b, :], gates_t[:, b * NQ:(b + 1) * NQ]).then_inc(top_chain, 1)
            dve.wait_ge(top_chain, 1 + BPT)
            for b in range(BPT):
                dve.max_index(top_i[:, b, :], top_v[:, b, :], gates_t[:, b * NQ:(b + 1) * NQ]).then_inc(top_chain, 1)
            dve.wait_ge(top_chain, 1 + 2 * BPT)
            for b in range(BPT):
                last = dve.tensor_scalar(top_f[:, b, :], top_i[:, b, :], float(b * NQ), None, ALU.add)
            last.then_inc(top_chain, 1)
            dve.wait_ge(top_chain, 2 + 2 * BPT)
            dve.tensor_tensor(slots[:, :, :], bc(top_f[:, :, :].rearrange("p b s -> p (b s)"), 1, [P, E, BPT * SLOTS]),
                              bc(c["expert_of_row"], 2, [P, E, BPT * SLOTS]), ALU.mult).then_inc(top_chain, 1)
            dve.wait_ge(top_chain, 3 + 2 * BPT)
            for k in range(T // 4):
                if k >= 2:
                    dve.wait_ge(picks_mm, k - 1)
                pk4 = picks[:, k % 2, :].rearrange("p (t s) -> p t s", t=4)
                dve.tensor_tensor(pk4, bc(slots[:, :, :].rearrange("p e s -> p (e s)"), 1, [P, 4, P]),
                                  bc(c["tile_of_row"][:, 4 * k:4 * k + 4], 2, [P, 4, P]), ALU.mult).then_inc(picks_ready, 1)
                w4 = won[:, 4 * k:4 * k + 4, :]
                dve.wait_ge(picks_mm, k + 1)
                dve.scalar_tensor_tensor(w4, split(bank[2 + k % 2][:, :], 4), c["token_id"],
                                         bc(c["slot_code"], 1, [P, 4, P]), ALU.is_equal, ALU.mult).then_inc(won_chain, 1)
                dve.wait_ge(won_chain, 5 * k + 1)
                dve.tensor_reduce(best[:, 0, :], w4, AX, ALU.max).then_inc(won_chain, 1)
                dve.wait_ge(won_chain, 5 * k + 2)
                dve.tensor_scalar(best[:, 1, :], best[:, 0, :], 0.5, None, ALU.max).then_inc(won_chain, 1)
                dve.wait_ge(won_chain, 5 * k + 3)
                dve.tensor_tensor(w4, w4, bc(best[:, 1, :], 2, [P, 4, P]), ALU.is_equal).then_inc(won_chain, 1)
                dve.wait_ge(won_chain, 5 * k + 4)
                g4 = yt[:, :].rearrange("p (t e s) -> p t e s", t=4, e=E)
                dve.tensor_tensor(g4, w4.rearrange("p t (e s) -> p t e s", e=E),
                                  bc(gates[:, 4 * k:4 * k + 4, :], 3, [P, 4, E, BPT * SLOTS]), ALU.mult).then_inc(won_chain, 1)
                dve.wait_ge(won_chain, 5 * k + 5)
                dve.tensor_copy(won16[:, 4 * k:4 * k + 4, :], w4)
                dve.tensor_reduce(gate_of[:, 4 * k:4 * k + 4], yt[:, :].rearrange("p (t s) -> p t s", t=4), AX, ALU.add)\
                    .then_inc(won_ready, 1)
            dve.wait_ge(stat_kept, T)
            dve.wait_ge(won_ready, T // 4)
            for t in range(T):
                if t >= 2:
                    dve.wait_ge(gather_mm, t - 1)
                    dve.wait_ge(y_again, t - 1)
                pair, z = y_ring[t % 2], (zq, zk)[t % 2]
                dve.tensor_scalar(z[:, :], res[:, t, :], stat_y[:, t, 0:1], stat_y[:, t, 1:2],
                                  ALU.subtract, ALU.mult).then_inc(y_chain, 1)
                dve.wait_ge(y_chain, 2 * t + 1)
                dve.tensor_scalar(pair[:, 0, :], z[:, :], Z_SCALE, None, ALU.mult).then_inc(y_chain, 1)
                dve.wait_ge(y_chain, 2 * t + 2)
                dve.scalar_tensor_tensor(pair[:, 1, :], z[:, :], Z_SCALE, pair[:, 0, :], ALU.mult, ALU.subtract)\
                    .then_inc(y_again, 1)
            for t in range(T):
                dve.wait_ge(scatter_mm, t + 1)
                dve.scalar_tensor_tensor(res[:, t, :], bank[2 + t % 2][:, :], gate_of[:, t:t + 1], res[:, t, :],
                                         ALU.mult, ALU.add).then_inc(x3_ready, 1)

        @block.tensor
        def _(pe):
            ident = c["ident"]

            def transposes_pair(bk, pair):
                for part in range(2):
                    for k in range(DC):
                        ins = pe.transpose(bank16(bk)[:, part, k, :], pair[:, part, k * P:(k + 1) * P], ident16[:, :])
                return ins

            def product3(out_, lhsT, rhs, n=DC, first=True, last=True):
                for k in range(n):
                    for step, (a_, b_) in enumerate(((0, 0), (0, 1), (1, 0))):
                        ins = pe.matmul(out_, lhsT(a_, k), rhs(b_, k), start=(first and k == 0 and step == 0),
                                        stop=(last and k == n - 1 and step == 2))
                return ins

            def transposes(bk, in_, n):
                for k in range(n):
                    ins = pe.transpose(bank[bk][:, k * P:(k + 1) * P], in_(k), ident)
                return ins

            def product(out_, pairs):
                for k, (lhsT, rhs) in enumerate(pairs):
                    ins = pe.matmul(out_, lhsT, rhs, start=(k == 0), stop=(k == len(pairs) - 1))
                return ins

            pe.wait_ge(in_const, 16)
            pe.wait_ge(in_cross, 48)
            for e in range(DC):
                transposes(e, lambda k: xwq[:, k, e * P:(e + 1) * P], DC)
            for e in range(DC):
                for k in range(CC):
                    at = (e % 2) * KD + k * P
                    last = pe.transpose(bank[4 + e // 2][:, at:at + P], xwk[:, k, e * P:(e + 1) * P], ident)
            last.then_inc(prep_t, 1)
            pe.wait_ge(prep_tcopy, 1)
            for k in range(DC):
                product(bank[6 + k // 2][:, (k % 2) * KD:(k % 2 + 1) * KD],
                        [(xwqT[:, e, k * P:(k + 1) * P], xwkT[:, e, :]) for e in range(DC)])
            pe.wait_ge(prep_bc, 1)
            for k in range(CC):
                product(bank[0][:, k:k + 1], [(xwkT[:, e, k * P:(k + 1) * P], col["x_bq"][:, e:e + 1]) for e in range(DC)])
            for k in range(DC):
                product(bank[0][:, 8 + k:9 + k],
                        [(xwqT[:, e, k * P:(k + 1) * P], col["x_bk"][:, e:e + 1]) for e in range(DC)])
            product(bank[0][:, 16:17], [(xbq_b[:, e, :], col["x_bk"][:, e:e + 1]) for e in range(DC)]).then_inc(prep_mm, 1)
            pe.wait_ge(qk_ready, 1)
            pe.wait_ge(squares, 1)
            pe.matmul(bank[0][:, 32:33], c["ones"], sums[:, 0:1], start=True, stop=True).then_inc(totals, 1)
            pe.wait_ge(chunk_split, 1)
            pe.wait_ge(consts16, 1)
            pe.wait_ge(gs_chain, 4)

            def total_of(out_, a, b):
                a, b = square_count[a], (square_count + [square_count[-1] + 1])[b]
                return product(out_, [(c["ones"], sums[:, k:k + 1]) for k in range(a, b)])

            def prepare_attention():
                pe.wait_ge(in_proj, 80)
                product(bank[2][:, :], [(betak_b[:, e, :], proj_32["wfk"][:, e, :]) for e in range(DC)])
                for f in range(DC):
                    last = product(bank[3][:, f:f + 1],
                                   [(proj_32["wfq"][:, e, f * P:(f + 1) * P], col["betaq"][:, e:e + 1])
                                    for e in range(DC)])
                last.then_inc(prep_mm, 1)
                pe.wait_ge(squares, square_count[6])
                for k in range(2):
                    total_of(bank[6][:, 32 + k:33 + k], 1 + k, 2 + k)
                for k in range(2, 5):
                    last = total_of(bank[6][:, 32 + k:33 + k], 1 + k, 2 + k)
                last.then_inc(totals, 1)

            def prepare_mlp():
                pe.wait_ge(in_w1, 16)
                for f in range(FC):
                    last = product(bank[5][:, f:f + 1],
                                   [(w1_32[:, e, f * P:(f + 1) * P], col["ba"][:, e:e + 1]) for e in range(DC)])
                last.then_inc(prep_mm, 1)
                pe.wait_ge(squares, square_count[14] + 1)
                total_of(bank[6][:, 32:33], 6, 10)
                total_of(bank[6][:, 33:34], 10, 14)
                total_of(bank[6][:, 34:35], 14, 15).then_inc(totals, 1)

            def body(i, x, a, b, m, g):
                def h1(j):
                    after(pe, g_raw, 4, m, j - 1)
                    for f in range(HC):
                        ff = j * HC + f
                        last = product3(bank[5 + j % 2][:, f * P:(f + 1) * P],
                                        lambda l, k: w1[k][:, l, ff * P:(ff + 1) * P], lambda l, k: hT[:, l, k, :])
                    last.then_inc(h1_mm, 1)

                def h2(j):
                    after(pe, g_ready, 4, m, j + 1)
                    product3(bank[7][:, :], lambda l, f: gT[:, j % 2, l, f, :], lambda l, f: w2[j][:, l, f, :],
                             HC, j == 0, j == 3).then_inc(h2_mm, 1)

                def context(k):
                    bt, cc = k // 2, k % 2
                    after(pe, a_tcopy, A_T, a, k + 1)
                    transposes(0, lambda kk: ctxs[:, bt, kk, cc * P:(cc + 1) * P], KC).then_inc(a_t, 1)

                def scores(bt):
                    after(pe, a_tcopy, A_T, a, 3 + 2 * bt)
                    if bt == 0:
                        after(pe, a_used, A_MM, a, 1)
                    product(bank[1][bt * NQ:(bt + 1) * NQ, :],
                            [(aT[:, k, bt * NQ:(bt + 1) * NQ], ctxT[:, k, :]) for k in range(CC)])\
                        .then_inc(scores0_done if bt == 0 else a_mm, 1)

                def row_product(bk, xT, w):
                    return product3(bank[bk][:, :], lambda l, k: xT[:, l, k, :], lambda l, k: w[:, l, k, :])

                if isinstance(i, int) and i == 0:
                    prepare_attention()
                if isinstance(i, int) and i == 1:
                    prepare_mlp()
                if a is not None:
                    after(pe, lnx_ready, 1, a, 1)
                    after(pe, a_tcopy, A_T, a, 0)
                    transposes_pair(0, lnx).then_inc(a_t, 1)
                if b is not None:
                    after(pe, xn_ready, 1, b, 1)
                    after(pe, b2_used, B2, b, 0)
                    transposes_pair(2, xn2).then_inc(b_mm, 1)
                if m is not None:
                    if isinstance(i, int) and i == 2:
                        pe.wait_ge(chunk_split, 14)
                    after(pe, b2_used, B2, m, B2)
                    h1(0)
                if g is not None:
                    after(pe, yt_ready, 1, g, 1)
                    transposes_pair(7, y2).then_inc(yT_mm, 1)
                if b is not None:
                    if isinstance(i, int) and i == 1:
                        pe.wait_ge(chunk_split, 6)
                    after(pe, b2_used, B2, b, 1)
                    after(pe, b3_used, B3, b, 0)
                    row_product(3, xnT, wq).then_inc(b_mm, 1)
                if g is not None:
                    after(pe, yT_ready, 1, g, 1)
                    product(bank[7][:, 0:E], [(yT[:, l, k, :], gw2[:, w_, k, :]) for k in range(DC) for l in range(2)
                                              for w_ in range(3)]).then_inc(gl_mm, 1)
                if a is not None:
                    after(pe, a_tcopy, A_T, a, 1)
                    after(pe, a_used, A_MM, a, 0)
                    for cc in range(CC):
                        product3(bank[1][:, cc * P:(cc + 1) * P],
                                 lambda l, k: qk[:, l, k, cc * P:(cc + 1) * P], lambda l, k: lnxT[:, l, k, :])
                    product(bank[1][:, 256:257], [(lnxT[:, l, k, :], q_bk[:, w_, k:k + 1]) for k in range(DC)
                                                  for l in range(2) for w_ in range(3)]).then_inc(a_mm, 1)
                if b is not None:
                    row_product(2, xnT, wk).then_inc(b_mm, 1)
                if a is not None:
                    after(pe, in_ctx, 32, a, 32)
                    context(0)
                if m is not None:
                    h1(1)
                if b is not None:
                    after(pe, b3_used, B3, b, 1)
                    row_product(3, xnT, wv).then_inc(b_mm, 1)
                if a is not None:
                    context(1)
                if m is not None:
                    after(pe, gl_used, 1, m, 0)
                    h2(0)
                if b is not None:
                    after(pe, z_ready["q"], 1, b, 1)
                    after(pe, b2_used, B2, b, 2)
                    transposes_pair(2, zq2).then_inc(b_mm, 1)
                if a is not None:
                    scores(0)
                if b is not None:
                    after(pe, z_ready["k"], 1, b, 1)
                    after(pe, b3_used, B3, b, 2)
                    transposes_pair(3, zk2).then_inc(b_mm, 1)
                if a is not None:
                    context(2)
                if m is not None:
                    h1(2)
                if b is not None:
                    after(pe, b2_used, B2, b, 3)
                    for f in range(DC):
                        last = product3(bank[2][:, f * P:(f + 1) * P],
                                        lambda l, k: wfq[:, l, k, f * P:(f + 1) * P], lambda l, k: zqT[:, l, k, :])
                    last.then_inc(b_mm, 1)
                if a is not None:
                    context(3)
                if b is not None:
                    after(pe, b3_used, B3, b, 3)
                    row_product(3, zkT, wfk).then_inc(b_mm, 1)
                if a is not None:
                    scores(1)
                if b is not None:
                    after(pe, pm_ready, 1, b, 1)
                    after(pe, sv_ready, 1, b, 0)
                    for k in range(DC):
                        product(bank[4][k * DH:(k + 1) * DH, 0:P], [(pm1s[:, w_, k, :], zkT[:, l, k, :])
                                                                    for w_ in range(3) for l in range(2)])
                        last = pe.matmul(bank[4][k * DH:(k + 1) * DH, P:P + 1], pm0[:, k, :], col["betak"][:, k:k + 1],
                                         start=True, stop=True)
                    last.then_inc(lg_mm, 1)
                if m is not None:
                    h2(1)
                if a is not None:
                    after(pe, a_used, A_MM, a, 2)
                    after(pe, a_tcopy, A_T, a, 5)
                    transposes(0, lambda k: probs[:, k * P:(k + 1) * P], KC).then_inc(a_t, 1)
                if m is not None:
                    h1(3)
                if b is not None:
                    after(pe, score_ready, 1, b, 1)
                    pe.matmul(bank[4][:, 256:256 + H], scd[:, :], c["head_of_row"], start=True, stop=True)
                    pe.matmul(bank[4][:, 288:288 + BPT * DC], c["row_to_feature"], s0bc[:, :], start=True, stop=True)\
                        .then_inc(ex_mm, 1)
                if a is not None:
                    after(pe, a_tcopy, A_T, a, 6)
                    for cc in range(CC):
                        for bt in range(BPT):
                            at = cc * P + bt * NQ
                            last = product(bank[1][:, at:at + NQ],
                                           [(ctxs[:, bt, k, cc * P:(cc + 1) * P], pT[:, k, bt * NQ:(bt + 1) * NQ])
                                            for k in range(KC)])
                    last.then_inc(a_mm, 1)
                if b is not None:
                    def keys_values(k):
                        bt, half = k // 2, k % 2
                        used, per = (b3_used, B3) if half else (b2_used, B2)
                        after(pe, used, per, b, 4 + k // 2)
                        for cc in range(2):
                            chunk = 2 * half + cc
                            last = pe.matmul(bank[2 + half][:, cc * KVW:(cc + 1) * KVW],
                                             pk[bt * NQ:(bt + 1) * NQ, chunk * P:(chunk + 1) * P],
                                             sv[bt * NQ:(bt + 1) * NQ, chunk, :], start=True, stop=True)
                        last.then_inc(b_mm, 1)
                    after(pe, pk_ready, 1, b, 1)
                    after(pe, sv_ready, 1, b, 1)
                    keys_values(0)
                    keys_values(1)
                if a is not None:
                    after(pe, a_used, A_MM, a, 3)
                    product(bank[1][:, :], [(oT[:, k, :], xwv[:, k, :]) for k in range(CC)]).then_inc(a_mm, 1)
                if b is not None:
                    keys_values(2)
                    keys_values(3)
                if b is not None:
                    after(pe, kv_ready, 1, b, 1)
                    for half in range(2):
                        for bt in range(BPT):
                            for cc in range(2):
                                chunk = 2 * half + cc
                                last = pe.matmul(bank[2 + half][bt * NQ:(bt + 1) * NQ, cc * KVW:(cc + 1) * KVW],
                                                 pqT[:, chunk, bt * NQ:(bt + 1) * NQ], kv[:, bt, chunk, :],
                                                 start=True, stop=True)
                        last.then_inc(b_mm, 1)
                if m is not None:
                    h2(2)
                if m is not None:
                    h2(3)
                if b is not None:
                    after(pe, za_ready, 1, b, 1)
                    transposes_pair(2, za2).then_inc(b_mm, 1)
            rounds(pe, body)

            with pe.Fori(0, SINKHORN_ROUNDS) as r:
                after(pe, sink_done, 1, r, 1)
                pe.matmul(bank[0][:, 0:T * E], c["same_batch"], gates[:, :, :].rearrange("p t e -> p (t e)"),
                          start=True, stop=True).then_inc(cs_mm, 1)
            pe.wait_ge(sink_done, SINKHORN_ROUNDS + 1)
            pe.transpose(bank[1][:, 0:P], gates[:, :, :].rearrange("p t e -> p (t e)"), ident).then_inc(gates_mm, 1)
            for k in range(T // 4):
                pe.wait_ge(picks_ready, k + 1)
                if k >= 2:
                    pe.wait_ge(won_ready, k - 1)
                pe.matmul(bank[2 + k % 2][:, :], c["ones"], picks[:, k % 2, :], start=True, stop=True).then_inc(picks_mm, 1)
                if k >= 1:
                    pe.wait_ge(won_ready, k)
                    if k >= 3:
                        pe.wait_ge(wonT_ready, k - 2)
                    transposes(4 + (k - 1) % 2, lambda kk: won[:, 4 * (k - 1) + kk, :], 4).then_inc(wonT_mm, 1)
            k = T // 4 - 1
            pe.wait_ge(won_ready, k + 1)
            pe.wait_ge(wonT_ready, k - 1)
            transposes(4 + k % 2, lambda kk: won[:, 4 * k + kk, :], 4).then_inc(wonT_mm, 1)
            pe.wait_ge(wonT_ready, T // 4)
            for t in range(T):
                pe.wait_ge(y_again, t + 1)
                if t >= 2:
                    pe.wait_ge(gathered, t - 1)
                for k in range(DC):
                    last = product(bank[4 + t % 2][:, k * P:(k + 1) * P],
                                   [(y_ring[t % 2][:, l, k * P:(k + 1) * P], won16[:, t, :]) for l in range(2)])
                last.then_inc(gather_mm, 1)
            pe.wait_ge(gathered, T)
            for u in range(2 * E):
                e, half = u // 2, u % 2
                pe.wait_ge(in_experts, 16 * E)
                if u >= 2:
                    pe.wait_ge(expert_copied, u - 1)
                product(bank[6 + u % 2][:, :], [(routed_x[:, k, e, half * P:(half + 1) * P], experts[:, e, k, :])
                                                for k in range(DC)]).then_inc(expert_mm, 1)
            for t in range(T):
                pe.wait_ge(in_returned[t % 4], 16 * (t // 4 + 1))
                if t >= 2:
                    pe.wait_ge(x3_ready, t - 1)
                pe.matmul(bank[2 + t % 2][:, :], wonT[:, t, :], returned[:, t % 4, :], start=True, stop=True)\
                    .then_inc(scatter_mm, 1)


_NAMES = {
    "x": "x", "ctx": "ctx_512", "x_wq": "L0_xattn_Wq", "x_wk": "L0_xattn_Wk", "x_wv": "L0_xattn_Wv",
    "c_x_bq": "L0_xattn_bq", "c_x_bk": "L0_xattn_bk", "r_x_bv": "L0_xattn_bv",
    "wq": "L0_attn_Wq", "wk": "L0_attn_Wk", "wv": "L0_attn_Wv", "wfq": "L0_attn_Wfq", "wfk": "L0_attn_Wfk",
    "r_bq": "L0_attn_bq", "r_bk": "L0_attn_bk", "r_bv": "L0_attn_bv", "c_gq": "L0_attn_gq", "c_betaq": "L0_attn_betaq",
    "c_gk": "L0_attn_gk", "c_betak": "L0_attn_betak", "r_gv": "L0_attn_gv", "r_betav": "L0_attn_betav",
    "c_bfq": "L0_attn_bfq", "bfk": "L0_attn_bfk", "ga": "L0_attn_ga", "c_ba": "L0_attn_ba",
    "w1": "L0_attn_W1", "b1": "L0_attn_b1", "w2": "L0_attn_W2", "r_b2": "L0_attn_b2",
    "gate_w": "L0_ffn_gate_w", "experts": "L0_ffn_experts",
}


def constants():
    import numpy as np
    p = np.arange(P)
    cc = np.zeros((P, CONST_WIDTH), np.float32)

    def put(name, value):
        a, b = CONST_COLS[name]
        cc[:, a:b] = value
    put("ident", np.eye(P))
    feature = p[:, None] // DH
    put("block_mask", np.concatenate([feature == p[None, :] // DH, feature == np.arange(HC)[None, :]], 1))
    chunk, rest = p // DH, p % DH
    bt, hd, real = rest // HC % BPT, rest % HC, rest < BPT * HC
    put("off_batch", np.where(bt[:, None] == p[None, :] // NQ, 0.0, -1e30))
    put("head_of_row", real[:, None] & ((chunk * HC + hd)[:, None] == np.arange(H)[None, :]))
    put("row_to_feature", real[:, None] & (hd[:, None] == p[None, :] // DH))
    put("row_is_bc", real[:, None] & ((bt * DC + chunk)[:, None] == np.arange(BPT * DC)[None, :]))
    put("same_batch", p[:, None] // NQ == p[None, :] // NQ)
    put("slot_code", (p % SLOTS * E + p // (BPT * SLOTS) + 1)[None, :])
    put("token_id", p[:, None])
    put("expert_of_row", p[:, None] % E == np.arange(E)[None, :])
    put("tile_of_row", p[:, None] // E == np.arange(T)[None, :])
    put("ones", 1.0)
    put("minus_half", -0.5)
    return cc


def kernel(**inputs):
    import numpy as np
    import concourse.bacc as bacc
    from concourse import mybir as _mybir
    from concourse.bass_utils import run_bass_kernel_spmd as run

    nc = bacc.Bacc("TRN2", target_bir_lowering=False, num_devices=1, dynamic_dma_scratch_size=1024)
    arrays, d = {}, {}
    for short, name in [*_NAMES.items(), ("consts", None)]:
        a = np.ascontiguousarray(inputs[name] if name else constants())
        arrays["in_" + short] = a
        d[short] = nc.dram_tensor("in_" + short, a.shape, _mybir.dt.from_np(a.dtype), kind="ExternalInput").ap()
    for n in ("bfk", "ga"):
        d["r_" + n] = d["c_" + n] = d[n]
    out = nc.dram_tensor("out", (B, NQ, D), _mybir.dt.float32, kind="ExternalOutput").ap()
    build(nc, d, out)
    return run(nc, [arrays], core_ids=[0]).results[0]["out"]
```

```python
import concourse.bass as bass
from concourse import mybir
from contextlib import ExitStack


B, NQ, D = 32, 64, 512
NK, KD = 512, 256
H, DH = 16, 32
MLP = 2048
E, SLOTS = 8, 8
P = 128
T = B * NQ // P
BPT = P // NQ
DC = D // P
CC = KD // P
KC = NK // P
FC = MLP // P
HC = P // DH
KVW = P + HC
LN_EPS = 1e-5
GATE_MIN = 1e-6
DEN_EPS = 1e-6
SINKHORN_ROUNDS = 8

Z_SCALE = 2.0 ** 11
W_TOP = 2.0 ** 14
G_TOP = 2.0 ** 15
Z_NORM = 22.75
EXPONENT_BITS = 0x7F800000
SCALES = ["qk", "wfq", "wfk", "wq", "wk", "wv", "w1", "w2", "b1", "g"]
MATS = {n: i for i, n in enumerate(SCALES)}
PROJ = ["wfq", "wfk", "wq", "wk", "wv"]
MLP_CHUNKS = [4, 5, 6, 7, 0, 1, 2, 3]
square_count = [0, 1, 5] + list(range(9, 21))

CONST_COLS = {}
_at = 0
for _name, _width in [("ident", P), ("block_mask", KVW), ("off_batch", P), ("head_of_row", H), ("row_to_feature", P),
                      ("row_is_bc", BPT * DC), ("same_batch", P), ("slot_code", P), ("token_id", 1),
                      ("expert_of_row", E), ("tile_of_row", T), ("ones", P), ("minus_half", 4)]:
    CONST_COLS[_name] = (_at, _at + _width)
    _at += _width
CONST_WIDTH = _at

ROWS = ["x_bv", "bq", "bk", "bv", "gv", "betav", "bfk", "ga", "b2"]
COLS = ["x_bq", "x_bk", "bfq", "betaq", "betak", "gq", "gk", "ga", "ba", "bfk"]


def build(nc, d, out):
    fp32 = mybir.dt.float32
    fp16 = mybir.dt.float16
    bf16 = mybir.dt.bfloat16
    i32 = mybir.dt.int32
    u32 = mybir.dt.uint32
    ALU = mybir.AluOpType
    ACT = mybir.ActivationFunctionType
    AX = mybir.AxisListType.X

    def after(eng, sem, per_tile, t, k):
        value = t * per_tile + k
        if isinstance(value, int) and value <= 0:
            return
        eng.wait_ge(sem, value)

    ctx = ExitStack()
    with ctx:
        def after_apart(eng, sem, per_tile, t, k):
            value = t * per_tile + k
            if isinstance(value, int):
                after(eng, sem, per_tile, t, k)
            else:
                eng.wait_ge(sem, value).then_inc(waits_passed, 1)

        def sb(name, shape, dt=fp32):
            return ctx.enter_context(nc.sbuf_tensor(name, shape, dt))

        def sem(name):
            return ctx.enter_context(nc.semaphore(name))

        cst = sb("cst", [P, CONST_WIDTH])
        c = {n: cst[:, a:b] for n, (a, b) in CONST_COLS.items()}
        rows = sb("rows", [P, len(ROWS), D])
        row = {n: rows[:, i, :] for i, n in enumerate(ROWS)}
        cols = sb("cols", [P, len(COLS), DC])
        col = {n: cols[:, i, :] for i, n in enumerate(COLS)}
        b1c = sb("b1c", [P, FC])
        res = sb("res", [P, T, D])
        w12 = sb("w12", [P, 2 * FC * D])
        w1_32 = w12[:, 0:FC * D].rearrange("p (c f) -> p c f", c=DC)
        w2_32 = w12[:, FC * D:2 * FC * D].rearrange("p (f d) -> p f d", f=FC)

        def as_pair(ap, **kw):
            return ap.bitcast(fp16).rearrange("p (l n) -> p l n", l=2)
        CHUNK = DC * D
        w1 = [as_pair(w12[:, k * CHUNK:(k + 1) * CHUNK]) for k in range(DC)]
        w2 = [as_pair(w12[:, FC * D + k * CHUNK:FC * D + (k + 1) * CHUNK]).rearrange("p l (f d) -> p l f d", f=FC // DC)
              for k in range(DC)]
        experts = w12[:, :].rearrange("p (e c d) -> p e c d", e=E, c=DC)
        scratch = w12[:, FC * D:2 * FC * D]
        xwq = scratch[:, 0:2048].rearrange("p (c e) -> p c e", c=DC)
        xwqT = scratch[:, 2048:4096].rearrange("p (c e) -> p c e", c=DC)
        xwk = scratch[:, 4096:5120].rearrange("p (c e) -> p c e", c=CC)
        xwkT = scratch[:, 5120:6144].rearrange("p (c e) -> p c e", c=DC)
        qk_32 = scratch[:, 7168:8192]
        xbq_b = scratch[:, 6656:7168].rearrange("p (c e) -> p c e", c=DC)
        proj = sb("proj", [P, 5, DC, D])
        proj_32 = {n: proj[:, i] for i, n in enumerate(("wq", "wk", "wv", "wfq", "wfk"))}
        wq, wk, wv, wfq, wfk = (as_pair(proj[:, i].rearrange("p c e -> p (c e)")).rearrange("p l (c e) -> p l c e", c=DC)
                                for i in range(5))
        xwv = sb("xwv", [P, CC, D])
        qk = sb("qk", [P, 2, DC, KD], fp16)
        qk_bias = sb("qk_bias", [P, CC])
        q_bk = sb("q_bk", [P, 3, DC], bf16)
        q_bk_rest = sb("q_bk_rest", [P, DC])
        bq_bk = sb("bq_bk", [P, 1])
        tq = sb("tq", [P, DC])
        s0feat = sb("s0feat", [P, DC])
        zero_key = sb("zero_key", [P, DC, HC])
        gw = sb("gw", [P, DC, E])
        ctxs = sb("ctxs", [P, BPT, KC, KD])
        ctxT = sb("ctxT", [P, CC, NK])
        probs = sb("probs", [P, NK])
        lnx = probs[:, :].bitcast(fp16).rearrange("p (l d) -> p l d", l=2)
        lnxT = sb("lnxT", [P, 2, DC, P], fp16)
        aT = sb("aT", [P, CC, P])
        s0 = sb("s0", [P, 1])
        amax = sb("amax", [P, 2])
        abias = sb("abias", [P, 1])
        lsum = sb("lsum", [P, 1])
        rl = sb("rl", [P, 1])
        pT = sb("pT", [P, KC, P])
        oT = aT
        xn = sb("xn", [P, D])
        xnT = sb("xnT", [P, 2, DC, P], fp16)
        zq, zk = (sb(n, [P, D]) for n in ("zq", "zk"))
        zq2, zk2 = (sb(n, [P, 2, D], fp16) for n in ("zq2", "zk2"))
        xn2 = zk2
        za2 = zq2
        pqT = sb("pqT", [P, DC, P])
        zqT = pqT[:, :, :].rearrange("p c q -> p (c q)").bitcast(fp16).rearrange("p (l c q) -> p l c q", l=2, c=DC)
        zkT = sb("zkT", [P, 2, DC, P], fp16)
        pk = zk
        probe = sb("probe", [P, DC, BPT])
        pm0 = sb("pm0", [P, DC, DH])
        pm1 = sb("pm1", [P, DC, BPT * HC])
        pm1s = sb("pm1s", [P, 3, DC, DH], bf16)
        lm = sb("lm", [P, P])
        lneg = sb("lneg", [P, 2])
        lsm = sb("lsm", [P, 4])
        scd = lm
        s0bc = sb("s0bc", [P, BPT * DC])
        s0kv = sb("s0kv", [P, BPT * DC, HC])
        sv = sb("sv", [P, DC, KVW])
        zv = sv[:, :, 0:P]
        kv = sb("kv", [P, BPT, DC, KVW])
        den = sb("den", [P, DC, HC])
        on = zq
        ztmp = zk
        hT = sb("hT", [P, 2, DC, P], fp16)
        gf = sb("gf", [P, HC, P])
        gT = sb("gT", [P, 2, 2, HC, P], fp16)
        yt = sb("yt", [P, D])
        betak_b = yt[:, :].rearrange("p (c e) -> p c e", c=DC)
        y2 = yt[:, :].bitcast(fp16).rearrange("p (l d) -> p l d", l=2)
        yT = pT[:, :, :].rearrange("p c q -> p (c q)").bitcast(fp16).rearrange("p (l c q) -> p l c q", l=2, c=DC)
        gw2 = sb("gw2", [P, 3, DC, E], bf16)
        ident16 = sb("ident16", [P, P], fp16)
        sums = sb("sums", [P, 21])
        total = sb("total", [P, len(SCALES)])
        root = sb("root", [P, len(SCALES)])
        scale = sb("scale", [P, len(SCALES)])
        unscale = sb("unscale", [P, len(SCALES)])
        gain_scale = {n: sb("gain_scale_" + n, [P, DC]) for n in ("wfq", "wfk", "w1")}
        squared = {0: kv[:, :, :, :].rearrange("p b c w -> p (b c w)").bitcast(bf16)[:, 0:CHUNK],
                   1: gT[:, :, :, :, :].rearrange("p a l f q -> p (a l f q)").bitcast(bf16)}
        NVEC = len(COLS) * DC + FC
        vectors = gf[:, :, :].rearrange("p f q -> p (f q)")[0:NVEC, 0:P]
        staged = [res[:, 8 + 4 * k:12 + 4 * k, :].rearrange("p t d -> p (t d)") for k in range(2)]
        gates = sb("gates", [P, T, E])
        stat_y = sb("stat_y", [P, T, 2])
        routed_x = proj[:, :, :, :].rearrange("p a c e -> p (a c e)")[:, 0:DC * E * T * P // E]\
            .rearrange("p (c e s) -> p c e s", c=DC, e=E)
        won = ctxs[:, :, :, :].rearrange("p b k c -> p (b k c)").rearrange("p (t s) -> p t s", t=T)
        won_gates = ctxT[:, 0, :]
        kv_flat = kv[:, :, :, :].rearrange("p b c w -> p (b c w)")
        y_again_of = [xn[:, :], zq[:, :], kv_flat[:, 0:D], kv_flat[:, D:2 * D],
                      zk2[:, :, :].rearrange("p l d -> p (l d)").bitcast(fp32)] + \
                     [a_[:, :, :, :].rearrange("p l c q -> p (l c q)").bitcast(fp32) for a_ in (xnT, zkT, lnxT)]
        scattered = (gf[:, :, :].rearrange("p f q -> p (f q)"), pT[:, :, :].rearrange("p c q -> p (c q)"))
        wonT = rows[:, 0:4, :].rearrange("p a c -> p (a c)").rearrange("p (t s) -> p t s", t=T)
        picks = rows[:, 4:6, :]
        expert_y = rows[:, 6:8, :]
        returned = proj[:, 4, :, :]
        TH = T // 2
        R = TH * E
        col_inv = probs[:, 0:R]
        gates_t = probs[0:R, P:2 * P]
        slots = probs[0:R, 2 * P:3 * P].rearrange("p (e s) -> p e s", e=E)
        row_sum = sb("row_sum", [P, T // 2])
        top_v = sb("top_v", [P, BPT, SLOTS])
        top_i = sb("top_i", [P, BPT, SLOTS], u32)
        top_f = sb("top_f", [P, BPT, SLOTS])
        best = sb("best", [P, 2, HC])
        gate_of = sb("gate_of", [P, T])
        NORMS = ["x", "x1", "q", "k", "v", "o", "y"]
        bn = {n: sb("bn_" + n, [P, 6]) for n in NORMS}
        mv = {n: sb("mv_" + n, [P, 2]) for n in NORMS}
        rstd = {n: sb("rstd_" + n, [P, 1]) for n in NORMS}
        var_eps = {n: sb("var_eps_" + n, [P, 1]) for n in NORMS}
        bank = [ctx.enter_context(nc.psum_tensor(f"bank{i}", [P, 512], fp32)) for i in range(8)]

        def bank16(k):
            return bank[k][:, :].bitcast(fp16).rearrange("p (l c q) -> p l c q", l=2, c=DC)

        def flat(ap):
            return ap.rearrange("p c e -> p (c e)")

        def split(ap, n):
            return ap.rearrange("p (a b) -> p a b", a=n)

        ctx_d = d["ctx"].rearrange("(t b) (k p) c -> t p b k c", b=BPT, p=P)
        x_d = d["x"].rearrange("(t b) q d -> (b q) t d", b=BPT)
        slot_rows = nc.dram_tensor("slot_rows", [T, E, BPT * SLOTS, D], fp32, kind="Internal").ap()
        out_d = out.rearrange("(t b) q d -> (b q) t d", b=BPT)

        in_x = sem("in_x")
        in_const = sem("in_const")
        in_cross = sem("in_cross")
        in_small = sem("in_small")
        in_cols = sem("in_cols")
        in_xwv = sem("in_xwv")
        cols_mm = sem("cols_mm")
        cols_ready = sem("cols_ready")
        in_proj = sem("in_proj")
        in_w1 = sem("in_w1")
        in_w2 = sem("in_w2")
        in_ctx = sem("in_ctx")
        prep_bc = sem("prep_bc")
        prep_t = sem("prep_t")
        prep_tcopy = sem("prep_tcopy")
        prep_mm = sem("prep_mm")
        prep_act = sem("prep_act")
        prep_chain = sem("prep_chain")
        qk_ready = sem("qk_ready")
        folded = sem("folded")
        squares = sem("squares")
        totals = sem("totals")
        scale_chain = sem("scale_chain")
        root_ready = sem("root_ready")
        scales_ready = sem("scales_ready")
        chunk_staged = sem("chunk_staged")
        chunk_split = sem("chunk_split")
        hi_split = sem("hi_split")
        consts16 = sem("consts16")
        stat_kept = sem("stat_kept")
        weights_ready = sem("weights_ready")
        mv_ready = {n: sem("mv_ready_" + n) for n in NORMS}
        rstd_ready = {n: sem("rstd_ready_" + n) for n in NORMS}
        waits_passed = sem("waits_passed")
        bn_done = {n: sem("bn_done_" + n) for n in NORMS}
        eps_done = {n: sem("eps_done_" + n) for n in NORMS}
        a_t = sem("a_t")
        a_tcopy = sem("a_tcopy")
        a_mm = sem("a_mm")
        a_used = sem("a_used")
        z_chain = {n: sem("z_chain_" + n) for n in NORMS}
        g_raw = sem("g_raw")
        g_hi = sem("g_hi")
        gs_chain = sem("gs_chain")
        qb_chain = sem("qb_chain")
        lnx_ready = sem("lnx_ready")
        xbv_ready = sem("xbv_ready")
        scores0_done = sem("scores0_done")
        amax_done = sem("amax_done")
        abias_ready = sem("abias_ready")
        rl_ready = sem("rl_ready")
        b_mm = sem("b_mm")
        b2_used = sem("b2_used")
        b3_used = sem("b3_used")
        xn_ready = sem("xn_ready")
        res_xn = sem("res_xn")
        z_ready = {n: sem("z_ready_" + n) for n in "qkv"}
        v_scaled = sem("v_scaled")
        v_ready = sem("v_ready")
        tanh_q = sem("tanh_q")
        tanh_k = sem("tanh_k")
        pk_ready = sem("pk_ready")
        probe_chain = sem("probe_chain")
        pm_ready = sem("pm_ready")
        lg_mm = sem("lg_mm")
        lm_chain = sem("lm_chain")
        lm_ready = sem("lm_ready")
        exp_ready = sem("exp_ready")
        sc_chain = sem("sc_chain")
        score_ready = sem("score_ready")
        ex_mm = sem("ex_mm")
        sv_ready = sem("sv_ready")
        kv_ready = sem("kv_ready")
        den_chain = sem("den_chain")
        za_ready = sem("za_ready")
        hT_mm = sem("hT_mm")
        hT_ready = sem("hT_ready")
        gated_chain = sem("gated_chain")
        res_ready = sem("res_ready")
        h1_mm = sem("h1_mm")
        g_ready = sem("g_ready")
        h2_mm = sem("h2_mm")
        x2_ready = sem("x2_ready")
        yt_ready = sem("yt_ready")
        yT_mm = sem("yT_mm")
        yT_ready = sem("yT_ready")
        gl_mm = sem("gl_mm")
        gl_used = sem("gl_used")

        out_done = sem("out_done")
        cs_mm = sem("cs_mm")
        sink_chain = sem("sink_chain")
        sink_done = sem("sink_done")
        gates_mm = sem("gates_mm")
        top_chain = sem("top_chain")
        picks_ready = sem("picks_ready")
        picks_mm = sem("picks_mm")
        won_chain = sem("won_chain")
        won_ready = sem("won_ready")
        wonT_mm = sem("wonT_mm")
        wonT_ready = sem("wonT_ready")
        y_again = [sem(f"y_again{h}") for h in range(2)]
        gather_mm = sem("gather_mm")
        gathered = sem("gathered")
        in_experts = [sem(f"in_expert{e}") for e in range(E)]
        expert_mm = sem("expert_mm")
        expert_copied = sem("expert_copied")
        expert_stored = [sem(f"expert_stored{k}") for k in range(2)]
        in_returned = [sem(f"in_returned{k}") for k in range(4)]
        scatter_mm = sem("scatter_mm")
        x3_ready = [sem(f"x3_ready{h}") for h in range(2)]
        row_scaled = sem("row_scaled")

        A_T, A_MM, B_MM, B2, B3 = 6, 4, 14, 7, 7
        O_MM = 3
        SMALL = 16 * (len(ROWS) + 2)
        VECTORS = 16 * (len(COLS) + 1)

        block = ctx.enter_context(nc.Block())

        def rounds(eng, body):
            def some(t):
                return t if 0 <= t < T else None
            for i in range(4):
                body(i, *(some(i + 1 - k) for k in range(5)))
            with eng.Fori(4, T - 1) as i:
                body(i, i + 1, i, i - 1, i - 2, i - 3)
            for i in range(T - 1, T + 3):
                body(i, *(some(i + 1 - k) for k in range(5)))

        @block.sync
        def _(sp):
            sp.dma_start(cst[:, :], d["consts"]).then_inc(in_const, 16)
            sp.dma_start(xwq, d["x_wq"].rearrange("(c p) e -> p c e", p=P)).then_inc(in_cross, 16)
            sp.dma_start(xwk, d["x_wk"].rearrange("(c p) e -> p c e", p=P)).then_inc(in_cross, 16)
            for n in COLS:
                at = COLS.index(n) * DC
                sp.dma_start(vectors[at:at + DC, :], d["c_" + n].rearrange("(c p) -> c p", p=P)).then_inc(in_cols, 16)
            sp.dma_start(vectors[len(COLS) * DC:, :], d["b1"].rearrange("(c p) -> c p", p=P)).then_inc(in_cols, 16)
            sp.dma_start(res[:, 0:4, :], x_d[:, 0:4, :]).then_inc(in_x, 16)
            sp.dma_start(ctxs[:, 0], ctx_d[0, :, 0]).then_inc(in_ctx, 16)
            sp.dma_start(ctxs[:, 1], ctx_d[0, :, 1]).then_inc(in_ctx, 16)
            sp.dma_start(xwv[:, :, :], d["x_wv"].rearrange("(c p) e -> p c e", p=P)).then_inc(in_xwv, 16)
            for n in ("wfq", "wfk", "wq", "wk", "wv"):
                sp.dma_start(proj_32[n], d[n].rearrange("(c p) e -> p c e", p=P)).then_inc(in_proj, 16)
            sp.dma_start(w1_32, d["w1"].rearrange("(c p) f -> p c f", p=P)).then_inc(in_w1, 16)
            sp.wait_ge(prep_mm, 2)
            sp.wait_ge(chunk_split, 1)
            sp.dma_start(w2_32, d["w2"].rearrange("(f p) e -> p f e", p=P)).then_inc(in_w2, 16)

            def reload(i, x, a, b, m, g):
                if a is not None and not (isinstance(a, int) and a == 0):
                    after(sp, a_mm, A_MM, a - 1, O_MM)
                    sp.dma_start(ctxs[:, 0], ctx_d[a, :, 0]).then_inc(in_ctx, 16)
                    sp.dma_start(ctxs[:, 1], ctx_d[a, :, 1]).then_inc(in_ctx, 16)
                if isinstance(i, int) and i == 2:
                    sp.wait_ge(chunk_split, 14)
                    sp.dma_start(res[:, 4:T, :], x_d[:, 4:T, :]).then_inc(in_x, 16)
            rounds(sp, reload)
            for e in range(E):
                if e == 0:
                    sp.wait_ge(h1_mm, 4 * T)
                if e == E // 2:
                    sp.wait_ge(h2_mm, 4 * T)
                sp.dma_start(experts[:, e], d["experts"][e].rearrange("(c p) f -> p c f", p=P)).then_inc(in_experts[e], 16)
            for h in range(2):
                for e in range(E):
                    u = E * h + e
                    sp.wait_ge(expert_copied, u + 1)
                    sp.dma_start(slot_rows[h * TH:(h + 1) * TH, e, :, :], expert_y[:, u % 2, :])\
                        .then_inc(expert_stored[u % 2], 16)
                for k in range(2):
                    sp.wait_ge(expert_stored[k], 16 * E // 2 * (h + 1))
                for t in range(h * TH, (h + 1) * TH + 3):
                    if t < (h + 1) * TH:
                        if t >= 4:
                            sp.wait_ge(scatter_mm, t - 3)
                        sp.dma_start(returned[:, t % 4, :], slot_rows[t].rearrange("e s f -> (e s) f"))\
                            .then_inc(in_returned[t % 4], 16)
                    if t >= h * TH + 3:
                        sp.wait_ge(x3_ready[h], t - 3 - h * TH + 1)
                        sp.dma_start(out_d[:, t - 3, :], res[:, t - 3, :]).then_inc(out_done, 16)
            sp.wait_ge(out_done, 16 * T)

        @block.gpsimd
        def _(pool):
            pool.wait_ge(in_const, 16)

            def roots(n, a, b, exponent=0):
                pool.wait_ge(scale_chain, n)
                pool.tensor_tensor(root[:, a:b], total[:, a:b], c["minus_half"][:, 0:1].broadcast_to([P, b - a]), ALU.pow)\
                    .then_inc(root_ready, 1)


            def rsqrt(n, t):
                after_apart(pool, mv_ready[n], 1, t, 1)
                pool.tensor_scalar(var_eps[n][:, :], mv[n][:, 1:2], LN_EPS, None, ALU.add).then_inc(eps_done[n], 1)
                after_apart(pool, eps_done[n], 1, t, 1)
                pool.tensor_tensor(rstd[n][:, :], var_eps[n][:, :], c["minus_half"][:, 0:1], ALU.pow)\
                    .then_inc(rstd_ready[n], 1)

            def norm_again(t):
                if t == 0:
                    pool.wait_ge(stat_kept, TH)
                    pool.wait_ge(res_ready, T)
                    pool.wait_ge(za_ready, T)
                pool.tensor_scalar(y_again_of[t % TH], res[:, t, :], stat_y[:, t, 0:1], stat_y[:, t, 1:2],
                                   ALU.subtract, ALU.mult).then_inc(y_again[0], 1)

            def body(i, x, a, b, m, g):
                if isinstance(i, int) and i == 0:
                    roots(2, 1, 6)
                if b is not None:
                    after_apart(pool, xn_ready, 1, b, 1)
                    pool.tensor_tensor(res[:, b, :], res[:, b, :], xn[:, :], ALU.add).then_inc(res_xn, 1)
                    rsqrt("q", b)
                if a is not None:
                    after_apart(pool, lnx_ready, 1, a, 1)
                    pool.tensor_tensor(res[:, a, :], res[:, a, :], row["x_bv"], ALU.add).then_inc(xbv_ready, 1)
                    if isinstance(i, int) and i == 0:
                        roots(3, 6, 8)
                if b is not None:
                    rsqrt("k", b)
                    rsqrt("v", b)
                    after_apart(pool, z_ready["v"], 1, b, 1)
                    pool.tensor_tensor(zv, zv, split(row["gv"], DC), ALU.mult).then_inc(v_scaled, 1)
                    after_apart(pool, v_scaled, 1, b, 1)
                    pool.tensor_tensor(zv, zv, split(row["betav"], DC), ALU.add).then_inc(v_ready, 1)
                    after_apart(pool, tanh_k, 1, b, 1)
                    pool.tensor_scalar(pk[:, :], pk[:, :], 1.0, None, ALU.add).then_inc(pk_ready, 1)
                if x is not None:
                    rsqrt("x", x)
                if isinstance(i, int) and i == 1:
                    roots(4, 8, 9)
                if a is not None:
                    rsqrt("x1", a)
                if b is not None:
                    rsqrt("o", b)
                if isinstance(i, int) and i == T + 1:
                    for t in range(TH):
                        norm_again(t)
                if m is not None:
                    rsqrt("y", m)
                if b is not None:
                    after_apart(pool, za_ready, 1, b, 1)
                    after_apart(pool, res_xn, 1, b, 1)
                    pool.tensor_tensor(on[:, :], on[:, :], row["ga"], ALU.mult).then_inc(gated_chain, 1)
                    pool.tensor_tensor(res[:, b, :], res[:, b, :], row["b2"], ALU.add).then_inc(gated_chain, 1)
                    after_apart(pool, gated_chain, 2, b, 2)
                    pool.tensor_tensor(res[:, b, :], res[:, b, :], on[:, :], ALU.add).then_inc(res_ready, 1)
            rsqrt("x", 0)
            roots(1, 0, 1)
            pool.wait_ge(in_small, SMALL)
            pool.wait_ge(prep_bc, 2)
            rounds(pool, body)
            for t in range(TH):
                pool.wait_ge(row_scaled, t + 1)
                pool.tensor_tensor(res[:, t, :], res[:, t, :], scattered[t % 2], ALU.add).then_inc(x3_ready[0], 1)

        @block.scalar
        def _(act):
            act.wait_ge(in_cols, VECTORS)
            act.dma_start(gw[:, :, :], d["gate_w"].rearrange("(c p) e -> p c e", p=P)).then_inc(in_small, 16)
            for n in ROWS:
                act.dma_start(row[n], d["r_" + n].partition_broadcast(P)).then_inc(in_small, 16)
            act.dma_start(on[:, :], d["c_ba"].partition_broadcast(P)).then_inc(in_small, 16)
            act.wait_ge(cols_ready, 1)
            act.activation(s0feat[:, :], col["bfk"], ACT.Tanh).then_inc(prep_act, 1)

            def parts(chunk, gains):
                n = 1 if gains is None else gains.shape[1]
                return [(slice(f * (chunk.shape[1] // n), (f + 1) * (chunk.shape[1] // n)),
                         None if gains is None else gains[:, f:f + 1]) for f in range(n)]

            def square(k, chunk, gains=None):
                for f, (at, gain) in enumerate(parts(chunk, gains)):
                    after(act, squares, 1, 0, square_count[k] + f)
                    act.activation(squared[int(k >= 6)][:, 0:at.stop - at.start], chunk[:, at], ACT.Square,
                                   scale=1.0 if gain is None else gain,
                                   accum_out=sums[:, square_count[k] + f:square_count[k] + f + 1]).then_inc(squares, 1)

            def stage(k, chunk, n, gains=None):
                if k >= 2:
                    act.wait_ge(chunk_split, k - 1)
                for at, gain in parts(chunk, gains):
                    last = act.activation(staged[k % 2][:, at], chunk[:, at], ACT.Copy,
                                          scale=scale[:, MATS[n]:MATS[n] + 1] if gain is None else gain)
                last.then_inc(chunk_staged, 1)

            def query_copy(x):
                after(act, a_t, A_T, x, 1)
                act.copy(lnxT[:, :, :, :], bank16(0)).then_inc(a_tcopy, 1)

            act.wait_ge(qk_ready, 1)
            square(0, qk_32)
            act.wait_ge(scales_ready, 1)
            stage(0, qk_32, "qk")
            query_copy(0)

            def square_mlp(k):
                if k == 0:
                    act.wait_ge(in_w1, 16)
                if k == DC:
                    act.wait_ge(in_w2, 16)
                square(6 + k, w12[:, k * CHUNK:(k + 1) * CHUNK], col["ga"][:, k:k + 1] if k < DC else None)

            def square_attention():
                act.wait_ge(in_proj, 80)
                for k, n in enumerate(PROJ):
                    square(1 + k, flat(proj_32[n]), {"wfq": col["gq"], "wfk": col["gk"]}.get(n))
                for k in range(3):
                    square_mlp(k)
                act.wait_ge(scales_ready, 2)

            def square_mlp_bias():
                act.wait_ge(folded, 1)
                square(14, b1c[:, :])

            def stage_attention(k):
                stage(1 + k, flat(proj_32[PROJ[k]]), PROJ[k], gain_scale.get(PROJ[k]))

            def stage_mlp(n):
                k = MLP_CHUNKS[n]
                stage(6 + n, w12[:, k * CHUNK:(k + 1) * CHUNK], "w1" if k < DC else "w2",
                      gain_scale["w1"][:, k:k + 1] if k < DC else None)

            def winners_copy(k):
                act.wait_ge(wonT_mm, k + 1)
                act.copy(wonT[:, 4 * k:4 * k + 4, :], split(bank[k % 2][:, :], 4)).then_inc(wonT_ready, 1)

            def gather_copy(t):
                act.wait_ge(gather_mm, t + 1)
                act.copy(routed_x[:, :, :, t * BPT * SLOTS:(t + 1) * BPT * SLOTS],
                         bank[2 + t % 2][:, :].rearrange("p (c e s) -> p c e s", c=DC, e=E)).then_inc(gathered, 1)

            def body(i, x, a, b, m, g):
                def weights(k):
                    if isinstance(i, int) and i == 0:
                        if k < 5:
                            stage_attention(k)
                            square_mlp(3 + k)
                        else:
                            if k == 5:
                                act.wait_ge(scales_ready, 3)
                            stage_mlp(k - 5)
                    if isinstance(i, int) and i == 1 and k < 5:
                        stage_mlp(3 + k)
                    if isinstance(i, int) and i == T + 1 and k == 7:
                        winners_copy(0)
                        winners_copy(1)

                if isinstance(i, int) and i == T + 2:
                    for t in range(TH // 2):
                        gather_copy(t)

                if isinstance(i, int) and i == 0:
                    square_attention()
                if isinstance(i, int) and i == 1:
                    square_mlp_bias()
                if isinstance(i, int) and i == 2:
                    act.wait_ge(scales_ready, 4)

                def gelu(j):
                    after(act, h1_mm, 4, m, j + 1)
                    after(act, g_ready, 4, m, j)
                    for f in range(HC):
                        g_ins = act.activation(gf[:, f, :], bank[5 + j % 2][:, f * P:(f + 1) * P], ACT.Gelu,
                                               bias=b1c[:, j * HC + f:j * HC + f + 1],
                                               scale=unscale[:, MATS["w1"]:MATS["w1"] + 1])
                    g_ins.then_inc(g_raw, 1)
                    after(act, g_raw, 4, m, j + 1)
                    after(act, h2_mm, 4, m, j - 1)
                    act.activation(gT[:, j % 2, 0], gf[:, :, :], ACT.Copy, scale=scale[:, MATS["g"]:MATS["g"] + 1])\
                        .then_inc(g_hi, 1)
                weights(0)
                if m is not None:
                    after(act, hT_mm, 1, m, 1)
                    act.copy(hT[:, :, :, :], bank16(4)).then_inc(hT_ready, 1)
                if b is not None:
                    after(act, b_mm, B_MM, b, 1)
                    act.copy(xnT[:, :, :, :], bank16(2)).then_inc(b2_used, 1)
                weights(1)
                if m is not None:
                    gelu(0)
                if g is not None:
                    after(act, yT_mm, 1, g, 1)
                    act.copy(yT, bank16(7)).then_inc(yT_ready, 1)
                if m is not None:
                    gelu(1)
                weights(2)
                if a is not None:
                    after(act, a_t, A_T, a, 3)
                    act.copy(ctxT[:, 1, :], bank[0][:, :]).then_inc(a_tcopy, 1)
                weights(3)
                if b is not None:
                    after(act, b_mm, B_MM, b, 6)
                    act.copy(zkT[:, :, :, :], bank16(3)).then_inc(b3_used, 1)
                if m is not None:
                    gelu(2)
                weights(4)
                if b is not None:
                    after(act, b_mm, B_MM, b, 7)
                    after(act, pm_ready, 1, b, 1)
                    for f in range(DC):
                        t_ins = act.activation(pqT[:, f, :], bank[2][:, f * P:(f + 1) * P], ACT.Tanh,
                                               bias=tq[:, f:f + 1], scale=unscale[:, MATS["wfq"]:MATS["wfq"] + 1])
                    t_ins.then_inc(tanh_q, 1)
                if a is not None:
                    after(act, a_t, A_T, a, 5)
                    act.copy(ctxT[:, 1, :], bank[0][:, :]).then_inc(a_tcopy, 1)
                weights(5)
                if b is not None:
                    after(act, b3_used, B3, b, 4)
                    act.activation(pk[:, :], pk[:, :], ACT.Tanh).then_inc(tanh_k, 1)
                if a is not None:
                    after(act, abias_ready, 1, a, 1)
                    act.activation(probs[:, :], bank[1][:, :], ACT.Exp, bias=abias[:, 0:1],
                                   accum_out=lsum[:, 0:1]).then_inc(a_used, 1)
                weights(6)
                if b is not None:
                    after(act, lm_ready, 1, b, 1)
                    act.activation(scd[:, :], lm[:, :], ACT.Exp, bias=lneg[:, 1:2], accum_out=lsm[:, 0:1])
                    act.activation(lsm[:, 1:2], lneg[:, 1:2], ACT.Exp).then_inc(exp_ready, 1)
                if m is not None:
                    gelu(3)
                weights(7)
                if x is not None:
                    query_copy(x)
            rounds(act, body)
            for t in range(TH // 2, TH):
                gather_copy(t)
            def copy_expert(u):
                act.wait_ge(expert_mm, u + 1)
                if u >= 2:
                    act.wait_ge(expert_stored[u % 2], 16 * (u // 2))
                act.copy(expert_y[:, u % 2, :], bank[6 + u % 2][:, :]).then_inc(expert_copied, 1)

            def scale_row(t):
                act.wait_ge(scatter_mm, t + 1)
                if t >= 2:
                    act.wait_ge(x3_ready[0], t - 1)
                act.activation(scattered[t % 2], bank[4 + t % 2][:, :], ACT.Copy, scale=gate_of[:, t:t + 1])\
                    .then_inc(row_scaled, 1)

            for u in range(E):
                copy_expert(u)
            for t in range(TH // 2):
                scale_row(t)
            winners_copy(2)
            for t in range(TH // 2, TH):
                scale_row(t)
            winners_copy(3)
            for t in range(TH, T):
                gather_copy(t)
            for u in range(E, 2 * E):
                copy_expert(u)

        @block.vector
        def _(dve):
            def bc(ap, n, shape):
                return ap.unsqueeze(n).broadcast_to(shape)

            def stats(n, t, ap):
                dve.bn_stats(bn[n][:, :], ap).then_inc(bn_done[n], 1)
                after_apart(dve, bn_done[n], 1, t, 1)
                dve.bn_aggr(mv[n][:, :], bn[n][:, :]).then_inc(mv_ready[n], 1)

            def norm_split(n, t, pair, z, in_, ready):
                norm(n, t, z, in_).then_inc(z_chain[n], 1)
                halves_of(n, t, pair, z, ready)

            def halves_of(n, t, pair, z, ready):
                after(dve, z_chain[n], 2, t, 1)
                dve.tensor_scalar(pair[:, 0, :], z, Z_SCALE, None, ALU.mult).then_inc(z_chain[n], 1)
                after(dve, z_chain[n], 2, t, 2)
                dve.scalar_tensor_tensor(pair[:, 1, :], z, Z_SCALE, pair[:, 0, :], ALU.mult, ALU.subtract)\
                    .then_inc(ready, 1)

            def norm(n, t, out_, in_):
                after(dve, rstd_ready[n], 1, t, 1)
                return dve.tensor_scalar(out_, in_, mv[n][:, 0:1], rstd[n][:, 0:1], ALU.subtract, ALU.mult)

            dve.memset(pm0[:, :, :], 0.0)
            dve.memset(pm1s[:, :, :, :], 0.0)
            dve.wait_ge(in_const, 16)
            dve.tensor_copy(ident16[:, :], c["ident"]).then_inc(consts16, 1)
            dve.wait_ge(prep_t, 1)
            for k in range(DC):
                dve.tensor_copy(xwqT[:, k, :], bank[k][:, :])
            dve.tensor_copy(xwkT[:, 0:2, :], split(bank[4][:, :], 2))
            dve.tensor_copy(xwkT[:, 2:4, :], split(bank[5][:, :], 2)).then_inc(prep_tcopy, 1)
            dve.wait_ge(cols_mm, 1)
            dve.tensor_copy(cols[:, :, :].rearrange("p n c -> p (n c)"), bank[6][:, 0:len(COLS) * DC])
            dve.tensor_copy(b1c[:, :], bank[6][:, len(COLS) * DC:NVEC]).then_inc(cols_ready, 1)
            dve.wait_ge(cols_ready, 1)
            for k in range(DC):
                dve.tensor_scalar(betak_b[:, k, :], c["ones"], col["betak"][:, k:k + 1], None, ALU.mult)
                last = dve.tensor_scalar(xbq_b[:, k, :], c["ones"], col["x_bq"][:, k:k + 1], None, ALU.mult)
            last.then_inc(prep_bc, 1)
            dve.wait_ge(in_x, 16)
            stats("x", 0, res[:, 0, :])
            norm_split("x", 0, lnx, xn[:, :], res[:, 0, :], lnx_ready)
            dve.wait_ge(prep_mm, 1)
            dve.tensor_copy(qk_32[:, 0:512], bank[6][:, :])
            dve.tensor_copy(qk_32[:, 512:1024], bank[7][:, :]).then_inc(qk_ready, 1)
            def scales(n, a, b, source):
                base = 3 * (n - 1) + (4 if n > 1 else 0)
                dve.wait_ge(totals, n)
                dve.tensor_scalar(total[:, a:b], source, 1e-30, None, ALU.add).then_inc(scale_chain, 1)
                dve.wait_ge(root_ready, n)
                dve.tensor_scalar(scale[:, a:b], root[:, a:b], W_TOP, None, ALU.mult).then_inc(gs_chain, 1)
                dve.wait_ge(gs_chain, base + 1)
                dve.tensor_scalar(scale[:, a:b].bitcast(i32), scale[:, a:b].bitcast(i32), EXPONENT_BITS, None,
                                  ALU.bitwise_and).then_inc(gs_chain, 1)
                dve.wait_ge(gs_chain, base + 2)
                dve.reciprocal(unscale[:, a:b], scale[:, a:b]).then_inc(gs_chain, 1)
                dve.wait_ge(gs_chain, base + 3)
                return dve.tensor_scalar(unscale[:, a:b], unscale[:, a:b], 1.0 / Z_SCALE, None, ALU.mult)

            def halves(k, pair):
                n = pair.shape[2]
                dve.wait_ge(chunk_staged, k + 1)
                dve.tensor_copy(pair[:, 0, :], staged[k % 2][:, 0:n]).then_inc(hi_split, 1)
                dve.wait_ge(hi_split, k + 1)
                dve.tensor_tensor(pair[:, 1, :], staged[k % 2][:, 0:n], pair[:, 0, :], ALU.subtract)\
                    .then_inc(chunk_split, 1)

            scales(1, 0, 1, bank[6][:, 32:33]).then_inc(scales_ready, 1)
            halves(0, qk[:, :, :, :].rearrange("p l c e -> p l (c e)"))
            dve.wait_ge(prep_mm, 2)
            dve.tensor_copy(qk_bias[:, :], bank[4][:, 0:CC])
            dve.tensor_copy(q_bk_rest[:, :], bank[4][:, 8:8 + DC])
            dve.tensor_copy(bq_bk[:, :], bank[4][:, 16:17]).then_inc(qb_chain, 1)

            dve.wait_ge(qb_chain, 1)
            dve.tensor_copy(q_bk[:, 0, :], q_bk_rest[:, :]).then_inc(qb_chain, 1)
            dve.wait_ge(qb_chain, 2)
            dve.tensor_tensor(q_bk_rest[:, :], q_bk_rest[:, :], q_bk[:, 0, :], ALU.subtract).then_inc(qb_chain, 1)
            dve.wait_ge(qb_chain, 3)
            dve.tensor_copy(q_bk[:, 1, :], q_bk_rest[:, :]).then_inc(qb_chain, 1)
            dve.wait_ge(qb_chain, 4)
            dve.tensor_tensor(q_bk[:, 2, :], q_bk_rest[:, :], q_bk[:, 1, :], ALU.subtract)
            dve.wait_ge(in_small, SMALL)
            dve.tensor_copy(gw2[:, 0], gw[:, :, :]).then_inc(gs_chain, 1)
            dve.wait_ge(gs_chain, 4)
            dve.tensor_tensor(gw[:, :, :], gw[:, :, :], gw2[:, 0], ALU.subtract).then_inc(gs_chain, 1)
            dve.wait_ge(gs_chain, 5)
            dve.tensor_copy(gw2[:, 1], gw[:, :, :]).then_inc(gs_chain, 1)
            dve.wait_ge(gs_chain, 6)
            dve.tensor_tensor(gw2[:, 2], gw[:, :, :], gw2[:, 1], ALU.subtract).then_inc(gs_chain, 1)

            dve.tensor_tensor(row["b2"], row["b2"], on[:, :], ALU.add).then_inc(prep_bc, 1)

            def gains(n, g_):
                return dve.tensor_scalar(gain_scale[n][:, :], col[g_], scale[:, MATS[n]:MATS[n] + 1], None, ALU.mult)

            def prepare_attention():
                dve.wait_ge(prep_mm, 3)
                dve.tensor_tensor(tq[:, :], bank[3][:, 0:DC], col["bfq"], ALU.add)
                dve.tensor_tensor(row["bfk"], bank[2][:, :], row["bfk"], ALU.add)
                dve.wait_ge(prep_act, 1)
                dve.tensor_scalar(s0feat[:, :], s0feat[:, :], 1.0, None, ALU.add).then_inc(prep_chain, 1)
                dve.wait_ge(prep_chain, 1)
                dve.tensor_tensor(zero_key[:, :, :], bc(s0feat[:, :], 2, [P, DC, HC]),
                                  bc(c["block_mask"][:, P:KVW], 1, [P, DC, HC]), ALU.mult)
                scales(2, 1, 6, bank[6][:, 32:37])
                gains("wfq", "gq")
                gains("wfk", "gk").then_inc(scales_ready, 1)
                dve.wait_ge(scales_ready, 2)
                dve.tensor_scalar(col["gq"], col["gq"], 1.0 / (NQ * DH ** 0.5 * Z_SCALE), None, ALU.mult)
                dve.tensor_scalar(col["betaq"], col["betaq"], 1.0 / DH ** 0.5, None, ALU.mult).then_inc(weights_ready, 1)
                dve.wait_ge(weights_ready, 1)

            def mlp_halves(n):
                k = MLP_CHUNKS[n]
                halves(6 + n, as_pair(w12[:, k * CHUNK:(k + 1) * CHUNK]))

            def prepare_mlp():
                dve.wait_ge(prep_mm, 4)
                dve.tensor_tensor(b1c[:, :], bank[5][:, 0:FC], b1c[:, :], ALU.add).then_inc(folded, 1)

            def scale_gelu():
                scales(4, 8, 9, bank[6][:, 34:35]).then_inc(gs_chain, 1)
                w1_, w2_, b1_, g_ = (MATS[n] for n in ("w1", "w2", "b1", "g"))
                dve.tensor_tensor(total[:, w1_:b1_ + 1], total[:, w1_:b1_ + 1], root[:, w1_:b1_ + 1], ALU.mult)\
                    .then_inc(gs_chain, 1)
                dve.wait_ge(gs_chain, 18)
                dve.scalar_tensor_tensor(total[:, g_:g_ + 1], total[:, w1_:w1_ + 1], Z_NORM, total[:, b1_:b1_ + 1],
                                         ALU.mult, ALU.add).then_inc(gs_chain, 1)
                dve.wait_ge(gs_chain, 19)
                dve.reciprocal(root[:, g_:g_ + 1], total[:, g_:g_ + 1]).then_inc(gs_chain, 1)
                dve.wait_ge(gs_chain, 20)
                dve.tensor_scalar(scale[:, g_:g_ + 1], root[:, g_:g_ + 1], G_TOP, None, ALU.mult).then_inc(gs_chain, 1)
                dve.wait_ge(gs_chain, 21)
                dve.tensor_scalar(scale[:, g_:g_ + 1].bitcast(i32), scale[:, g_:g_ + 1].bitcast(i32), EXPONENT_BITS, None,
                                  ALU.bitwise_and).then_inc(gs_chain, 1)
                dve.wait_ge(gs_chain, 22)
                dve.reciprocal(unscale[:, g_:g_ + 1], scale[:, g_:g_ + 1]).then_inc(gs_chain, 1)
                dve.wait_ge(gs_chain, 23)
                dve.tensor_scalar(unscale[:, w2_:w2_ + 1], unscale[:, w2_:w2_ + 1], unscale[:, g_:g_ + 1], Z_SCALE,
                                  ALU.mult, ALU.mult).then_inc(scales_ready, 1)

            def sinkhorn(h, r):
                half = gates[:, h * TH:(h + 1) * TH, :]
                done = 4 * SINKHORN_ROUNDS * h
                after(dve, cs_mm, 1, r, SINKHORN_ROUNDS * h + 1)
                dve.reciprocal(col_inv, bank[0][:, 0:R]).then_inc(sink_chain, 1)
                after(dve, sink_chain, 4, r, done + 1)
                dve.tensor_tensor(half, half, split(col_inv, TH), ALU.mult).then_inc(sink_chain, 1)
                after(dve, sink_chain, 4, r, done + 2)
                dve.tensor_reduce(row_sum[:, :], half, AX, ALU.add).then_inc(sink_chain, 1)
                after(dve, sink_chain, 4, r, done + 3)
                dve.reciprocal(row_sum[:, :], row_sum[:, :]).then_inc(sink_chain, 1)
                after(dve, sink_chain, 4, r, done + 4)
                dve.tensor_tensor(half, half, bc(row_sum[:, :], 2, [P, TH, E]), ALU.mult).then_inc(sink_done, 1)

            def top(h):
                done = h * (3 + 2 * BPT)
                dve.wait_ge(gates_mm, h + 1)
                dve.tensor_copy(gates_t, bank[1][0:R, 0:P]).then_inc(top_chain, 1)
                dve.wait_ge(top_chain, done + 1)
                for b in range(BPT):
                    dve.max(top_v[0:R, b, :], gates_t[:, b * NQ:(b + 1) * NQ]).then_inc(top_chain, 1)
                dve.wait_ge(top_chain, done + 1 + BPT)
                for b in range(BPT):
                    dve.max_index(top_i[0:R, b, :], top_v[0:R, b, :], gates_t[:, b * NQ:(b + 1) * NQ]).then_inc(top_chain, 1)
                dve.wait_ge(top_chain, done + 1 + 2 * BPT)
                for b in range(BPT):
                    last = dve.tensor_scalar(top_f[0:R, b, :], top_i[0:R, b, :], float(b * NQ), None, ALU.add)
                last.then_inc(top_chain, 1)
                dve.wait_ge(top_chain, done + 2 + 2 * BPT)
                dve.tensor_tensor(slots, bc(top_f[0:R, :, :].rearrange("p b s -> p (b s)"), 1, [R, E, BPT * SLOTS]),
                                  bc(c["expert_of_row"][0:R], 2, [R, E, BPT * SLOTS]), ALU.mult).then_inc(top_chain, 1)
                dve.wait_ge(top_chain, done + 3 + 2 * BPT)
                if h == 1:
                    dve.wait_ge(picks_mm, 2)
                for k in range(2):
                    dve.tensor_tensor(picks[0:R, k, :].rearrange("p (t s) -> p t s", t=4),
                                      bc(slots.rearrange("p e s -> p (e s)"), 1, [R, 4, P]),
                                      bc(c["tile_of_row"][0:R, 4 * k:4 * k + 4], 2, [R, 4, P]), ALU.mult)\
                        .then_inc(picks_ready, 1)

            def winners(k):
                w4 = won[:, 4 * k:4 * k + 4, :]
                dve.wait_ge(picks_mm, k + 1)
                dve.scalar_tensor_tensor(w4, split(bank[2 + k % 2][:, :], 4), c["token_id"],
                                         bc(c["slot_code"], 1, [P, 4, P]), ALU.is_equal, ALU.mult).then_inc(won_chain, 1)
                dve.wait_ge(won_chain, 5 * k + 1)
                dve.tensor_reduce(best[:, 0, :], w4, AX, ALU.max).then_inc(won_chain, 1)
                dve.wait_ge(won_chain, 5 * k + 2)
                dve.tensor_scalar(best[:, 1, :], best[:, 0, :], 0.5, None, ALU.max).then_inc(won_chain, 1)
                dve.wait_ge(won_chain, 5 * k + 3)
                dve.tensor_tensor(w4, w4, bc(best[:, 1, :], 2, [P, 4, P]), ALU.is_equal).then_inc(won_chain, 1)
                dve.wait_ge(won_chain, 5 * k + 4)
                g4 = won_gates.rearrange("p (t e s) -> p t e s", t=4, e=E)
                dve.tensor_tensor(g4, w4.rearrange("p t (e s) -> p t e s", e=E),
                                  bc(gates[:, 4 * k:4 * k + 4, :], 3, [P, 4, E, BPT * SLOTS]), ALU.mult).then_inc(won_chain, 1)
                dve.wait_ge(won_chain, 5 * k + 5)
                dve.tensor_reduce(gate_of[:, 4 * k:4 * k + 4], won_gates.rearrange("p (t s) -> p t s", t=4), AX, ALU.add)\
                    .then_inc(won_ready, 1)

            def project(n, z, bk, k, used, per_tile, count, b):
                after(dve, b_mm, B_MM, b, k)
                dve.scalar_tensor_tensor(z, split(bank[bk][:, :], DC), unscale[:, MATS["w" + n]:MATS["w" + n] + 1],
                                         split(row["b" + n], DC), ALU.mult, ALU.add).then_inc(used, 1)
                after(dve, used, per_tile, b, count)
                stats(n, b, z)

            def body(i, x, a, b, m, g):
                def weights(k):
                    if isinstance(i, int) and i == 0 and k < 5:
                        halves(1 + k, (wfq, wfk, wq, wk, wv)[k].rearrange("p l c e -> p l (c e)"))
                    if isinstance(i, int) and i == 0 and k >= 5 and k < 8:
                        if k == 5:
                            scales(3, 6, 8, bank[6][:, 32:34])
                            gains("w1", "ga").then_inc(scales_ready, 1)
                        mlp_halves(k - 5)
                    if isinstance(i, int) and i == 1 and k < 5:
                        mlp_halves(3 + k)
                    if isinstance(i, int) and i == 1 and k == 7:
                        scale_gelu()
                    if isinstance(i, int) and i == T and k != 7:
                        sinkhorn(0, min(k, 7))
                    if isinstance(i, int) and i == T + 1 and k == 0:
                        top(0)
                    if isinstance(i, int) and i == T + 1 and k in (2, 4):
                        winners(k // 2 - 1)

                def gelu_low(j):
                    after(dve, g_hi, 4, m, j + 1)
                    dve.scalar_tensor_tensor(gT[:, j % 2, 1], gf[:, :, :], scale[:, MATS["g"]:MATS["g"] + 1],
                                             gT[:, j % 2, 0], ALU.mult, ALU.subtract).then_inc(g_ready, 1)

                if isinstance(i, int) and i == 0:
                    prepare_attention()
                if isinstance(i, int) and i == 1:
                    prepare_mlp()
                if m is not None:
                    gelu_low(0)
                weights(0)
                if b is not None:
                    after(dve, res_ready, 1, b, 0)
                    project("q", split(zq[:, :], DC), 3, 2, b3_used, B3, 1, b)
                if g is not None:
                    after(dve, gl_mm, 1, g, 1)
                    dve.tensor_scalar(gates[:, g, :], bank[7][:, 0:E], 1.0 / Z_SCALE, GATE_MIN, ALU.mult, ALU.max).then_inc(gl_used, 1)
                if a is not None:
                    after(dve, a_mm, A_MM, a, 1)
                    for k in range(CC):
                        dve.tensor_scalar(aT[:, k, :], bank[1][:, k * P:(k + 1) * P], unscale[:, 0:1], qk_bias[:, k:k + 1],
                                          ALU.mult, ALU.add)
                    dve.scalar_tensor_tensor(s0[:, :], bank[1][:, 256:257], 1.0 / Z_SCALE, bq_bk[:, :], ALU.mult, ALU.add)\
                        .then_inc(a_used, 1)
                weights(1)
                if b is not None:
                    norm_split("q", b, zq2, zq[:, :], zq[:, :], z_ready["q"])
                    project("k", split(zk[:, :], DC), 2, 3, b2_used, B2, 2, b)
                if a is not None:
                    after(dve, a_t, A_T, a, 2)
                    dve.tensor_copy(ctxT[:, 0, :], bank[0][:, :]).then_inc(a_tcopy, 1)
                if m is not None:
                    gelu_low(1)
                weights(2)
                if b is not None:
                    norm_split("k", b, zk2, zk[:, :], zk[:, :], z_ready["k"])
                    project("v", zv, 3, 4, b3_used, B3, 2, b)
                    after(dve, b_mm, B_MM, b, 5)
                    dve.tensor_copy(zqT, bank16(2)).then_inc(b2_used, 1)
                    norm("v", b, zv, zv).then_inc(z_ready["v"], 1)
                    after(dve, b2_used, B2, b, 3)
                    dve.tensor_reduce(probe[:, :, :].rearrange("p c b -> p (c b)"),
                                      zqT.rearrange("p l c (b q) -> p (c b) l q", b=BPT), mybir.AxisListType.XY, ALU.add)\
                        .then_inc(probe_chain, 1)
                    after(dve, probe_chain, 9, b, 1)
                    dve.tensor_tensor(probe[:, :, :], probe[:, :, :], bc(col["gq"], 2, [P, DC, BPT]), ALU.mult)\
                        .then_inc(probe_chain, 1)
                    after(dve, probe_chain, 9, b, 2)
                    dve.tensor_tensor(probe[:, :, :], probe[:, :, :], bc(col["betaq"], 2, [P, DC, BPT]), ALU.add)\
                        .then_inc(probe_chain, 1)
                    after(dve, probe_chain, 9, b, 3)
                    dve.tensor_tensor(pm0[:, :, 0:BPT * HC].rearrange("p c (b h) -> p c b h", b=BPT),
                                      bc(probe[:, :, :], 3, [P, DC, BPT, HC]),
                                      c["block_mask"][:, P:KVW].unsqueeze(1).unsqueeze(1).broadcast_to([P, DC, BPT, HC]),
                                      ALU.mult).then_inc(probe_chain, 1)
                    after(dve, probe_chain, 9, b, 4)
                    dve.tensor_tensor(pm1[:, :, :], pm0[:, :, 0:BPT * HC],
                                      bc(col["gk"], 2, [P, DC, BPT * HC]), ALU.mult).then_inc(probe_chain, 1)
                    n_ = BPT * HC
                    after(dve, probe_chain, 9, b, 5)
                    dve.tensor_copy(pm1s[:, 0, :, 0:n_], pm1[:, :, :]).then_inc(probe_chain, 1)
                    after(dve, probe_chain, 9, b, 6)
                    dve.tensor_tensor(pm1[:, :, :], pm1[:, :, :], pm1s[:, 0, :, 0:n_], ALU.subtract).then_inc(probe_chain, 1)
                    after(dve, probe_chain, 9, b, 7)
                    dve.tensor_copy(pm1s[:, 1, :, 0:n_], pm1[:, :, :]).then_inc(probe_chain, 1)
                    after(dve, probe_chain, 9, b, 8)
                    dve.tensor_tensor(pm1[:, :, :], pm1[:, :, :], pm1s[:, 1, :, 0:n_], ALU.subtract).then_inc(probe_chain, 1)
                    after(dve, probe_chain, 9, b, 9)
                    dve.tensor_copy(pm1s[:, 2, :, 0:n_], pm1[:, :, :]).then_inc(pm_ready, 1)
                if a is not None:
                    after(dve, a_t, A_T, a, 4)
                    dve.tensor_copy(ctxT[:, 0, :], bank[0][:, :]).then_inc(a_tcopy, 1)
                weights(3)
                if m is not None:
                    gelu_low(2)
                weights(4)
                if b is not None:
                    after(dve, tanh_q, 1, b, 1)
                    dve.tensor_scalar(pqT[:, :, :], pqT[:, :, :], 1.0, None, ALU.add).then_inc(b2_used, 1)
                    after(dve, b_mm, B_MM, b, 8)
                    dve.scalar_tensor_tensor(pk[:, :], bank[3][:, :], unscale[:, MATS["wfk"]:MATS["wfk"] + 1], row["bfk"],
                                             ALU.mult, ALU.add).then_inc(b3_used, 1)
                if a is not None:
                    after(dve, a_mm, A_MM, a, 2)
                    dve.tensor_reduce(amax[:, 0:1], bank[1][:, :], AX, ALU.max).then_inc(amax_done, 1)
                    after(dve, amax_done, 2, a, 1)
                    dve.tensor_tensor(amax[:, 1:2], amax[:, 0:1], s0[:, :], ALU.add).then_inc(amax_done, 1)
                    after(dve, amax_done, 2, a, 2)
                    dve.tensor_tensor(abias[:, :], s0[:, :], amax[:, 1:2], ALU.subtract).then_inc(abias_ready, 1)
                weights(5)
                if b is not None:
                    after(dve, lg_mm, 1, b, 1)
                    dve.tensor_copy(lsm[:, 3:4], bank[4][:, P:P + 1]).then_inc(lm_chain, 1)
                    after(dve, lm_chain, 4, b, 1)
                    dve.tensor_scalar(lm[:, :], bank[4][:, 0:P], 1.0 / Z_SCALE, lsm[:, 3:4], ALU.mult, ALU.add)\
                        .then_inc(lm_chain, 1)
                    after(dve, lm_chain, 4, b, 2)
                    dve.tensor_tensor(lm[:, :], lm[:, :], c["off_batch"], ALU.add).then_inc(lm_chain, 1)
                    after(dve, lm_chain, 4, b, 3)
                    dve.tensor_reduce(lneg[:, 0:1], lm[:, :], AX, ALU.max).then_inc(lm_chain, 1)
                    after(dve, lm_chain, 4, b, 4)
                    dve.tensor_scalar(lneg[:, 1:2], lneg[:, 0:1], 0.0, -1.0, ALU.max, ALU.mult).then_inc(lm_ready, 1)
                if a is not None:
                    after(dve, a_t, A_T, a, 6)
                    dve.tensor_copy(pT[:, :, :], split(bank[0][:, :], KC)).then_inc(a_tcopy, 1)
                    dve.reciprocal(rl[:, :], lsum[:, :]).then_inc(rl_ready, 1)
                if x is not None:
                    if isinstance(i, int) and i == 3:
                        dve.wait_ge(in_x, 32)
                    stats("x", x, res[:, x, :])
                if b is not None:
                    after(dve, exp_ready, 1, b, 1)
                    dve.tensor_tensor(lsm[:, 2:3], lsm[:, 0:1], lsm[:, 1:2], ALU.add).then_inc(sc_chain, 1)
                    after(dve, sc_chain, 2, b, 1)
                    dve.reciprocal(lsm[:, 2:3], lsm[:, 2:3]).then_inc(sc_chain, 1)
                    after(dve, sc_chain, 2, b, 2)
                    dve.tensor_scalar(scd[:, :], scd[:, :], lsm[:, 2:3], None, ALU.mult)
                    dve.tensor_scalar(s0bc[:, :], c["row_is_bc"], lsm[:, 1:2], lsm[:, 2:3], ALU.mult, ALU.mult)\
                        .then_inc(score_ready, 1)
                    after(dve, ex_mm, 1, b, 1)
                    after(dve, v_ready, 1, b, 1)
                    score = bank[4][:, 256:256 + H].rearrange("p (c h) -> p c h", c=DC)
                    zvh = zv.rearrange("p c (h e) -> p c h e", h=HC)
                    dve.tensor_tensor(zvh, zvh,
                                      bc(score, 3, [P, DC, HC, DH]), ALU.mult)
                    dve.tensor_copy(sv[:, :, P:KVW], score)
                    dve.tensor_tensor(s0kv[:, :, :].rearrange("p (b c) h -> p b c h", b=BPT),
                                      bc(bank[4][:, 288:288 + BPT * DC].rearrange("p (b c) -> p b c", b=BPT), 3,
                                         [P, BPT, DC, HC]),
                                      zero_key[:, :, :].unsqueeze(1).broadcast_to([P, BPT, DC, HC]), ALU.mult)\
                        .then_inc(sv_ready, 1)
                if x is not None:
                    if b is not None:
                        after(dve, res_xn, 1, b, 1)
                    norm_split("x", x, lnx, xn[:, :], res[:, x, :], lnx_ready)
                if m is not None:
                    gelu_low(3)
                weights(6)
                if a is not None:
                    after(dve, a_mm, A_MM, a, 3)
                    dve.tensor_copy(oT[:, :, :], split(bank[1][:, 0:CC * P], CC)).then_inc(a_used, 1)
                weights(7)
                if b is not None:
                    for k in range(4):
                        bt, half = k // 2, k % 2
                        after(dve, b_mm, B_MM, b, 9 + k)
                        dve.tensor_tensor(kv[:, bt, 2 * half:2 * half + 2, :], split(bank[2 + half][:, 0:2 * KVW], 2),
                                          bc(c["block_mask"], 1, [P, 2, KVW]), ALU.mult)\
                            .then_inc(b3_used if half else b2_used, 1)
                    after(dve, b2_used, B2, b, 6)
                    after(dve, b3_used, B3, b, 6)
                    after(dve, sv_ready, 1, b, 1)
                    dve.tensor_tensor(kv[:, :, :, P:KVW], kv[:, :, :, P:KVW],
                                      s0kv[:, :, :].rearrange("p (b c) h -> p b c h", b=BPT), ALU.add).then_inc(kv_ready, 1)
                if a is not None:
                    after(dve, a_mm, A_MM, a, 4)
                    after(dve, xbv_ready, 1, a, 1)
                    after(dve, rl_ready, 1, a, 1)
                    dve.scalar_tensor_tensor(res[:, a, :], bank[1][:, :], rl[:, 0:1], res[:, a, :], ALU.mult, ALU.add)\
                        .then_inc(a_used, 1)
                    after_apart(dve, a_used, A_MM, a, 4)
                    stats("x1", a, res[:, a, :])
                if b is not None:
                    for half in range(2):
                        after(dve, b_mm, B_MM, b, 13 + half)
                        pv = split(bank[2 + half][:, 0:2 * KVW], 2)
                        dn = den[:, 2 * half:2 * half + 2, :]
                        dve.tensor_scalar(dn, pv[:, :, P:KVW], DEN_EPS, None, ALU.add).then_inc(den_chain, 1)
                        after(dve, den_chain, 4, b, 2 * half + 1)
                        dve.reciprocal(dn, dn).then_inc(den_chain, 1)
                        after(dve, den_chain, 4, b, 2 * half + 2)
                        dve.tensor_tensor(on[:, half * 256:(half + 1) * 256].rearrange("p (c h e) -> p c h e", c=2, h=HC),
                                          pv[:, :, 0:P].rearrange("p c (h e) -> p c h e", h=HC),
                                          bc(dn, 3, [P, 2, HC, DH]), ALU.mult).then_inc(b3_used if half else b2_used, 1)
                    after(dve, b2_used, B2, b, 7)
                    after(dve, b3_used, B3, b, 7)
                    stats("o", b, on[:, :])
                if a is not None:
                    norm("x1", a, xn[:, :], res[:, a, :]).then_inc(z_chain["x1"], 1)
                if b is not None:
                    norm_split("o", b, za2, on[:, :], on[:, :], za_ready)
                if a is not None:
                    halves_of("x1", a, xn2, xn[:, :], xn_ready)
                weights(8)
                if m is not None:
                    after(dve, h2_mm, 4, m, 4)
                    after(dve, res_ready, 1, m, 1)
                    dve.scalar_tensor_tensor(res[:, m, :], bank[7][:, :], unscale[:, MATS["w2"]:MATS["w2"] + 1],
                                             res[:, m, :], ALU.mult, ALU.add).then_inc(x2_ready, 1)
                    after_apart(dve, x2_ready, 1, m, 1)
                    stats("y", m, res[:, m, :])
                    norm_split("y", m, y2, ztmp[:, :], res[:, m, :], yt_ready)
                    dve.tensor_copy(stat_y[:, m, 0:1], mv["y"][:, 0:1])
                    dve.tensor_copy(stat_y[:, m, 1:2], rstd["y"][:, 0:1]).then_inc(stat_kept, 1)
            rounds(dve, body)

            with dve.Fori(0, SINKHORN_ROUNDS) as r:
                sinkhorn(1, r)
            top(1)
            for k in range(2, 4):
                winners(k)
            dve.wait_ge(gather_mm, TH)
            for t in range(TH, T):
                dve.tensor_scalar(y_again_of[t % TH], res[:, t, :], stat_y[:, t, 0:1], stat_y[:, t, 1:2],
                                  ALU.subtract, ALU.mult).then_inc(y_again[1], 1)
            for t in range(TH, T):
                dve.wait_ge(scatter_mm, t + 1)
                dve.scalar_tensor_tensor(res[:, t, :], bank[4 + t % 2][:, :], gate_of[:, t:t + 1], res[:, t, :],
                                         ALU.mult, ALU.add).then_inc(x3_ready[1], 1)

        @block.tensor
        def _(pe):
            ident = c["ident"]

            def transposes_pair(bk, pair):
                for part in range(2):
                    for k in range(DC):
                        ins = pe.transpose(bank16(bk)[:, part, k, :], pair[:, part, k * P:(k + 1) * P], ident16[:, :])
                return ins

            def product3(out_, lhsT, rhs, n=DC, first=True, last=True):
                for k in range(n):
                    for step, (a_, b_) in enumerate(((0, 0), (0, 1), (1, 0))):
                        ins = pe.matmul(out_, lhsT(a_, k), rhs(b_, k), start=(first and k == 0 and step == 0),
                                        stop=(last and k == n - 1 and step == 2))
                return ins

            def transposes(bk, in_, n):
                for k in range(n):
                    ins = pe.transpose(bank[bk][:, k * P:(k + 1) * P], in_(k), ident)
                return ins

            def product(out_, pairs):
                for k, (lhsT, rhs) in enumerate(pairs):
                    ins = pe.matmul(out_, lhsT, rhs, start=(k == 0), stop=(k == len(pairs) - 1))
                return ins

            def query_transposes(x):
                after(pe, lnx_ready, 1, x, 1)
                after(pe, a_tcopy, A_T, x, 0)
                transposes_pair(0, lnx).then_inc(a_t, 1)

            pe.wait_ge(in_const, 16)
            pe.wait_ge(in_cross, 32)
            for e in range(DC):
                transposes(e, lambda k: xwq[:, k, e * P:(e + 1) * P], DC)
            for e in range(DC):
                for k in range(CC):
                    at = (e % 2) * KD + k * P
                    last = pe.transpose(bank[4 + e // 2][:, at:at + P], xwk[:, k, e * P:(e + 1) * P], ident)
            last.then_inc(prep_t, 1)
            pe.wait_ge(in_cols, VECTORS)
            pe.transpose(bank[6][:, 0:NVEC], vectors, ident[0:NVEC, 0:NVEC]).then_inc(cols_mm, 1)
            pe.wait_ge(prep_tcopy, 1)
            pe.wait_ge(cols_ready, 1)
            for k in range(DC):
                last = product(bank[6 + k // 2][:, (k % 2) * KD:(k % 2 + 1) * KD],
                        [(xwqT[:, e, k * P:(k + 1) * P], xwkT[:, e, :]) for e in range(DC)])
            last.then_inc(prep_mm, 1)
            pe.wait_ge(qk_ready, 1)
            pe.wait_ge(squares, 1)
            pe.matmul(bank[6][:, 32:33], c["ones"], sums[:, 0:1], start=True, stop=True).then_inc(totals, 1)
            query_transposes(0)
            pe.wait_ge(prep_bc, 1)
            for k in range(CC):
                product(bank[4][:, k:k + 1], [(xwkT[:, e, k * P:(k + 1) * P], col["x_bq"][:, e:e + 1]) for e in range(DC)])
            for k in range(DC):
                product(bank[4][:, 8 + k:9 + k],
                        [(xwqT[:, e, k * P:(k + 1) * P], col["x_bk"][:, e:e + 1]) for e in range(DC)])
            product(bank[4][:, 16:17], [(xbq_b[:, e, :], col["x_bk"][:, e:e + 1]) for e in range(DC)]).then_inc(prep_mm, 1)
            pe.wait_ge(chunk_split, 1)
            pe.wait_ge(consts16, 1)
            pe.wait_ge(gs_chain, 7)

            def total_of(out_, a, b):
                a, b = square_count[a], (square_count + [square_count[-1] + 1])[b]
                return product(out_, [(c["ones"], sums[:, k:k + 1]) for k in range(a, b)])

            def prepare_attention():
                pe.wait_ge(in_proj, 80)
                product(bank[2][:, :], [(betak_b[:, e, :], proj_32["wfk"][:, e, :]) for e in range(DC)])
                for f in range(DC):
                    last = product(bank[3][:, f:f + 1],
                                   [(proj_32["wfq"][:, e, f * P:(f + 1) * P], col["betaq"][:, e:e + 1])
                                    for e in range(DC)])
                last.then_inc(prep_mm, 1)
                pe.wait_ge(squares, square_count[6])
                for k in range(2):
                    total_of(bank[6][:, 32 + k:33 + k], 1 + k, 2 + k)
                for k in range(2, 5):
                    last = total_of(bank[6][:, 32 + k:33 + k], 1 + k, 2 + k)
                last.then_inc(totals, 1)

            def mlp_bias(j):
                if j == 0:
                    pe.wait_ge(in_w1, 16)
                for f in range(j * HC, (j + 1) * HC):
                    last = product(bank[5][:, f:f + 1],
                                   [(w1_32[:, e, f * P:(f + 1) * P], col["ba"][:, e:e + 1]) for e in range(DC)])
                if j == 3:
                    last.then_inc(prep_mm, 1)

            def prepare_mlp():
                pe.wait_ge(squares, square_count[14])
                total_of(bank[6][:, 32:33], 6, 10)
                total_of(bank[6][:, 33:34], 10, 14).then_inc(totals, 1)

            def column_sums(h, r):
                if r == 0:
                    pe.wait_ge(gl_used, (h + 1) * TH)
                    if h == 1:
                        pe.wait_ge(wonT_ready, 2)
                else:
                    pe.wait_ge(sink_done, SINKHORN_ROUNDS * h + r)
                pe.matmul(bank[0][:, 0:R], c["same_batch"], gates[:, h * TH:(h + 1) * TH, :].rearrange("p t e -> p (t e)"),
                          start=True, stop=True).then_inc(cs_mm, 1)

            def gates_transpose(h):
                pe.wait_ge(sink_done, SINKHORN_ROUNDS * (h + 1))
                pe.transpose(bank[1][0:R, 0:P], gates[:, h * TH:(h + 1) * TH, :].rearrange("p t e -> p (t e)"), ident)\
                    .then_inc(gates_mm, 1)

            def pick(k):
                pe.wait_ge(picks_ready, k + 1)
                if k < 2:
                    pe.wait_ge(b2_used, B2 * T)
                    pe.wait_ge(b3_used, B3 * T)
                else:
                    pe.wait_ge(gathered, TH)
                pe.matmul(bank[2 + k % 2][:, :], c["ones"][0:R, :], picks[0:R, k % 2, :], start=True, stop=True)\
                    .then_inc(picks_mm, 1)

            def winners_transpose(k):
                pe.wait_ge(won_ready, k + 1)
                if k >= 2:
                    pe.wait_ge(wonT_ready, k - 1)
                transposes(k % 2, lambda kk: won[:, 4 * k + kk, :], 4).then_inc(wonT_mm, 1)

            def gather(t):
                pe.wait_ge(y_again[t // TH], t % TH + 1)
                pe.wait_ge(won_ready, 2 * (t // TH + 1))
                if t >= 2:
                    pe.wait_ge(gathered, t - 1)
                for k in range(DC):
                    last = pe.matmul(bank[2 + t % 2][:, k * P:(k + 1) * P], y_again_of[t % TH][:, k * P:(k + 1) * P],
                                     won[:, t, :], start=True, stop=True)
                last.then_inc(gather_mm, 1)

            def expert(u):
                h, e = u // E, u % E
                pe.wait_ge(gathered, TH * (h + 1))
                pe.wait_ge(in_experts[e], 16)
                if u >= 2:
                    pe.wait_ge(expert_copied, u - 1)
                product(bank[6 + u % 2][:, :], [(routed_x[:, k, e, h * P:(h + 1) * P], experts[:, e, k, :])
                                                for k in range(DC)]).then_inc(expert_mm, 1)

            def scatter(t):
                pe.wait_ge(in_returned[t % 4], 16 * (t // 4 + 1))
                pe.wait_ge(wonT_ready, t // 4 + 1)
                if t >= TH + 2:
                    pe.wait_ge(x3_ready[1], t - TH - 1)
                elif t >= 2:
                    pe.wait_ge(row_scaled, t - 1)
                pe.matmul(bank[4 + t % 2][:, :], wonT[:, t, :], returned[:, t % 4, :], start=True, stop=True)\
                    .then_inc(scatter_mm, 1)

            def body(i, x, a, b, m, g):
                def routing(k):
                    if isinstance(i, int) and i == 0 and k in (2, 3, 5, 6):
                        if k == 5:
                            prepare_mlp()
                        mlp_bias((2, 3, 5, 6).index(k))
                    if isinstance(i, int) and i == T and k != 7:
                        column_sums(0, min(k, 7))
                    if isinstance(i, int) and i == T + 1:
                        if k == 0:
                            gates_transpose(0)
                        if k == 2:
                            pick(0)
                            pick(1)
                        if k == 7:
                            winners_transpose(0)
                            winners_transpose(1)
                    if isinstance(i, int) and i == T + 2 and k == 0:
                        for t in range(TH // 2):
                            gather(t)

                def h1(j):
                    after(pe, g_raw, 4, m, j - 1)
                    for f in range(HC):
                        ff = j * HC + f
                        last = product3(bank[5 + j % 2][:, f * P:(f + 1) * P],
                                        lambda l, k: w1[k][:, l, ff * P:(ff + 1) * P], lambda l, k: hT[:, l, k, :])
                    last.then_inc(h1_mm, 1)

                def h2(j, half=None):
                    n, base = (HC, 0) if half is None else (HC // 2, half * HC // 2)
                    if half != 1:
                        after(pe, g_ready, 4, m, j + 1)
                    last = product3(bank[7][:, :], lambda l, f: gT[:, j % 2, l, base + f, :],
                                    lambda l, f: w2[j][:, l, base + f, :], n, j == 0 and base == 0, j == 3 and base + n == HC)
                    if half != 0:
                        last.then_inc(h2_mm, 1)

                def context(k):
                    bt, cc = k // 2, k % 2
                    after(pe, a_tcopy, A_T, a, k + 1)
                    transposes(0, lambda kk: ctxs[:, bt, kk, cc * P:(cc + 1) * P], KC).then_inc(a_t, 1)

                def scores(bt):
                    after(pe, a_tcopy, A_T, a, 3 + 2 * bt)
                    if bt == 0:
                        after(pe, a_used, A_MM, a, 1)
                    product(bank[1][bt * NQ:(bt + 1) * NQ, :],
                            [(aT[:, k, bt * NQ:(bt + 1) * NQ], ctxT[:, k, :]) for k in range(CC)])\
                        .then_inc(scores0_done if bt == 0 else a_mm, 1)

                def row_product(bk, xT, w):
                    return product3(bank[bk][:, :], lambda l, k: xT[:, l, k, :], lambda l, k: w[:, l, k, :])

                if isinstance(i, int) and i == 0:
                    prepare_attention()
                if isinstance(i, int) and i == 1:
                    pe.wait_ge(squares, square_count[14] + 1)
                    total_of(bank[6][:, 34:35], 14, 15).then_inc(totals, 1)
                routing(0)
                if a is not None:
                    after(pe, a_tcopy, A_T, a, 1)
                    after(pe, a_used, A_MM, a, 0)
                    for cc in range(CC):
                        product3(bank[1][:, cc * P:(cc + 1) * P],
                                 lambda l, k: qk[:, l, k, cc * P:(cc + 1) * P], lambda l, k: lnxT[:, l, k, :])
                    product(bank[1][:, 256:257], [(lnxT[:, l, k, :], q_bk[:, w_, k:k + 1]) for k in range(DC)
                                                  for l in range(2) for w_ in range(3)]).then_inc(a_mm, 1)
                if m is not None:
                    after(pe, za_ready, 1, m, 1)
                    after(pe, sv_ready, 1, m, 1)
                    transposes_pair(4, za2).then_inc(hT_mm, 1)
                if b is not None:
                    after(pe, xn_ready, 1, b, 1)
                    after(pe, b2_used, B2, b, 0)
                    transposes_pair(2, xn2).then_inc(b_mm, 1)
                if m is not None:
                    if isinstance(i, int) and i == 2:
                        pe.wait_ge(chunk_split, 14)
                    after(pe, hT_ready, 1, m, 1)
                    h1(0)
                if b is not None:
                    if isinstance(i, int) and i == 1:
                        pe.wait_ge(chunk_split, 6)
                    after(pe, b2_used, B2, b, 1)
                    after(pe, b3_used, B3, b, 0)
                    row_product(3, xnT, wq).then_inc(b_mm, 1)
                if g is not None:
                    after(pe, yt_ready, 1, g, 1)
                    transposes_pair(7, y2).then_inc(yT_mm, 1)
                if b is not None:
                    row_product(2, xnT, wk).then_inc(b_mm, 1)
                routing(1)
                if g is not None:
                    after(pe, yT_ready, 1, g, 1)
                    product(bank[7][:, 0:E], [(yT[:, l, k, :], gw2[:, w_, k, :]) for k in range(DC) for l in range(2)
                                              for w_ in range(3)]).then_inc(gl_mm, 1)
                if a is not None:
                    after(pe, in_ctx, 32, a, 32)
                    context(0)
                if m is not None:
                    h1(1)
                routing(2)
                if b is not None:
                    after(pe, b3_used, B3, b, 1)
                    row_product(3, xnT, wv).then_inc(b_mm, 1)
                if a is not None:
                    context(1)
                if m is not None:
                    after(pe, gl_used, 1, m, 0)
                    h2(0)
                routing(3)
                if b is not None:
                    after(pe, z_ready["q"], 1, b, 1)
                    after(pe, b2_used, B2, b, 2)
                    transposes_pair(2, zq2).then_inc(b_mm, 1)
                if a is not None:
                    scores(0)
                if b is not None:
                    after(pe, z_ready["k"], 1, b, 1)
                    after(pe, b3_used, B3, b, 2)
                    transposes_pair(3, zk2).then_inc(b_mm, 1)
                if a is not None:
                    context(2)
                if m is not None:
                    h1(2)
                if b is not None:
                    after(pe, b2_used, B2, b, 3)
                    for f in range(DC):
                        last = product3(bank[2][:, f * P:(f + 1) * P],
                                        lambda l, k: wfq[:, l, k, f * P:(f + 1) * P], lambda l, k: zqT[:, l, k, :])
                    last.then_inc(b_mm, 1)
                routing(4)
                if a is not None:
                    context(3)
                if b is not None:
                    after(pe, b3_used, B3, b, 3)
                    row_product(3, zkT, wfk).then_inc(b_mm, 1)
                if a is not None:
                    scores(1)
                if b is not None:
                    after(pe, pm_ready, 1, b, 1)
                    after(pe, hT_ready, 1, b, 0)
                    for k in range(DC):
                        product(bank[4][k * DH:(k + 1) * DH, 0:P], [(pm1s[:, w_, k, :], zkT[:, l, k, :])
                                                                    for w_ in range(3) for l in range(2)])
                        last = pe.matmul(bank[4][k * DH:(k + 1) * DH, P:P + 1], pm0[:, k, :], col["betak"][:, k:k + 1],
                                         start=True, stop=True)
                    last.then_inc(lg_mm, 1)
                routing(5)
                if m is not None:
                    h2(1)
                if a is not None:
                    after(pe, a_used, A_MM, a, 2)
                    after(pe, a_tcopy, A_T, a, 5)
                    transposes(0, lambda k: probs[:, k * P:(k + 1) * P], KC).then_inc(a_t, 1)
                if m is not None:
                    h1(3)
                routing(6)
                if b is not None:
                    after(pe, score_ready, 1, b, 1)
                    pe.matmul(bank[4][:, 256:256 + H], scd[:, :], c["head_of_row"], start=True, stop=True)
                    pe.matmul(bank[4][:, 288:288 + BPT * DC], c["row_to_feature"], s0bc[:, :], start=True, stop=True)\
                        .then_inc(ex_mm, 1)
                if a is not None:
                    after(pe, a_tcopy, A_T, a, 6)
                    for cc in range(CC):
                        for bt in range(BPT):
                            at = cc * P + bt * NQ
                            last = product(bank[1][:, at:at + NQ],
                                           [(ctxs[:, bt, k, cc * P:(cc + 1) * P], pT[:, k, bt * NQ:(bt + 1) * NQ])
                                            for k in range(KC)])
                    last.then_inc(a_mm, 1)
                routing(7)
                if b is not None:
                    def keys_values(k):
                        bt, half = k // 2, k % 2
                        used, per = (b3_used, B3) if half else (b2_used, B2)
                        after(pe, used, per, b, 4 + k // 2)
                        for cc in range(2):
                            chunk = 2 * half + cc
                            last = pe.matmul(bank[2 + half][:, cc * KVW:(cc + 1) * KVW],
                                             pk[bt * NQ:(bt + 1) * NQ, chunk * P:(chunk + 1) * P],
                                             sv[bt * NQ:(bt + 1) * NQ, chunk, :], start=True, stop=True)
                        last.then_inc(b_mm, 1)
                    after(pe, pk_ready, 1, b, 1)
                    after(pe, sv_ready, 1, b, 1)
                    keys_values(0)
                    keys_values(1)
                if m is not None:
                    h2(2, 0)
                if b is not None:
                    keys_values(2)
                    keys_values(3)
                if a is not None:
                    after(pe, a_used, A_MM, a, 3)
                    if isinstance(i, int) and i == 0:
                        pe.wait_ge(in_xwv, 16)
                    product(bank[1][:, :], [(oT[:, k, :], xwv[:, k, :]) for k in range(CC)]).then_inc(a_mm, 1)
                if b is not None:
                    after(pe, kv_ready, 1, b, 1)
                    for half in range(2):
                        for bt in range(BPT):
                            for cc in range(2):
                                chunk = 2 * half + cc
                                last = pe.matmul(bank[2 + half][bt * NQ:(bt + 1) * NQ, cc * KVW:(cc + 1) * KVW],
                                                 pqT[:, chunk, bt * NQ:(bt + 1) * NQ], kv[:, bt, chunk, :],
                                                 start=True, stop=True)
                        last.then_inc(b_mm, 1)
                if m is not None:
                    h2(2, 1)
                routing(8)
                if x is not None:
                    query_transposes(x)
                if m is not None:
                    h2(3)
            rounds(pe, body)

            column_sums(1, 0)
            for t in range(TH // 2, TH):
                gather(t)
            pe.wait_ge(g_raw, 4 * T)
            for r in range(SINKHORN_ROUNDS):
                if r >= 1:
                    column_sums(1, r)
                expert(r)
            gates_transpose(1)
            pick(2)
            for t in range(TH // 2):
                scatter(t)
            pick(3)
            winners_transpose(2)
            for t in range(TH // 2, TH):
                scatter(t)
            winners_transpose(3)
            for t in range(TH, T):
                gather(t)
            for u in range(E, 2 * E):
                expert(u)
            for t in range(TH, T):
                scatter(t)


_NAMES = {
    "x": "x", "ctx": "ctx_512", "x_wq": "L0_xattn_Wq", "x_wk": "L0_xattn_Wk", "x_wv": "L0_xattn_Wv",
    "c_x_bq": "L0_xattn_bq", "c_x_bk": "L0_xattn_bk", "r_x_bv": "L0_xattn_bv",
    "wq": "L0_attn_Wq", "wk": "L0_attn_Wk", "wv": "L0_attn_Wv", "wfq": "L0_attn_Wfq", "wfk": "L0_attn_Wfk",
    "r_bq": "L0_attn_bq", "r_bk": "L0_attn_bk", "r_bv": "L0_attn_bv", "c_gq": "L0_attn_gq", "c_betaq": "L0_attn_betaq",
    "c_gk": "L0_attn_gk", "c_betak": "L0_attn_betak", "r_gv": "L0_attn_gv", "r_betav": "L0_attn_betav",
    "c_bfq": "L0_attn_bfq", "bfk": "L0_attn_bfk", "ga": "L0_attn_ga", "c_ba": "L0_attn_ba",
    "w1": "L0_attn_W1", "b1": "L0_attn_b1", "w2": "L0_attn_W2", "r_b2": "L0_attn_b2",
    "gate_w": "L0_ffn_gate_w", "experts": "L0_ffn_experts",
}


def constants():
    import numpy as np
    p = np.arange(P)
    cc = np.zeros((P, CONST_WIDTH), np.float32)

    def put(name, value):
        a, b = CONST_COLS[name]
        cc[:, a:b] = value
    put("ident", np.eye(P))
    feature = p[:, None] // DH
    put("block_mask", np.concatenate([feature == p[None, :] // DH, feature == np.arange(HC)[None, :]], 1))
    chunk, rest = p // DH, p % DH
    bt, hd, real = rest // HC % BPT, rest % HC, rest < BPT * HC
    put("off_batch", np.where(bt[:, None] == p[None, :] // NQ, 0.0, -1e30))
    put("head_of_row", real[:, None] & ((chunk * HC + hd)[:, None] == np.arange(H)[None, :]))
    put("row_to_feature", real[:, None] & (hd[:, None] == p[None, :] // DH))
    put("row_is_bc", real[:, None] & ((bt * DC + chunk)[:, None] == np.arange(BPT * DC)[None, :]))
    put("same_batch", p[:, None] // NQ == p[None, :] // NQ)
    put("slot_code", (p % SLOTS * E + p // (BPT * SLOTS) + 1)[None, :])
    put("token_id", p[:, None])
    put("expert_of_row", p[:, None] % E == np.arange(E)[None, :])
    put("tile_of_row", p[:, None] // E == np.arange(T)[None, :])
    put("ones", 1.0)
    put("minus_half", -0.5)
    return cc


def kernel(**inputs):
    import numpy as np
    import concourse.bacc as bacc
    from concourse import mybir as _mybir
    from concourse.bass_utils import run_bass_kernel_spmd as run

    nc = bacc.Bacc("TRN2", target_bir_lowering=False, num_devices=1, dynamic_dma_scratch_size=1024)
    arrays, d = {}, {}
    for short, name in [*_NAMES.items(), ("consts", None)]:
        a = np.ascontiguousarray(inputs[name] if name else constants())
        arrays["in_" + short] = a
        d[short] = nc.dram_tensor("in_" + short, a.shape, _mybir.dt.from_np(a.dtype), kind="ExternalInput").ap()
    for n in ("bfk", "ga"):
        d["r_" + n] = d["c_" + n] = d[n]
    out = nc.dram_tensor("out", (B, NQ, D), _mybir.dt.float32, kind="ExternalOutput").ap()
    build(nc, d, out)
    return run(nc, [arrays], core_ids=[0]).results[0]["out"]
```
